# Optimizing a Trainium2 kernel written in Bass

```python
import numpy as np
import jax
import jax.numpy as jnp

def _softmax(x, axis=-1):
    return jax.nn.softmax(x, axis=axis)

def _gelu(x):
    return jax.nn.gelu(x, approximate=True)

def _silu(x):
    return jax.nn.silu(x)

def _sigmoid(x):
    return jax.nn.sigmoid(x)

def _layernorm(x, axis=-1, eps=1e-05):
    m = jnp.mean(x, axis=axis, keepdims=True)
    v = jnp.var(x, axis=axis, keepdims=True)
    return (x - m) / jnp.sqrt(v + eps)

def _scatter_add(tgt, idx, src, axis=0):
    return tgt.at[idx].add(src)

def _segment_sum(src, seg, n):
    return jax.ops.segment_sum(src, seg, n)
kernel_name = 'mk_decoder_preln_d2_seqx_r4_7f3829'

def setup_inputs(seed: int=0):
    np.random.seed(seed)
    _w = jnp.asarray

    def _rec_inputs():
        import jax
        import jax.numpy as jnp
        _rk = jax.random.key(seed)
        x = 0.0002417 + 0.9998 * jax.random.normal(jax.random.fold_in(_rk, 1), (2, 1024, 256), jnp.float32)
        _lenS = 1024 - jax.random.randint(jax.random.fold_in(_rk, 7), (2,), 0, max(1, 1024 // 4) + 1, jnp.int32)
        _lenS2 = 77 - jax.random.randint(jax.random.fold_in(_rk, 8), (2,), 0, max(1, 77 // 4) + 1, jnp.int32)
        _ctx_1024P = jax.random.normal(jax.random.fold_in(_rk, 11), (2, 16, 256), jnp.float32)
        _ctx_1024c = jax.random.dirichlet(jax.random.fold_in(_rk, 511), 0.3 * jnp.ones((16,), jnp.float32), (2, 77))
        _ctx_1024t = jnp.einsum('bsk,bkd->bsd', _ctx_1024c, _ctx_1024P)
        _ctx_1024t = _ctx_1024t * jax.lax.rsqrt(jnp.mean(jnp.square(_ctx_1024t)) + 1e-12) * 0.953939
        ctx_1024 = 7.22013e-05 + 1.00017 * (_ctx_1024t + 0.3 * jax.random.normal(jax.random.fold_in(_rk, 611), (2, 77, 256), jnp.float32))
        _validS = jnp.arange(1024)[None, :] < _lenS[:, None]
        _validS2 = jnp.arange(77)[None, :] < _lenS2[:, None]
        _causal = jnp.tril(jnp.ones((1024, 1024), dtype=bool))
        mask_1x1xSxS2_ik0 = jnp.where(jnp.broadcast_to(_validS2[0:1, None, None, :], (1, 1, 1024, 77)), 0, 1).astype(jnp.int32)
        return (x, ctx_1024, mask_1x1xSxS2_ik0)
    x, ctx_1024, mask_1x1xSxS2_ik0 = _rec_inputs()

    def _L0_attn_setup():
        import jax, jax.numpy as jnp
        import numpy as np
        B, T, D = (2, 512, 256)
        H = 16
        DH = D // H
        EPS = 1e-06

        def _feature_map(x):
            return jax.nn.elu(x) + 1.0
        key = jax.random.key(seed)
        ks = jax.random.split(key, 9)
        s = 0.02
        return {'x': jax.random.normal(ks[0], (B, T, D), dtype=jnp.float32), 'Wq': jax.random.normal(ks[1], (D, D), dtype=jnp.float32) * s, 'bq': jnp.zeros((D,), dtype=jnp.float32), 'Wk': jax.random.normal(ks[2], (D, D), dtype=jnp.float32) * s, 'bk': jnp.zeros((D,), dtype=jnp.float32), 'Wv': jax.random.normal(ks[3], (D, D), dtype=jnp.float32) * s, 'bv': jnp.zeros((D,), dtype=jnp.float32), 'Wo': jax.random.normal(ks[4], (D, D), dtype=jnp.float32) * s, 'bo': jnp.zeros((D,), dtype=jnp.float32)}
    _L0_attn_all = _L0_attn_setup()
    _L0_attn_in = {k: v for k, v in _L0_attn_all.items() if k in ('Wq', 'bq', 'Wk', 'bk', 'Wv', 'bv', 'Wo', 'bo')}
    del _L0_attn_all

    def _L0_xattn_setup():
        import jax, jax.numpy as jnp
        import numpy as np
        EMBED = 256
        HEADS = 16
        HEAD_DIM = EMBED // HEADS
        EXP_DIM = 2 * HEAD_DIM

        def _feature_map(x, fm_w, fm_b):
            z = jnp.einsum('nshd,ed->nshe', x, fm_w) + fm_b
            return jnp.concatenate([jnp.exp(z), jnp.exp(-z)], axis=-1)
        key = jax.random.key(seed)
        ks = jax.random.split(key, 7)
        N, S = (4, 512)
        values = jax.random.normal(ks[0], (N, S, EMBED), dtype=jnp.float32)
        keys_ = jax.random.normal(ks[1], (N, S, EMBED), dtype=jnp.float32)
        query = jax.random.normal(ks[2], (N, S, EMBED), dtype=jnp.float32)
        fm_w = jnp.eye(HEAD_DIM, dtype=jnp.float32) + 0.02 * jax.random.normal(ks[3], (HEAD_DIM, HEAD_DIM), dtype=jnp.float32)
        fm_b = 0.02 * jax.random.normal(ks[4], (HEAD_DIM,), dtype=jnp.float32)
        fc_w = jax.random.normal(ks[5], (EMBED, HEADS * EXP_DIM), dtype=jnp.float32) * (1.0 / np.sqrt(HEADS * EXP_DIM))
        fc_b = jnp.zeros((EMBED,), dtype=jnp.float32)
        return {'values': values, 'keys': keys_, 'query': query, 'fm_w': fm_w, 'fm_b': fm_b, 'fc_w': fc_w, 'fc_b': fc_b}
    _L0_xattn_all = _L0_xattn_setup()
    _L0_xattn_in = {k: v for k, v in _L0_xattn_all.items() if k in ('fm_w', 'fm_b', 'fc_w', 'fc_b')}
    del _L0_xattn_all

    def _L0_ffn_setup():
        import jax, jax.numpy as jnp
        import numpy as np
        D_MODEL = 256
        NUM_TILES = 64
        TPC = 8
        NUM_CLUSTERS = NUM_TILES // TPC
        GRID = 16
        COMP_H = 64
        NUM_KNOTS = 8
        EPS_LN = 1e-05

        def _calibrate(scores, knots, temperature):
            K = knots.shape[0]
            normalized = jax.nn.sigmoid(scores / (temperature[0] + 1e-06))
            idx_float = normalized * (K - 1)
            idx_low = jnp.clip(idx_float.astype(jnp.int32), 0, K - 2)
            idx_high = idx_low + 1
            t = idx_float - idx_low.astype(scores.dtype)
            val_low = knots[idx_low]
            val_high = knots[idx_high]
            return val_low + t * (val_high - val_low)

        def _forward(x, signatures_raw, knot_values, temperature, compress_w1, compress_b1, compress_w2, compress_b2, spline_w1, spline_b1, spline_w2, spline_b2, directions, norm_gamma, norm_beta, output_scale):
            B, T, D = x.shape
            xf = x.reshape(-1, D)
            q = jnp.where(signatures_raw > 0.3, 1.0, jnp.where(signatures_raw < -0.3, -1.0, 0.0)).astype(signatures_raw.dtype)
            sigs = signatures_raw + jax.lax.stop_gradient(q - signatures_raw)
            cluster_sigs = jnp.sign(sigs.reshape(NUM_CLUSTERS, TPC, D).mean(axis=1))
            cluster_scores = xf @ cluster_sigs.T
            cluster_gates = _calibrate(cluster_scores, knot_values, temperature)
            cluster_idx = jnp.argmax(cluster_gates, axis=-1)
            tile_scores = xf @ sigs.T
            tile_gates = _calibrate(tile_scores, knot_values, temperature)
            gates_by_cluster = tile_gates.reshape(-1, NUM_CLUSTERS, TPC)
            sel_gates = jnp.take_along_axis(gates_by_cluster, cluster_idx[:, None, None], axis=1)[:, 0, :]
            local_idx = jnp.argmax(sel_gates, axis=-1)
            tile_idx = cluster_idx * TPC + local_idx
            h = jax.nn.gelu(xf @ compress_w1 + compress_b1, approximate=False)
            comp = jnp.tanh(h @ compress_w2 + compress_b2)
            w1 = spline_w1[tile_idx]
            b1 = spline_b1[tile_idx]
            hh = jax.nn.relu(jnp.einsum('ni,nig->ng', comp, w1) + b1)
            w2 = spline_w2[tile_idx]
            b2 = spline_b2[tile_idx]
            mag = jnp.einsum('ng,ngo->no', hh, w2) + b2
            ffn_out = mag * directions[tile_idx] * output_scale[0]
            y = xf + ffn_out
            mu = y.mean(axis=-1, keepdims=True)
            var = ((y - mu) ** 2).mean(axis=-1, keepdims=True)
            y = (y - mu) / jnp.sqrt(var + EPS_LN) * norm_gamma + norm_beta
            return y.reshape(B, T, D)
        key = jax.random.key(seed)
        ks = jax.random.split(key, 12)
        B, T = (4, 1024)
        x = jax.random.normal(ks[0], (B, T, D_MODEL), dtype=jnp.float32)
        signatures_raw = jax.random.normal(ks[1], (NUM_TILES, D_MODEL), dtype=jnp.float32) * 0.5
        knot_values = jax.nn.sigmoid(jnp.linspace(-3.0, 3.0, NUM_KNOTS).astype(jnp.float32))
        temperature = jnp.ones((1,), dtype=jnp.float32)
        compress_w1 = jax.random.normal(ks[2], (D_MODEL, COMP_H), dtype=jnp.float32) * (1.0 / np.sqrt(D_MODEL))
        compress_b1 = jnp.zeros((COMP_H,), dtype=jnp.float32)
        compress_w2 = jax.random.normal(ks[3], (COMP_H, 2), dtype=jnp.float32) * (1.0 / np.sqrt(COMP_H))
        compress_b2 = jnp.zeros((2,), dtype=jnp.float32)
        spline_w1 = jax.random.normal(ks[4], (NUM_TILES, 2, GRID), dtype=jnp.float32) * (1.0 / np.sqrt(2.0))
        spline_b1 = jnp.zeros((NUM_TILES, GRID), dtype=jnp.float32)
        spline_w2 = jax.random.normal(ks[5], (NUM_TILES, GRID, 1), dtype=jnp.float32) * (1.0 / np.sqrt(GRID))
        spline_b2 = jnp.zeros((NUM_TILES, 1), dtype=jnp.float32)
        directions = jax.random.normal(ks[6], (NUM_TILES, D_MODEL), dtype=jnp.float32) * 0.02
        norm_gamma = jnp.ones((D_MODEL,), dtype=jnp.float32)
        norm_beta = jnp.zeros((D_MODEL,), dtype=jnp.float32)
        output_scale = jnp.ones((1,), dtype=jnp.float32) * 0.1
        return dict(x=x, signatures_raw=signatures_raw, knot_values=knot_values, temperature=temperature, compress_w1=compress_w1, compress_b1=compress_b1, compress_w2=compress_w2, compress_b2=compress_b2, spline_w1=spline_w1, spline_b1=spline_b1, spline_w2=spline_w2, spline_b2=spline_b2, directions=directions, norm_gamma=norm_gamma, norm_beta=norm_beta, output_scale=output_scale)
    _L0_ffn_all = _L0_ffn_setup()
    _L0_ffn_in = {k: v for k, v in _L0_ffn_all.items() if k in ('signatures_raw', 'knot_values', 'temperature', 'compress_w1', 'compress_b1', 'compress_w2', 'compress_b2', 'spline_w1', 'spline_b1', 'spline_w2', 'spline_b2', 'directions', 'norm_gamma', 'norm_beta', 'output_scale')}
    del _L0_ffn_all

    def _L1_attn_setup():
        import jax, jax.numpy as jnp
        import numpy as np
        B, S, D, H = (4, 512, 256, 16)
        HD = D // H
        key = jax.random.key(seed)
        ks = jax.random.split(key, 5)
        hidden_states = jax.random.normal(ks[0], (B, S, D), dtype=jnp.float32)
        w_attn = jax.random.normal(ks[1], (D, 3 * D), dtype=jnp.float32) * 0.02
        b_attn = jnp.zeros((3 * D,), dtype=jnp.float32)
        w_proj = jax.random.normal(ks[2], (D, D), dtype=jnp.float32) * 0.02
        b_proj = jnp.zeros((D,), dtype=jnp.float32)
        return {'hidden_states': hidden_states, 'w_attn': w_attn, 'b_attn': b_attn, 'w_proj': w_proj, 'b_proj': b_proj}
    _L1_attn_all = _L1_attn_setup()
    _L1_attn_in = {k: v for k, v in _L1_attn_all.items() if k in ('w_attn', 'b_attn', 'w_proj', 'b_proj')}
    del _L1_attn_all

    def _L1_xattn_setup():
        import jax, jax.numpy as jnp
        import numpy as np
        import math
        B, S, D, H = (2, 512, 256, 16)
        DK = D // H

        def _split_heads(x):
            b, s, _ = x.shape
            return x.reshape(b, s, H, DK).transpose(0, 2, 1, 3)
        key = jax.random.key(seed)
        ks = jax.random.split(key, 12)
        std = 1.0 / math.sqrt(D)
        inp = {'q': jax.random.normal(ks[0], (B, S, D), jnp.float32), 'k': jax.random.normal(ks[1], (B, S, D), jnp.float32), 'v': jax.random.normal(ks[2], (B, S, D), jnp.float32), 'mask': jnp.tril(jnp.ones((S, S), jnp.int32))[None, None, :, :], 'wq': jax.random.normal(ks[3], (D, D), jnp.float32) * std, 'bq': jax.random.normal(ks[4], (D,), jnp.float32) * std, 'wk': jax.random.normal(ks[5], (D, D), jnp.float32) * std, 'bk': jax.random.normal(ks[6], (D,), jnp.float32) * std, 'wv': jax.random.normal(ks[7], (D, D), jnp.float32) * std, 'bv': jax.random.normal(ks[8], (D,), jnp.float32) * std, 'wo': jax.random.normal(ks[9], (D, D), jnp.float32) * std, 'bo': jax.random.normal(ks[10], (D,), jnp.float32) * std}
        return inp
    _L1_xattn_all = _L1_xattn_setup()
    _L1_xattn_in = {k: v for k, v in _L1_xattn_all.items() if k in ('wq', 'bq', 'wk', 'bk', 'wv', 'bv', 'wo', 'bo')}
    del _L1_xattn_all

    def _L1_ffn_setup():
        import jax, jax.numpy as jnp
        import numpy as np
        H = 256
        I = 128
        E = 16
        K = 4
        B, S = (2, 256)
        key = jax.random.key(seed)
        ks = jax.random.split(key, 8)
        scale = 0.05
        return {'hidden_states': jax.random.normal(ks[0], (B, S, H), dtype=jnp.float32), 'gate_w': jax.random.normal(ks[1], (E, H), dtype=jnp.float32) * scale, 'Wg': jax.random.normal(ks[2], (E, H, I), dtype=jnp.float32) * scale, 'Wu': jax.random.normal(ks[3], (E, H, I), dtype=jnp.float32) * scale, 'Wd': jax.random.normal(ks[4], (E, I, H), dtype=jnp.float32) * scale, 'sg': jax.random.normal(ks[5], (H, I), dtype=jnp.float32) * scale, 'su': jax.random.normal(ks[6], (H, I), dtype=jnp.float32) * scale, 'sd': jax.random.normal(ks[7], (I, H), dtype=jnp.float32) * scale}
    _L1_ffn_all = _L1_ffn_setup()
    _L1_ffn_in = {k: v for k, v in _L1_ffn_all.items() if k in ('gate_w', 'Wg', 'Wu', 'Wd', 'sg', 'su', 'sd')}
    del _L1_ffn_all
    return {'x': x, 'ctx_1024': ctx_1024, 'mask_1x1xSxS2_ik0': mask_1x1xSxS2_ik0, 'L0_attn_Wq': _L0_attn_in['Wq'], 'L0_attn_bq': _L0_attn_in['bq'], 'L0_attn_Wk': _L0_attn_in['Wk'], 'L0_attn_bk': _L0_attn_in['bk'], 'L0_attn_Wv': _L0_attn_in['Wv'], 'L0_attn_bv': _L0_attn_in['bv'], 'L0_attn_Wo': _L0_attn_in['Wo'], 'L0_attn_bo': _L0_attn_in['bo'], 'L0_xattn_fm_w': _L0_xattn_in['fm_w'], 'L0_xattn_fm_b': _L0_xattn_in['fm_b'], 'L0_xattn_fc_w': _L0_xattn_in['fc_w'], 'L0_xattn_fc_b': _L0_xattn_in['fc_b'], 'L0_ffn_signatures_raw': _L0_ffn_in['signatures_raw'], 'L0_ffn_knot_values': _L0_ffn_in['knot_values'], 'L0_ffn_temperature': _L0_ffn_in['temperature'], 'L0_ffn_compress_w1': _L0_ffn_in['compress_w1'], 'L0_ffn_compress_b1': _L0_ffn_in['compress_b1'], 'L0_ffn_compress_w2': _L0_ffn_in['compress_w2'], 'L0_ffn_compress_b2': _L0_ffn_in['compress_b2'], 'L0_ffn_spline_w1': _L0_ffn_in['spline_w1'], 'L0_ffn_spline_b1': _L0_ffn_in['spline_b1'], 'L0_ffn_spline_w2': _L0_ffn_in['spline_w2'], 'L0_ffn_spline_b2': _L0_ffn_in['spline_b2'], 'L0_ffn_directions': _L0_ffn_in['directions'], 'L0_ffn_norm_gamma': _L0_ffn_in['norm_gamma'], 'L0_ffn_norm_beta': _L0_ffn_in['norm_beta'], 'L0_ffn_output_scale': _L0_ffn_in['output_scale'], 'L1_attn_w_attn': _L1_attn_in['w_attn'], 'L1_attn_b_attn': _L1_attn_in['b_attn'], 'L1_attn_w_proj': _L1_attn_in['w_proj'], 'L1_attn_b_proj': _L1_attn_in['b_proj'], 'L1_xattn_wq': _L1_xattn_in['wq'], 'L1_xattn_bq': _L1_xattn_in['bq'], 'L1_xattn_wk': _L1_xattn_in['wk'], 'L1_xattn_bk': _L1_xattn_in['bk'], 'L1_xattn_wv': _L1_xattn_in['wv'], 'L1_xattn_bv': _L1_xattn_in['bv'], 'L1_xattn_wo': _L1_xattn_in['wo'], 'L1_xattn_bo': _L1_xattn_in['bo'], 'L1_ffn_gate_w': _L1_ffn_in['gate_w'], 'L1_ffn_Wg': _L1_ffn_in['Wg'], 'L1_ffn_Wu': _L1_ffn_in['Wu'], 'L1_ffn_Wd': _L1_ffn_in['Wd'], 'L1_ffn_sg': _L1_ffn_in['sg'], 'L1_ffn_su': _L1_ffn_in['su'], 'L1_ffn_sd': _L1_ffn_in['sd']}

def reference(x, ctx_1024, mask_1x1xSxS2_ik0, L0_attn_Wq, L0_attn_bq, L0_attn_Wk, L0_attn_bk, L0_attn_Wv, L0_attn_bv, L0_attn_Wo, L0_attn_bo, L0_xattn_fm_w, L0_xattn_fm_b, L0_xattn_fc_w, L0_xattn_fc_b, L0_ffn_signatures_raw, L0_ffn_knot_values, L0_ffn_temperature, L0_ffn_compress_w1, L0_ffn_compress_b1, L0_ffn_compress_w2, L0_ffn_compress_b2, L0_ffn_spline_w1, L0_ffn_spline_b1, L0_ffn_spline_w2, L0_ffn_spline_b2, L0_ffn_directions, L0_ffn_norm_gamma, L0_ffn_norm_beta, L0_ffn_output_scale, L1_attn_w_attn, L1_attn_b_attn, L1_attn_w_proj, L1_attn_b_proj, L1_xattn_wq, L1_xattn_bq, L1_xattn_wk, L1_xattn_bk, L1_xattn_wv, L1_xattn_bv, L1_xattn_wo, L1_xattn_bo, L1_ffn_gate_w, L1_ffn_Wg, L1_ffn_Wu, L1_ffn_Wd, L1_ffn_sg, L1_ffn_su, L1_ffn_sd):
    import jax
    import jax.numpy as jnp

    def _L0_attn_ref(x, Wq, bq, Wk, bk, Wv, bv, Wo, bo):
        import jax, jax.numpy as jnp
        import numpy as np
        B, T, D = (2, 512, 256)
        H = 16
        DH = D // H
        EPS = 1e-06

        def _feature_map(x):
            return jax.nn.elu(x) + 1.0
        b, t, d = x.shape
        q = (x @ Wq.T + bq).reshape(b, t, H, DH).transpose(0, 2, 1, 3)
        k = (x @ Wk.T + bk).reshape(b, t, H, DH).transpose(0, 2, 1, 3)
        v = (x @ Wv.T + bv).reshape(b, t, H, DH).transpose(0, 2, 1, 3)
        q = _feature_map(q)
        k = _feature_map(k)
        kv = jnp.einsum('bhtd,bhte->bhtde', k, v)
        kv_cum = jnp.cumsum(kv, axis=2)
        numerator = jnp.einsum('bhtd,bhtde->bhte', q, kv_cum)
        k_cum = jnp.cumsum(k, axis=2)
        denominator = jnp.einsum('bhtd,bhtd->bht', q, k_cum)
        denominator = jnp.maximum(denominator, EPS)[..., None]
        out = numerator / denominator
        out = out.transpose(0, 2, 1, 3).reshape(b, t, d)
        return out @ Wo.T + bo

    def _L0_xattn_ref(values, keys, query, fm_w, fm_b, fc_w, fc_b):
        import jax, jax.numpy as jnp
        import numpy as np
        EMBED = 256
        HEADS = 16
        HEAD_DIM = EMBED // HEADS
        EXP_DIM = 2 * HEAD_DIM

        def _feature_map(x, fm_w, fm_b):
            z = jnp.einsum('nshd,ed->nshe', x, fm_w) + fm_b
            return jnp.concatenate([jnp.exp(z), jnp.exp(-z)], axis=-1)
        N, S, _ = query.shape
        v = values.reshape(N, -1, HEADS, HEAD_DIM)
        k = keys.reshape(N, -1, HEADS, HEAD_DIM)
        q = query.reshape(N, -1, HEADS, HEAD_DIM)
        v, k, q = (_feature_map(x, fm_w, fm_b) for x in (v, k, q))
        scores = jnp.einsum('nqhd,nkhd->nhqk', q, k) / jnp.sqrt(jnp.float32(EMBED))
        attn = jax.nn.softmax(scores, axis=-1)
        out = jnp.einsum('nhql,nlhd->nqhd', attn, v)
        out = out.reshape(N, S, HEADS * EXP_DIM)
        return out @ fc_w.T + fc_b

    def _L0_ffn_ref(x, signatures_raw, knot_values, temperature, compress_w1, compress_b1, compress_w2, compress_b2, spline_w1, spline_b1, spline_w2, spline_b2, directions, norm_gamma, norm_beta, output_scale):
        import jax, jax.numpy as jnp
        import numpy as np
        D_MODEL = 256
        NUM_TILES = 64
        TPC = 8
        NUM_CLUSTERS = NUM_TILES // TPC
        GRID = 16
        COMP_H = 64
        NUM_KNOTS = 8
        EPS_LN = 1e-05

        def _calibrate(scores, knots, temperature):
            K = knots.shape[0]
            normalized = jax.nn.sigmoid(scores / (temperature[0] + 1e-06))
            idx_float = normalized * (K - 1)
            idx_low = jnp.clip(idx_float.astype(jnp.int32), 0, K - 2)
            idx_high = idx_low + 1
            t = idx_float - idx_low.astype(scores.dtype)
            val_low = knots[idx_low]
            val_high = knots[idx_high]
            return val_low + t * (val_high - val_low)

        def _forward(x, signatures_raw, knot_values, temperature, compress_w1, compress_b1, compress_w2, compress_b2, spline_w1, spline_b1, spline_w2, spline_b2, directions, norm_gamma, norm_beta, output_scale):
            B, T, D = x.shape
            xf = x.reshape(-1, D)
            q = jnp.where(signatures_raw > 0.3, 1.0, jnp.where(signatures_raw < -0.3, -1.0, 0.0)).astype(signatures_raw.dtype)
            sigs = signatures_raw + jax.lax.stop_gradient(q - signatures_raw)
            cluster_sigs = jnp.sign(sigs.reshape(NUM_CLUSTERS, TPC, D).mean(axis=1))
            cluster_scores = xf @ cluster_sigs.T
            cluster_gates = _calibrate(cluster_scores, knot_values, temperature)
            cluster_idx = jnp.argmax(cluster_gates, axis=-1)
            tile_scores = xf @ sigs.T
            tile_gates = _calibrate(tile_scores, knot_values, temperature)
            gates_by_cluster = tile_gates.reshape(-1, NUM_CLUSTERS, TPC)
            sel_gates = jnp.take_along_axis(gates_by_cluster, cluster_idx[:, None, None], axis=1)[:, 0, :]
            local_idx = jnp.argmax(sel_gates, axis=-1)
            tile_idx = cluster_idx * TPC + local_idx
            h = jax.nn.gelu(xf @ compress_w1 + compress_b1, approximate=False)
            comp = jnp.tanh(h @ compress_w2 + compress_b2)
            w1 = spline_w1[tile_idx]
            b1 = spline_b1[tile_idx]
            hh = jax.nn.relu(jnp.einsum('ni,nig->ng', comp, w1) + b1)
            w2 = spline_w2[tile_idx]
            b2 = spline_b2[tile_idx]
            mag = jnp.einsum('ng,ngo->no', hh, w2) + b2
            ffn_out = mag * directions[tile_idx] * output_scale[0]
            y = xf + ffn_out
            mu = y.mean(axis=-1, keepdims=True)
            var = ((y - mu) ** 2).mean(axis=-1, keepdims=True)
            y = (y - mu) / jnp.sqrt(var + EPS_LN) * norm_gamma + norm_beta
            return y.reshape(B, T, D)
        return _forward(x, signatures_raw, knot_values, temperature, compress_w1, compress_b1, compress_w2, compress_b2, spline_w1, spline_b1, spline_w2, spline_b2, directions, norm_gamma, norm_beta, output_scale)

    def _L1_attn_ref(hidden_states, w_attn, b_attn, w_proj, b_proj):
        import jax, jax.numpy as jnp
        import numpy as np
        B, S, D, H = (4, 512, 256, 16)
        HD = D // H
        b, s, d = hidden_states.shape
        qkv = hidden_states @ w_attn + b_attn
        q, k, v = jnp.split(qkv, 3, axis=-1)

        def heads(x):
            return x.reshape(b, s, H, HD).transpose(0, 2, 1, 3)
        q, k, v = (heads(q), heads(k), heads(v))
        scores = jnp.einsum('bhqd,bhkd->bhqk', q, k) / jnp.sqrt(jnp.float32(HD))
        causal = jnp.tril(jnp.ones((s, s), dtype=bool))
        neg = jnp.finfo(scores.dtype).min
        scores = jnp.where(causal[None, None, :, :], scores, neg)
        attn = jax.nn.softmax(scores, axis=-1)
        ctx = jnp.einsum('bhqk,bhkd->bhqd', attn, v)
        ctx = ctx.transpose(0, 2, 1, 3).reshape(b, s, d)
        return ctx @ w_proj + b_proj

    def _L1_xattn_ref(q, k, v, mask, wq, bq, wk, bk, wv, bv, wo, bo):
        import jax, jax.numpy as jnp
        import numpy as np
        import math
        B, S, D, H = (2, 512, 256, 16)
        DK = D // H

        def _split_heads(x):
            b, s, _ = x.shape
            return x.reshape(b, s, H, DK).transpose(0, 2, 1, 3)
        query = _split_heads(q @ wq.T + bq)
        key_h = _split_heads(k @ wk.T + bk)
        value = _split_heads(v @ wv.T + bv)
        scale = 1.0 / math.sqrt(DK)
        scores = jnp.einsum('bhqd,bhkd->bhqk', query, key_h) * scale
        scores = jnp.where(mask == 0, jnp.float32(-1000000000.0), scores)
        attn = jax.nn.softmax(scores, axis=-1)
        x = jnp.einsum('bhqk,bhkd->bhqd', attn, value)
        x = x.transpose(0, 2, 1, 3).reshape(q.shape[0], -1, H * DK)
        return x @ wo.T + bo

    def _L1_ffn_ref(hidden_states, gate_w, Wg, Wu, Wd, sg, su, sd):
        import jax, jax.numpy as jnp
        import numpy as np
        H = 256
        I = 128
        E = 16
        K = 4
        B, S = (2, 256)
        b, s, h = hidden_states.shape
        x = hidden_states.reshape(-1, h)
        T = x.shape[0]
        scores = jax.nn.sigmoid(x @ gate_w.T)
        topk_w, topk_ids = jax.lax.top_k(scores, K)
        topk_w = topk_w / topk_w.sum(-1, keepdims=True)
        comb = jnp.zeros((T, E), dtype=x.dtype).at[jnp.arange(T)[:, None], topk_ids].add(topk_w)
        g = jnp.einsum('th,ehi->tei', x, Wg)
        u = jnp.einsum('th,ehi->tei', x, Wu)
        eo = jnp.einsum('tei,eih->teh', jax.nn.silu(g) * u, Wd)
        routed = jnp.einsum('teh,te->th', eo, comb)
        shared = jax.nn.silu(x @ sg) * (x @ su) @ sd
        return (shared + routed).reshape(b, s, h)
    x = x + _L0_attn_ref(_layernorm(x, axis=-1), L0_attn_Wq, L0_attn_bq, L0_attn_Wk, L0_attn_bk, L0_attn_Wv, L0_attn_bv, L0_attn_Wo, L0_attn_bo)
    x = x + _L0_xattn_ref(ctx_1024, ctx_1024, _layernorm(x, axis=-1), L0_xattn_fm_w, L0_xattn_fm_b, L0_xattn_fc_w, L0_xattn_fc_b)
    x = x + _L0_ffn_ref(_layernorm(x, axis=-1), L0_ffn_signatures_raw, L0_ffn_knot_values, L0_ffn_temperature, L0_ffn_compress_w1, L0_ffn_compress_b1, L0_ffn_compress_w2, L0_ffn_compress_b2, L0_ffn_spline_w1, L0_ffn_spline_b1, L0_ffn_spline_w2, L0_ffn_spline_b2, L0_ffn_directions, L0_ffn_norm_gamma, L0_ffn_norm_beta, L0_ffn_output_scale)
    x = x + _L1_attn_ref(_layernorm(x, axis=-1), L1_attn_w_attn, L1_attn_b_attn, L1_attn_w_proj, L1_attn_b_proj)
    x = x + _L1_xattn_ref(_layernorm(x, axis=-1), ctx_1024, ctx_1024, mask_1x1xSxS2_ik0, L1_xattn_wq, L1_xattn_bq, L1_xattn_wk, L1_xattn_bk, L1_xattn_wv, L1_xattn_bv, L1_xattn_wo, L1_xattn_bo)
    x = x + _L1_ffn_ref(_layernorm(x, axis=-1), L1_ffn_gate_w, L1_ffn_Wg, L1_ffn_Wu, L1_ffn_Wd, L1_ffn_sg, L1_ffn_su, L1_ffn_sd)
    return x

_drawn_inputs = setup_inputs


def setup_inputs(seed=0):
    import zlib

    import numpy as np

    out = dict(_drawn_inputs(seed))
    spreads = {'L0_attn_bq': (0.0, 0.8),
     'L0_attn_bk': (0.0, 0.8),
     'L0_attn_bv': (0.0, 0.1),
     'L0_attn_bo': (0.0, 0.1),
     'L0_xattn_fc_b': (0.0, 0.715),
     'L0_ffn_compress_b1': (0.0, 0.8),
     'L0_ffn_compress_b2': (0.0, 0.8),
     'L0_ffn_spline_b1': (0.0, 0.8),
     'L0_ffn_spline_b2': (0.0, 2.0),
     'L0_ffn_norm_gamma': (1.0, 0.6),
     'L0_ffn_norm_beta': (0.0, 0.8),
     'L1_attn_b_attn': (0.0, 0.8),
     'L1_attn_b_proj': (0.0, 0.8)}
    factors = {'L0_attn_Wq': 8.0,
     'L0_attn_Wk': 8.0,
     'L0_attn_Wv': 6.296,
     'L0_ffn_signatures_raw': 8.0,
     'L0_ffn_knot_values': 8.0,
     'L0_ffn_compress_w1': 8.0,
     'L0_ffn_compress_w2': 8.0,
     'L0_ffn_spline_w1': 8.0,
     'L0_ffn_spline_w2': 8.0,
     'L0_ffn_directions': 8.0,
     'L1_attn_w_attn': 7.404,
     'L1_attn_w_proj': 6.985,
     'L1_xattn_bq': 8.0,
     'L1_xattn_bk': 64.0,
     'L1_xattn_bv': 8.0,
     'L1_xattn_bo': 8.0,
     'L1_ffn_gate_w': 7.052,
     'L1_ffn_Wg': 6.233,
     'L1_ffn_Wu': 5.237,
     'L1_ffn_Wd': 5.661,
     'L1_ffn_sg': 3.194,
     'L1_ffn_su': 2.732,
     'L1_ffn_sd': 2.8}
    for name, (base, spread) in spreads.items():
        noise = np.random.default_rng([zlib.crc32(name.encode()), seed]).standard_normal(out[name].shape)
        drawn = base * np.exp(spread * noise) if base else spread * noise
        out[name] = jnp.asarray(drawn.astype(out[name].dtype))
    for name, factor in factors.items():
        out[name] = (out[name] * factor).astype(out[name].dtype)
    return out
```

```python
from contextlib import ExitStack

import numpy as np

import concourse.bass as bass
from concourse import mybir

BATCH, SEQ, D = 2, 1024, 256
CTX = 77
HEADS, HD = 16, 16
P = 128
TILES = SEQ // P
DC = D // P
GROUPS = 4
HPG = HEADS // GROUPS
STRIP = 32
HALF_HEADS = P // HD
SPAN = 512
SPANS = SEQ // SPAN
TPS = SPAN // P
PARTS = 3
KSTACK = 6 * HD
EXPERTS, TOPK, INNER = 16, 4, 128
TILES_FFN, CLUSTERS, TPC = 64, 8, 8
GRID, COMP, KNOTS = 16, 64, 8
GATE_COLS = CLUSTERS + TILES_FFN + COMP
TABLE = 2 * GRID + GRID + GRID + 1
LN_EPS = 1e-5
DEN_EPS = 1e-6
MASKED = -1e30

F32, BF16, I32 = mybir.dt.float32, mybir.dt.bfloat16, mybir.dt.int32
ALU = mybir.AluOpType
ACT = mybir.ActivationFunctionType
AX = mybir.AxisListType

Q_PARTS = (0, 1, 2, 0, 1, 0)
K_PARTS = (0, 0, 0, 1, 1, 2)

CONSTS = {}
_at = 0
for _name, _width in (("ident", P), ("causal01", P), ("headmask", HALF_HEADS), ("sign", 1), ("iota8", 8), ("parts", EXPERTS),
                      ("before", EXPERTS * EXPERTS), ("halfneg", TILES), ("mask_qk", P), ("mask_kq", P)):
    CONSTS[_name] = (_at, _width)
    _at += _width
CONST_COLS = _at
KEPT_COLS = CONSTS["mask_qk"][0]


def constants():
    c = np.zeros((P, CONST_COLS), np.float32)

    def put(name, value):
        at, width = CONSTS[name]
        c[:, at:at + width] = value

    r, k = np.arange(P)[:, None], np.arange(P)[None, :]
    put("ident", r == k)
    put("causal01", r <= k)
    put("mask_qk", np.where(k <= r, 0.0, MASKED))
    put("mask_kq", np.where(r <= k, 0.0, MASKED))
    put("headmask", r // HD == np.arange(HALF_HEADS)[None, :])
    put("sign", np.where(r % STRIP < HD, 1.0, -1.0))
    put("iota8", np.arange(8)[None, :])
    put("parts", (r % EXPERTS == np.arange(EXPERTS)[None, :]) & (r < PARTS * EXPERTS))
    i, j = np.arange(EXPERTS)[:, None], np.arange(EXPERTS)[None, :]
    put("before", (j < i).reshape(1, -1))
    put("halfneg", -0.5)
    return c


class Engine:

    def __init__(self, engine, sem):
        self.engine, self.sem, self.count, self.waited = engine, sem, 0, {}

    def wait(self, *tokens):
        for token in tokens:
            if token is None:
                continue
            sem, value = token
            if self.waited.get(id(sem), 0) < value:
                self.waited[id(sem)] = value
                self.engine.wait_ge(sem, value)

    def do(self, emit, *waits, signal=True):
        self.wait(*waits)
        instruction = emit(self.engine)
        if not signal:
            return None
        self.count += 1
        instruction.then_inc(self.sem, 1)
        return self.last()

    def dma(self, out, in_, landing, *waits):
        self.wait(*waits)
        landing.count += 16
        self.engine.dma_start(out, in_).then_inc(landing.sem, 16)
        return landing.last()

    def last(self):
        return (self.sem, self.count)


class Slots:

    def __init__(self, buffers):
        self.buffers, self.readers, self.n = buffers, [()] * len(buffers), 0

    def take(self):
        i = self.n % len(self.buffers)
        self.n += 1
        return i, self.buffers[i], self.readers[i]

    def free(self, i, *readers):
        self.readers[i] = readers


def build(nc, A, out, phases="abcdef"):
    with ExitStack() as ctx:
        def sb(name, shape, dt=F32):
            return ctx.enter_context(nc.sbuf_tensor(name, shape, dt))

        sems = {}

        def sem(name):
            sems[name] = ctx.enter_context(nc.semaphore(name))
            return sems[name]

        pe = Engine(nc.tensor, sem("pe_done"))
        act = Engine(nc.scalar, sem("act_done"))
        dve = Engine(nc.vector, sem("dve_done"))
        pool = Engine(nc.gpsimd, sem("pool_done"))
        sp = Engine(nc.sync, sem("sp_done"))

        def landing(name):
            return Engine(None, sem(name))

        psum = ctx.enter_context(nc.psum_tensor("psum", [P, 8, SPAN], F32))
        ring_a = Slots([psum[:, i, :] for i in (0, 1, 2)])
        ring_b = Slots([psum[:, i, :] for i in (3, 4, 5)])
        ring_c = Slots([psum[:, i, :] for i in (6, 7)])

        X = sb("X", [P, BATCH * TILES, D])
        H = [sb(f"H{b}", [P, TILES, D]) for b in range(BATCH)]
        HT = [sb(f"HT{b}", [P, DC, SEQ]) for b in range(BATCH)]
        region_a = sb("region_a", [P, 14336])
        region_b = sb("region_b", [P, 13056])
        work = Slots([sb(f"work{i}", [P, SPAN]) for i in range(8)])
        raw = Slots([sb(f"raw{i}", [P, SPAN]) for i in range(1)])
        W1 = sb("W1", [P, 2048])
        W2 = sb("W2", [P, 2048])
        consts = sb("const_tile", [P, KEPT_COLS])
        ident_bf = sb("ident_bf", [P, P], BF16)
        mask_qk_bf = sb("mask_qk_bf", [P, P], BF16)
        mask_kq_bf = sb("mask_kq_bf", [P, P], BF16)
        bias_row = sb("bias_row", [P, 6, D])
        bias_col = sb("bias_col", [P, 17])
        stats = [sb(f"stats{b}", [P, TILES, 6]) for b in range(BATCH)]
        mv = [sb(f"mv{b}", [P, TILES, 2]) for b in range(BATCH)]
        rstd = [sb(f"rstd{b}", [P, 2, TILES]) for b in range(BATCH)]
        small = sb("small", [P, 456])

        masks_once = region_b[:, 0:CONST_COLS - KEPT_COLS]

        def const(name):
            at, width = CONSTS[name]
            if at >= KEPT_COLS:
                return masks_once[:, at - KEPT_COLS:at - KEPT_COLS + width]
            return consts[:, at:at + width]

        ident = const("ident")

        def carve(region, at, n, dt=F32):
            view = region[:, at:at + n]
            return view if dt is F32 else view.bitcast(dt)

        parts_words = DC * PARTS * SEQ // 2
        parts = {n: carve(region_a, i * parts_words, parts_words, BF16).rearrange("p (m s t) -> p m s t", m=DC, s=PARTS)
                 for i, n in enumerate("qk")}
        stack_words = HPG * SEQ // 2
        stacks = Slots([{n: carve(region_a, 2 * parts_words + (2 * s + i) * stack_words, stack_words, BF16)
                         .rearrange("p (j t) -> p j t", j=HPG) for i, n in enumerate("qk")} for s in range(2)])
        stack_landing = [landing(f"stack_landed{s}") for s in range(2)]
        max_landing = [landing(f"max_landed{s}") for s in range(2)]

        vaug = [carve(region_b, b * 4096, 4096).rearrange("p (t h e) -> p t h e", t=TILES, h=HEADS) for b in range(BATCH)]
        qfeat = carve(region_b, 4096, 2048).rearrange("p (m t) -> p m t", m=DC)
        ktok = carve(region_b, 6144, 2048).rearrange("p (t d) -> p t d", t=TILES)
        state = carve(region_b, 8192, 7 * SPAN).rearrange("p (c n) -> p c n", c=7)

        loads = {}

        def load(group, dst, src, *waits):
            if group not in loads:
                loads[group] = landing(f"landed_{group}")
            return sp.dma(dst, src, loads[group], *waits)

        def spread(vector, n, partitions=P):
            return vector.rearrange("(a n) -> a n", a=1).to_broadcast([partitions, n])

        def rows(name, n):
            return spread(A[name], n)

        x_tiles = A["x"].rearrange("b (t p) d -> p (b t) d", p=P)
        x_landed = [load(f"x{b}", X[:, b * TILES:(b + 1) * TILES, :], x_tiles[:, b * TILES:(b + 1) * TILES, :])
                    for b in range(1)]
        load("consts", consts[:, :], A["consts"][:, 0:KEPT_COLS])
        consts_landed = load("consts", masks_once, A["consts"][:, KEPT_COLS:])
        w_attn0 = W1[:, :].rearrange("p (c n) -> p c n", c=DC)
        w0_landed = load("w0", w_attn0, A["L0_attn_w"].rearrange("(c p) n -> p c n", p=P))
        for i, n in enumerate(("L0_attn_bk", "L0_attn_bv", "L0_attn_bo")):
            row0_landed = load("row0", bias_row[:, i, :], rows(n, D))
        cols_landed = load("cols", bias_col[:, 0:16], A["bias_cols"])
        x_landed.append(load("x1", X[:, TILES:, :], x_tiles[:, TILES:, :]))
        w_fc = W2[:, 0:1024].rearrange("p (g n) -> p g n", g=GROUPS)
        wa_landed = load("wa", w_fc, A["fc_w_t"].rearrange("(g p) n -> p g n", p=P))

        casts = [act.do(lambda e, o=o, n=n: e.copy(o[:, :], const(n)), consts_landed)
                 for o, n in ((ident_bf, "ident"), (mask_qk_bf, "mask_qk"), (mask_kq_bf, "mask_kq"))]
        masks_ready = casts[-1]

        x_ready = [[x_landed[b]] * TILES for b in range(BATCH)]
        batch_free = [[] for _ in range(BATCH)]
        region_a_free, region_b_free = [], [masks_ready]
        w1_free, w2_free = [], []

        def lasts():
            return [pe.last(), act.last(), dve.last(), pool.last()]

        def normalise(b):
            h, ht, base = H[b], HT[b], b * TILES
            ready, ht_ready = [], []
            for half in range(2):
                ts = range(half * 4, half * 4 + 4)
                for t in ts:
                    s = dve.do(lambda e, t=t: e.bn_stats(stats[b][:, t, :], X[:, base + t, :]), x_ready[b][t], *batch_free[b])
                    done = dve.do(lambda e, t=t: e.bn_aggr(mv[b][:, t, :], stats[b][:, t, :]), s)
                sl = slice(half * 4, half * 4 + 4)
                v = pool.do(lambda e, sl=sl: e.tensor_scalar(rstd[b][:, 0, sl], mv[b][:, sl, 1], LN_EPS, None, ALU.add), done,
                            consts_landed)
                v = pool.do(lambda e, sl=sl: e.tensor_tensor(rstd[b][:, 1, sl], rstd[b][:, 0, sl],
                                                             const("halfneg")[:, 0:4], ALU.pow), v)
                for t in ts:
                    ready.append(dve.do(lambda e, t=t: e.tensor_scalar(
                        h[:, t, :], X[:, base + t, :], mv[b][:, t, 0:1], rstd[b][:, 1, t:t + 1], ALU.subtract, ALU.mult), v))
            for pair in range(TILES // 2):
                ht_ready.append(turn(h, ht, b, pair, ready[2 * pair + 1]))
            return ready, ht_ready

        def turn(src, dst, b, pair, src_ready):
            i, bank, free = ring_a.take()
            for q in range(4):
                t, c = 2 * pair + q // 2, q % 2
                done = pe.do(lambda e, q=q, t=t, c=c, bank=bank: e.transpose(bank[:, q * P:(q + 1) * P], src[:, t, c * P:(c + 1) * P], ident),
                             src_ready, consts_landed, *free, signal=q == 3)
            copied = act.do(lambda e, bank=bank: e.copy(
                dst[:, :, pair * 2 * P:(pair + 1) * 2 * P].rearrange("p c (t n) -> p t c n", t=2),
                bank.rearrange("p (t c n) -> p t c n", t=2, c=DC)), done, *batch_free[b])
            ring_a.free(i, copied)
            return copied

        def add_bias(b, bias, landed, *readers):
            sl = slice(b * TILES, (b + 1) * TILES)
            return pool.do(lambda e: e.tensor_tensor(X[:, sl, :], X[:, sl, :],
                                                     bias.unsqueeze(1).to_broadcast([P, TILES, D]), ALU.add), landed, *readers)

        def project_out(b, chunks, weight, waits_for, extra):
            for pair in range(TILES // 2):
                i, bank, free = ring_a.take()
                for q in range(2):
                    t = 2 * pair + q
                    for c, chunk in enumerate(chunks):
                        done = pe.do(lambda e, q=q, t=t, c=c, chunk=chunk, bank=bank: e.matmul(
                            bank[:, q * D:(q + 1) * D], chunk[:, t * P:(t + 1) * P], weight[:, c, :],
                            start=(q == 0 and c == 0), stop=(c == len(chunks) - 1), skip_group_check=True),
                            *waits_for(t), *free, signal=(q == 1 and c == len(chunks) - 1))
                t0 = b * TILES + 2 * pair
                added = dve.do(lambda e, t0=t0, bank=bank: e.tensor_tensor(
                    X[:, t0:t0 + 2, :], X[:, t0:t0 + 2, :], bank.rearrange("p (t d) -> p t d", t=2), ALU.add), done, *extra)
                ring_a.free(i, added)
                x_ready[b][2 * pair] = x_ready[b][2 * pair + 1] = added
            batch_free[b] = lasts()

        parts_free = [[], []]
        vaug_ready = {}
        first_fill = {}

        def split(name, m, n, f, f_ready, *free):
            dst = parts[name]
            cols = slice(n * SPAN, (n + 1) * SPAN)
            hi = act.do(lambda e: e.copy(dst[:, m, 0, cols], f), f_ready, *free)
            j, rest, rest_free = work.take()
            r1 = dve.do(lambda e: e.tensor_tensor(rest[:, :], f, dst[:, m, 0, cols], ALU.subtract), hi, *rest_free)
            mid = act.do(lambda e: e.copy(dst[:, m, 1, cols], rest[:, :]), r1)
            lo = pool.do(lambda e: e.tensor_tensor(dst[:, m, 2, cols], rest[:, :], dst[:, m, 1, cols], ALU.subtract), mid, *free)
            work.free(j, lo, mid)
            return lo, r1

        def load_stacks(g, parts_ready):
            s, stack, free = stacks.take()
            for name, which in (("q", Q_PARTS), ("k", K_PARTS)):
                for r, part in enumerate(which):
                    for j in range(HPG):
                        head = g * HPG + j
                        row = head % HALF_HEADS * HD
                        landed = sp.dma(stack[name][r * HD:(r + 1) * HD, j, :],
                                        parts[name][row:row + HD, head // HALF_HEADS, part, :],
                                        stack_landing[s], *parts_ready, *free)
            return s, stack, landed

        def ones_column(va, *waits):
            z = pool.do(lambda e: e.memset(va[:, :, :, HD:STRIP], 0.0), *waits)
            return pool.do(lambda e: e.memset(va[:, :, :, HD:HD + 1], 1.0), z)

        def head_outputs(b, g, c, bank_i, bank, pv_done, eps):
            r, o, free = raw.take()
            copied = act.do(lambda e: e.copy(o[:, :], bank), pv_done, *free)
            ring_c.free(bank_i, copied)
            i, tb, tfree = ring_a.take()
            for t in range(TPS):
                turned = pe.do(lambda e, t=t: e.transpose(tb[:, t * P:(t + 1) * P], o[:, t * P:(t + 1) * P], ident),
                               copied, *tfree, signal=t == TPS - 1)
            raw.free(r, turned)
            v = tb.rearrange("p (t j e) -> p t j e", t=TPS, j=HPG)
            den = small[:, 0:16].rearrange("p (t j) -> p t j", t=TPS)
            if eps:
                d = dve.do(lambda e: e.tensor_scalar(den, v[:, :, :, HD], eps, None, ALU.max), turned, dve.last())
                d = dve.do(lambda e: e.reciprocal(den, den), d)
            else:
                d = dve.do(lambda e: e.reciprocal(den, v[:, :, :, HD]), turned, dve.last())
            dst = H[b][:, c * TPS:(c + 1) * TPS, g * HPG * HD:(g + 1) * HPG * HD].rearrange("p t (j e) -> p t j e", j=HPG)
            done = dve.do(lambda e: e.tensor_tensor(dst, v[:, :, :, 0:HD], den.unsqueeze(3).to_broadcast([P, TPS, HPG, HD]),
                                                    ALU.mult), d, *batch_free[b])
            ring_a.free(i, done)
            return done

        def linear_attention(b):
            nonlocal region_a_free, region_b_free
            h_ready, ht_ready = normalise(b)
            biased = add_bias(b, bias_row[:, 2, :], row0_landed, h_ready[-1])
            ht, va = HT[b], vaug[0]
            free_b = list(region_b_free)
            if b == 0:
                first_fill["v0"] = ones_column(va, *free_b)
            parts_ready = []
            for name, wcol, bcol in (("q", 0, 0), ("k", D, 2)):
                for m in range(DC):
                    for n in range(SPANS):
                        i, bank, free = ring_b.take()
                        for c in range(DC):
                            done = pe.do(lambda e, c=c, m=m, n=n, wcol=wcol, bank=bank: e.matmul(
                                bank, w_attn0[:, c, wcol + m * P:wcol + (m + 1) * P], ht[:, c, n * SPAN:(n + 1) * SPAN],
                                start=c == 0, stop=c == DC - 1), w0_landed, ht_ready[2 * n + 1], *free, signal=c == DC - 1)
                        bias = bias_col[:, bcol + m:bcol + m + 1]
                        j1, low, low_free = work.take()
                        j2, pos, pos_free = work.take()
                        z = act.do(lambda e: e.activation(pos[:, :], bank, ACT.Identity, bias=bias), done, cols_landed, *pos_free)
                        ring_b.free(i, z)
                        t = dve.do(lambda e: e.tensor_scalar(low[:, :], pos[:, :], 0.0, None, ALU.min), z, *low_free)
                        t = act.do(lambda e: e.activation(low[:, :], low[:, :], ACT.Exp), t)
                        f = qfeat[:, m, n * SPAN:(n + 1) * SPAN] if name == "q" else pos[:, :]
                        f_done = dve.do(lambda e: e.scalar_tensor_tensor(f, pos[:, :], 0.0, low[:, :], ALU.max, ALU.add), t, *free_b)
                        work.free(j1, f_done)
                        lo, r1 = split(name, m, n, f, f_done, *parts_free[0], *region_a_free)
                        work.free(j2, f_done, r1)
                        parts_ready.append(lo)
            q_ready = parts_ready[:2 * DC]
            tok_ready = []
            for t in range(TILES):
                i, bank, free = ring_b.take()
                for c in range(DC):
                    done = pe.do(lambda e, c=c, t=t, bank=bank: e.matmul(bank, ht[:, c, t * P:(t + 1) * P], w_attn0[:, c, D:3 * D],
                                                              start=c == 0, stop=c == DC - 1), w0_landed, ht_ready[t // 2], *free, signal=c == DC - 1)
                j1, z, zfree = work.take()
                j2, low, low_free = work.take()
                zd = dve.do(lambda e, z=z, bank=bank: e.tensor_tensor(z[:, 0:D], bank[:, 0:D], bias_row[:, 0, :], ALU.add), done, row0_landed, *zfree)
                vd = dve.do(lambda e, t=t, bank=bank: e.tensor_tensor(
                    va[:, t, :, 0:HD], bank[:, D:2 * D].rearrange("p (h e) -> p h e", h=HEADS),
                    bias_row[:, 1, :].rearrange("p (h e) -> p h e", h=HEADS), ALU.add), done, *free_b)
                ring_b.free(i, zd, vd)
                l = dve.do(lambda e, z=z, low=low: e.tensor_scalar(low[:, 0:D], z[:, 0:D], 0.0, None, ALU.min), zd, *low_free)
                l = act.do(lambda e, low=low: e.activation(low[:, 0:D], low[:, 0:D], ACT.Exp), l)
                kd = dve.do(lambda e, t=t, z=z, low=low: e.scalar_tensor_tensor(ktok[:, t, :], z[:, 0:D], 0.0, low[:, 0:D], ALU.max, ALU.add), l)
                work.free(j1, kd)
                work.free(j2, kd)
                tok_ready.append(kd)
            bank_i, sbank, sfree = ring_c.take()
            state_ready = [None]
            copied = None
            for c in range(TILES - 1):
                for half in range(DC):
                    done = pe.do(lambda e, c=c, half=half: e.matmul(
                        sbank[:, half * D:(half + 1) * D], ktok[:, c, half * P:(half + 1) * P],
                        va[:, c, half * HALF_HEADS:(half + 1) * HALF_HEADS, :].rearrange("p h e -> p (h e)"),
                        start=(c == 0 and half == 0), stop=True, skip_group_check=True),
                        tok_ready[c], first_fill["v0"], copied, *sfree, signal=half == DC - 1)
                copied = dve.do(lambda e, c=c: e.tensor_tensor(
                    state[:, c, :].rearrange("p (m h e) -> p m h e", m=DC, h=HALF_HEADS),
                    sbank.rearrange("p (m h e) -> p m h e", m=DC, h=HALF_HEADS),
                    const("headmask").unsqueeze(1).unsqueeze(3).to_broadcast([P, DC, HALF_HEADS, STRIP]), ALU.mult), done)
                state_ready.append(copied)
            ring_c.free(bank_i, copied)
            out_done = []
            loaded = load_stacks(0, parts_ready)
            for g in range(GROUPS):
                s, stack, landed = loaded
                if g + 1 < GROUPS:
                    loaded = load_stacks(g + 1, parts_ready)
                items = []
                for c in range(SPANS):
                    items += [(c, q) for q in range(TPS)]
                outs = {}
                pending = {}

                def scores(item):
                    c, q = item
                    t = c * TPS + q
                    i, bank, free = ring_b.take()
                    for j in range(HPG):
                        done = pe.do(lambda e, j=j: e.matmul(
                            bank[:, j * P:(j + 1) * P], stack["k"][0:KSTACK, j, t * P:(t + 1) * P],
                            stack["q"][0:KSTACK, j, t * P:(t + 1) * P], start=j == 0, stop=True, skip_group_check=True),
                            landed, *free, signal=j == HPG - 1)
                    w, a, afree = work.take()
                    masked = dve.do(lambda e: e.tensor_tensor(
                        a[:, :].rearrange("p (j n) -> p j n", j=HPG), bank.rearrange("p (j n) -> p j n", j=HPG),
                        const("causal01").unsqueeze(1).to_broadcast([P, HPG, P]), ALU.mult), done, *afree)
                    ring_b.free(i, masked)
                    pending[item] = (w, a, masked)

                def sums(item):
                    c, q = item
                    t = c * TPS + q
                    w, a, masked = pending.pop(item)
                    if q == 0:
                        outs[c] = ring_c.take()
                    bank_i, bank, free = outs[c]
                    if t:
                        pe.do(lambda e: e.matmul(bank[:, q * P:(q + 1) * P],
                                                 state[:, t - 1, g * P:(g + 1) * P],
                                                 qfeat[:, g // 2, t * P:(t + 1) * P], start=q == 0, stop=False, skip_group_check=True),
                              state_ready[t], *q_ready, *free, signal=False)
                    for j in range(HPG):
                        done = pe.do(lambda e, j=j: e.matmul(
                            bank[j * STRIP:(j + 1) * STRIP, q * P:(q + 1) * P], va[:, t, g * HPG + j, :],
                            a[:, j * P:(j + 1) * P], start=t == 0, stop=True, skip_group_check=True),
                            masked, tok_ready[t], *free, signal=j == HPG - 1)
                    work.free(w, done)
                    if q == TPS - 1:
                        out_done.append(head_outputs(b, g, c, bank_i, bank, done, DEN_EPS))

                for n in range(len(items) + 2):
                    if n < len(items):
                        scores(items[n])
                    if n >= 2:
                        sums(items[n - 2])
                stacks.free(s, pe.last())
            parts_free[0] = [landed]
            region_b_free = lasts()
            region_a_free = lasts() + [landed]
            finish_attention(b, out_done[-1], w_attn0[:, :, 3 * D:4 * D], w0_landed, biased)

        def finish_attention(b, outputs_ready, weight, weight_landed, biased):
            turned = [turn(H[b], HT[b], b, pair, outputs_ready) for pair in range(TILES // 2)]
            project_out(b, [HT[b][:, c, :] for c in range(DC)], weight, lambda t: [turned[t // 2], weight_landed], [biased])

        qx = carve(region_a, 0, 4096).rearrange("p (g t) -> p g t", g=GROUPS)
        ox = carve(region_a, 4096, 4096).rearrange("p (g t) -> p g t", g=GROUPS)
        pt = Slots([carve(region_a, 8192 + 2048 * s, 2048).rearrange("p (j t) -> p j t", j=HPG) for s in range(2)])
        kbd = carve(region_a, 12288, GROUPS * HPG * CTX).rearrange("p (g j k) -> p g j k", g=GROUPS, j=HPG)
        vx = carve(region_a, 13520, HEADS * STRIP).rearrange("p (h e) -> p h e", h=HEADS)
        ctx_t = sb("ctx_t", [P, BATCH, DC, CTX])
        ctx_landed = load("ctx", ctx_t[:, :, :, :], A["ctx_t"].rearrange("b (c p) k -> p b c k", p=P))
        fmbd = sb("fmbd", [P, 2, P])
        fm_row = sb("fm_row", [CTX, 2, HPG * STRIP])
        load("fm", fmbd[:, :, :], A["fm_bd"].rearrange("v p n -> p v n"))
        load("fm", fm_row[:, 0, :], A["fm_b_row"].to_broadcast([CTX, P]))
        fm_landed = load("fm", fm_row[:, 1, :], A["sign_row"].to_broadcast([CTX, P]))
        load("row1", bias_row[:, 3, :], rows("L0_xattn_fc_b", D))
        load("row1", bias_row[:, 4, :], rows("L0_ffn_norm_gamma", D))
        row1_landed = load("row1", bias_row[:, 5, :], rows("L0_ffn_norm_beta", D))
        mask_i = region_a[:, 0:TILES * CTX].bitcast(I32).rearrange("p (t k) -> p t k", t=TILES)
        maskneg = sb("maskneg", [P, TILES, CTX], BF16)
        mask_landed = load("mask", mask_i, A["mask"].rearrange("(t p) k -> p t k", p=P))
        fm_b_signed = pool.do(lambda e: e.tensor_tensor(bias_col[:, 16:17], bias_col[:, 4:5], const("sign"), ALU.mult),
                              cols_landed, consts_landed)

        def context_attention(b, q_halves, q_ready, kv_ready, heads_v, masked):
            groups_out = {}
            for c in range(SPANS):
                for g in range(GROUPS):
                    pi, p_t, pt_free = pt.take()
                    items = list(range(TPS))
                    hold = {}

                    def soft(q):
                        t = c * TPS + q
                        i, bank, free = ring_b.take()
                        s = bank[:, 0:HPG * CTX]
                        done = pe.do(lambda e: e.matmul(
                            s, qx[:, g if q_halves == GROUPS else g // 2, t * P:(t + 1) * P],
                            kbd[:, g, :, :].rearrange("p j k -> p (j k)"), start=True, stop=not masked, skip_group_check=True),
                            *q_ready, *kv_ready, *free)
                        if masked:
                            done = pe.do(lambda e: e.matmul(
                                s.rearrange("p (j k) -> p j k", j=HPG), ident_bf[:, :],
                                maskneg[:, t, :].unsqueeze(1).to_broadcast([P, HPG, CTX]), start=False, stop=True,
                                skip_group_check=True), masks_ready, mask_ready)
                        s3 = s.rearrange("p (j k) -> p j k", j=HPG)
                        at = 32 + 16 * (t % 4)
                        mx, den = small[:, at:at + HPG], small[:, at + 4:at + 8]
                        m = dve.do(lambda e: e.tensor_reduce(mx, s3, AX.X, ALU.max), done, small_free.get(at))
                        w, ex, wfree = work.take()
                        ex3 = ex[:, 0:HPG * CTX].rearrange("p (j k) -> p j k", j=HPG)
                        d = dve.do(lambda e: e.tensor_tensor(ex3, s3, mx.unsqueeze(2).to_broadcast([P, HPG, CTX]),
                                                             ALU.subtract), m, *wfree)
                        ring_b.free(i, d)
                        scale = rowany[:, t:t + 1] if masked else 1.0
                        x = act.do(lambda e: e.activation(ex[:, 0:HPG * CTX], ex[:, 0:HPG * CTX], ACT.Exp, scale=scale), d)
                        r = dve.do(lambda e: e.tensor_reduce(den, ex3, AX.X, ALU.add), x)
                        r = dve.do(lambda e: e.reciprocal(den, den), r)
                        n = pool.do(lambda e: e.tensor_tensor(ex3, ex3, den.unsqueeze(2).to_broadcast([P, HPG, CTX]), ALU.mult), r)
                        small_free[at] = n
                        hold[q] = (w, ex, n)

                    def turn_p(q):
                        w, ex, n = hold[q]
                        i, bank, free = ring_a.take()
                        for j in range(HPG):
                            done = pe.do(lambda e, j=j: e.transpose(bank[0:CTX, j * P:(j + 1) * P], ex[:, j * CTX:(j + 1) * CTX], ident),
                                         n, *free, signal=j == HPG - 1)
                        work.free(w, done)
                        copied = act.do(lambda e: e.copy(p_t[0:CTX, :, q * P:(q + 1) * P], bank[0:CTX, :].rearrange("p (j n) -> p j n", j=HPG)),
                                        done, *pt_free)
                        ring_a.free(i, copied)
                        return copied

                    yield from run_staged(items, soft, turn_p)
                    copied = act.last()
                    if heads_v == 1 or g % 2 == 0:
                        groups_out[c] = ring_c.take()
                    oi, obank, ofree = groups_out[c]
                    for j in range(HPG):
                        head = g * HPG + j
                        strip = j if heads_v == 1 else (head % HALF_HEADS) // 2
                        done = pe.do(lambda e, j=j, head=head, strip=strip: e.matmul(
                            obank[strip * STRIP:(strip + 1) * STRIP, :], vx[0:CTX, head, :], p_t[0:CTX, j, :],
                            start=(heads_v == 1 or head % 2 == 0), stop=(heads_v == 1 or head % 2 == 1), skip_group_check=True),
                            copied, *kv_ready, *ofree, signal=j == HPG - 1)
                    pt.free(pi, done)
                    if heads_v == 1 or g % 2 == 1:
                        slot = g if heads_v == 1 else g // 2
                        copied = act.do(lambda e, slot=slot, obank=obank: e.copy(ox[:, slot, c * SPAN:(c + 1) * SPAN], obank), done, *ox_free)
                        ring_c.free(oi, copied)
                        ox_ready[c] = copied

        small_free = {}
        ox_free = []
        ox_ready = {}

        def run_staged(items, first, second, lag=2):
            for n in range(len(items) + lag):
                if n < len(items):
                    first(items[n])
                if n >= lag:
                    second(items[n - lag])
                yield

        def feature_attention(b):
            nonlocal region_a_free, ox_free
            h_ready, ht_ready = normalise(b)
            biased = add_bias(b, bias_row[:, 3, :], row1_landed, h_ready[-1])
            free_a = list(region_a_free)
            q_ready = []
            for g in range(GROUPS):
                for n in range(SPANS):
                    i, bank, free = ring_b.take()
                    done = pe.do(lambda e, g=g, n=n, bank=bank: e.matmul(bank, fmbd[:, g % 2, :], HT[b][:, g // 2, n * SPAN:(n + 1) * SPAN],
                                                              start=True, stop=True), fm_landed, ht_ready[2 * n + 1], *free)
                    q = act.do(lambda e, g=g, n=n, bank=bank: e.activation(qx[:, g, n * SPAN:(n + 1) * SPAN], bank, ACT.Exp,
                                                                bias=bias_col[:, 16:17], scale=const("sign")), done, fm_b_signed, *free_a)
                    ring_b.free(i, q)
                    q_ready.append(q)
            z = pool.do(lambda e: e.memset(kbd[:, :, :, :], 0.0), *free_a)
            kv_ready = []
            for g in range(GROUPS):
                i, bank, free = ring_b.take()
                done = pe.do(lambda e, g=g, bank=bank: e.matmul(bank[:, 0:CTX], fmbd[:, g % 2, :], ctx_t[:, b, g // 2, :], start=True, stop=True),
                             fm_landed, ctx_landed, *free)
                for j in range(HPG):
                    st = slice(j * STRIP, (j + 1) * STRIP)
                    k = act.do(lambda e, g=g, j=j, st=st, bank=bank: e.activation(kbd[st, g, j, :], bank[st, 0:CTX], ACT.Exp, bias=bias_col[st, 16:17],
                                                                       scale=const("sign")[st, :]), done, z)
                ring_b.free(i, k)
                kv_ready.append(dve.do(lambda e, g=g: e.tensor_scalar(kbd[:, g, :, :], kbd[:, g, :, :], 1.0 / 16.0, None, ALU.mult), k))
                i, bank, free = ring_b.take()
                done = pe.do(lambda e, g=g, bank=bank: e.matmul(bank[0:CTX, 0:P], ctx_t[:, b, g // 2, :], fmbd[:, g % 2, :], start=True, stop=True), *free)
                j1, tmp, tfree = work.take()
                s = dve.do(lambda e, bank=bank, tmp=tmp: e.tensor_tensor(tmp[0:CTX, 0:P], bank[0:CTX, 0:P], fm_row[:, 0, :], ALU.add), done, fm_landed, *tfree)
                ring_b.free(i, s)
                s = dve.do(lambda e, tmp=tmp: e.tensor_tensor(tmp[0:CTX, 0:P], tmp[0:CTX, 0:P], fm_row[:, 1, :], ALU.mult), s)
                s = act.do(lambda e, g=g, tmp=tmp: e.activation(vx[0:CTX, g * HPG:(g + 1) * HPG, :].rearrange("p h e -> p (h e)"), tmp[0:CTX, 0:P],
                                                     ACT.Exp), s, *free_a)
                work.free(j1, s)
                kv_ready.append(s)
            for _ in context_attention(b, GROUPS, q_ready, kv_ready, 1, False):
                pass
            project_out(b, [ox[:, g, :] for g in range(GROUPS)], w_fc, lambda t: [ox_ready[t // TPS], wa_landed], [biased])
            region_a_free = lasts()
            ox_free = lasts()

        gate_w = W2[:, 1024:1024 + DC * GATE_COLS].rearrange("p (c n) -> p c n", c=DC)
        table = W2[:, 1300:1300 + TABLE + D]
        raw_t = W2[:, 1640:1640 + DC * TILES_FFN].rearrange("p (c n) -> p c n", c=DC)
        ffn_rows = sb("ffn_rows", [P, 3 * COMP + 2 + KNOTS + 2])
        load("ffn", raw_t, A["sig_t"].rearrange("(c p) n -> p c n", p=P))
        load("ffn", gate_w[:, :, CLUSTERS + TILES_FFN:], A["L0_ffn_compress_w1"].rearrange("(c p) n -> p c n", p=P))
        load("ffn", table[0:TILES_FFN, :], A["spline_table"])
        R_B1, R_W2, R_B2, R_KN, R_TEMP, R_SCALE = 0, COMP, 3 * COMP, 3 * COMP + 2, 3 * COMP + 2 + KNOTS, 3 * COMP + 3 + KNOTS
        load("ffn", ffn_rows[:, R_B1:R_B1 + COMP], rows("L0_ffn_compress_b1", COMP))
        load("ffn", ffn_rows[:, R_W2:R_W2 + 2 * COMP], A["compress_w2_t"].rearrange("(a i) n -> a (i n)", a=1).to_broadcast([P, 2 * COMP]))
        load("ffn", ffn_rows[:, R_B2:R_B2 + 2], rows("L0_ffn_compress_b2", 2))
        load("ffn", ffn_rows[:, R_KN:R_KN + KNOTS], rows("L0_ffn_knot_values", KNOTS))
        load("ffn", ffn_rows[:, R_TEMP:R_TEMP + 1], rows("L0_ffn_temperature", 1))
        ffn_landed = load("ffn", ffn_rows[:, R_SCALE:R_SCALE + 1], rows("L0_ffn_output_scale", 1))

        def ffn_weights():
            q = small[:, 128:256].rearrange("p (c n) -> p c n", c=DC)
            n = small[:, 256:384].rearrange("p (c n) -> p c n", c=DC)
            a = dve.do(lambda e: e.tensor_scalar(q, raw_t, 0.3, None, ALU.is_gt), ffn_landed)
            bb = dve.do(lambda e: e.tensor_scalar(n, raw_t, -0.3, None, ALU.is_lt), ffn_landed)
            a = dve.do(lambda e: e.tensor_tensor(q, q, n, ALU.subtract), a, bb)
            a = dve.do(lambda e: e.tensor_tensor(q, q, raw_t, ALU.subtract), a)
            sig = gate_w[:, :, CLUSTERS:CLUSTERS + TILES_FFN]
            a = dve.do(lambda e: e.tensor_tensor(sig, raw_t, q, ALU.add), a)
            cs = small[:, 384:400].rearrange("p (c n) -> p c n", c=DC)
            a = dve.do(lambda e: e.tensor_reduce(cs, sig.rearrange("p c (n k) -> p c n k", k=TPC), AX.X, ALU.add), a)
            pos = small[:, 400:416].rearrange("p (c n) -> p c n", c=DC)
            neg = small[:, 416:432].rearrange("p (c n) -> p c n", c=DC)
            a1 = dve.do(lambda e: e.tensor_scalar(pos, cs, 0.0, None, ALU.is_gt), a)
            a2 = dve.do(lambda e: e.tensor_scalar(neg, cs, 0.0, None, ALU.is_lt), a)
            a = dve.do(lambda e: e.tensor_tensor(gate_w[:, :, 0:CLUSTERS], pos, neg, ALU.subtract), a2)
            a = dve.do(lambda e: e.tensor_tensor(small[:, 440:440 + KNOTS - 1], ffn_rows[:, R_KN + 1:R_KN + KNOTS],
                                                 ffn_rows[:, R_KN:R_KN + KNOTS - 1], ALU.subtract), a)
            a = dve.do(lambda e: e.tensor_scalar(small[:, 448:449], ffn_rows[:, R_TEMP:R_TEMP + 1], 1e-6, None, ALU.add), a)
            a = dve.do(lambda e: e.reciprocal(small[:, 449:450], small[:, 448:449]), a)
            return dve.do(lambda e: e.tensor_scalar(small[:, 450:451], small[:, 449:450], -1.0, None, ALU.mult), a)

        def calibrate(dst, s, scratch, ready):
            u, low, diff, step = scratch
            a = act.do(lambda e: e.activation(u, s, ACT.Exp, scale=small[:, 450:451]), ready)
            a = dve.do(lambda e: e.tensor_scalar(u, u, 1.0, None, ALU.add), a)
            a = dve.do(lambda e: e.reciprocal(u, u), a)
            a = dve.do(lambda e: e.tensor_scalar(u, u, float(KNOTS - 1), None, ALU.mult), a)
            a = dve.do(lambda e: e.tensor_scalar(low, u, 1.0, None, ALU.is_ge), a)
            for k in range(2, KNOTS - 1):
                a = dve.do(lambda e, k=k: e.scalar_tensor_tensor(low, u, float(k), low, ALU.is_ge, ALU.add), a)
            a = dve.do(lambda e: e.tensor_tensor(u, u, low, ALU.subtract), a)
            a = dve.do(lambda e: e.tensor_scalar(dst, low, 0.0, ffn_rows[:, R_KN:R_KN + 1], ALU.is_equal, ALU.mult), a)
            a = dve.do(lambda e: e.tensor_scalar(diff, low, 0.0, small[:, 440:441], ALU.is_equal, ALU.mult), a)
            for k in range(1, KNOTS - 1):
                for acc, col in ((dst, ffn_rows[:, R_KN + k:R_KN + k + 1]), (diff, small[:, 440 + k:441 + k])):
                    a = dve.do(lambda e, k=k, col=col: e.tensor_scalar(step, low, float(k), col, ALU.is_equal, ALU.mult), a)
                    a = dve.do(lambda e, acc=acc: e.tensor_tensor(acc, acc, step, ALU.add), a)
            a = dve.do(lambda e: e.tensor_tensor(diff, diff, u, ALU.mult), a)
            return dve.do(lambda e: e.tensor_tensor(dst, dst, diff, ALU.add), a)

        def first_max(onehot, g, scratch, col, ready):
            eq = scratch
            a = dve.do(lambda e: e.tensor_reduce(col, g, AX.X, ALU.max), ready)
            a = dve.do(lambda e: e.tensor_tensor(eq, g, col.unsqueeze(2).to_broadcast([P, TILES, 8]), ALU.is_equal), a)
            a = dve.do(lambda e: e.tensor_scalar(onehot, const("iota8").unsqueeze(1).to_broadcast([P, TILES, 8]), -8.0, None, ALU.add), a)
            a2 = dve.do(lambda e: e.tensor_tensor(eq, eq, onehot, ALU.mult), a)
            a3 = dve.do(lambda e: e.tensor_reduce(col, eq, AX.X, ALU.min), a2)
            return dve.do(lambda e: e.tensor_tensor(onehot, onehot, col.unsqueeze(2).to_broadcast([P, TILES, 8]), ALU.is_equal), a3)

        def spline_ffn(b):
            nonlocal region_a_free
            weights_ready = weights_done[0]
            h_ready, ht_ready = normalise(b)
            at = [b * 7168]

            def area(n, shape=None):
                v = carve(region_a, at[0], n)
                at[0] += n
                return v
            S = area(TILES * GATE_COLS).rearrange("p (t n) -> p t n", t=TILES)
            free_a = list(region_a_free)
            s_ready = []
            for t in range(TILES):
                i, bank, free = ring_b.take()
                for c in range(DC):
                    done = pe.do(lambda e, c=c, t=t, bank=bank: e.matmul(bank[:, 0:GATE_COLS], HT[b][:, c, t * P:(t + 1) * P], gate_w[:, c, :],
                                                              start=c == 0, stop=c == DC - 1), weights_ready, ht_ready[t // 2], *free, signal=c == 1)
                s = act.do(lambda e, t=t, bank=bank: e.copy(S[:, t, :], bank[:, 0:GATE_COLS]), done, *free_a)
                ring_b.free(i, s)
            cs, ts, zc = S[:, :, 0:CLUSTERS], S[:, :, CLUSTERS:CLUSTERS + TILES_FFN], S[:, :, CLUSTERS + TILES_FFN:]
            n8 = TILES * 8
            v8 = [area(n8).rearrange("p (t n) -> p t n", t=TILES) for _ in range(8)]
            gate, oc, ol, sel = v8[4], v8[5], v8[6], v8[7]
            col = area(TILES)
            w = dve.do(lambda e: e.tensor_tensor(zc, zc, ffn_rows[:, R_B1:R_B1 + COMP].unsqueeze(1).to_broadcast([P, TILES, COMP]), ALU.add), s)
            gl = act.do(lambda e: e.activation(zc, zc, ACT.Gelu), w)
            big = area(TILES * COMP)
            big3 = big.rearrange("p (t n) -> p t n", t=TILES)
            comp = area(2 * TILES).rearrange("p (i t) -> p i t", i=2)
            a = calibrate(gate, cs, v8[0:4], s)
            a = first_max(oc, gate, v8[0], col, a)
            big4 = big.rearrange("p (t c k) -> p t c k", t=TILES, c=CLUSTERS)
            a = dve.do(lambda e: e.tensor_tensor(big4, ts.rearrange("p t (c k) -> p t c k", c=CLUSTERS),
                                                 oc.unsqueeze(3).to_broadcast([P, TILES, CLUSTERS, TPC]), ALU.mult), a)
            a = dve.do(lambda e: e.tensor_reduce(sel, big.rearrange("p (t c k) -> p t k c", t=TILES, c=CLUSTERS), AX.X, ALU.add), a)
            a = calibrate(gate, sel, v8[0:4], a)
            a = first_max(ol, gate, v8[0], col, a)
            a = dve.do(lambda e: e.tensor_tensor(big4, oc.unsqueeze(3).to_broadcast([P, TILES, CLUSTERS, TPC]),
                                                 ol.unsqueeze(2).to_broadcast([P, TILES, CLUSTERS, TPC]), ALU.mult), a)
            onehot_ready = a
            prod = area(TILES * COMP).rearrange("p (t n) -> p t n", t=TILES)
            a = gl
            for i2 in range(2):
                w2 = ffn_rows[:, R_W2 + i2 * COMP:R_W2 + (i2 + 1) * COMP].unsqueeze(1).to_broadcast([P, TILES, COMP])
                a = dve.do(lambda e, w2=w2: e.tensor_tensor(prod, zc, w2, ALU.mult), a)
                a = dve.do(lambda e, i2=i2: e.tensor_reduce(comp[:, i2, :], prod, AX.X, ALU.add), a)
            for i2 in range(2):
                cd = act.do(lambda e, i2=i2: e.activation(comp[:, i2, :], comp[:, i2, :], ACT.Tanh, bias=ffn_rows[:, R_B2 + i2:R_B2 + i2 + 1]), a)
            par = area(TILES * TABLE).rearrange("p (t n) -> p t n", t=TILES)
            dirs = area(TILES * D).rearrange("p (t n) -> p t n", t=TILES)
            got = []
            for pair in range(TILES // TPS):
                i, bank, free = ring_a.take()
                for q in range(TPS):
                    done = pe.do(lambda e, q=q, pair=pair, bank=bank: e.transpose(bank[0:TILES_FFN, q * P:(q + 1) * P], big3[:, pair * TPS + q, :], ident),
                                 onehot_ready, *free, signal=q == TPS - 1)
                wi, oh, ofree = work.take()
                turned = act.do(lambda e, oh=oh, bank=bank: e.copy(oh[0:TILES_FFN, :], bank[0:TILES_FFN, :]), done, *ofree)
                ring_a.free(i, turned)
                for q in range(TPS):
                    t = pair * TPS + q
                    i, bank, free = ring_b.take()
                    done = pe.do(lambda e, q=q, oh=oh, bank=bank: e.matmul(bank[:, 0:TABLE + D], oh[0:TILES_FFN, q * P:(q + 1) * P], table[0:TILES_FFN, :],
                                                            start=True, stop=True), turned, *free)
                    c1 = act.do(lambda e, t=t, bank=bank: e.copy(par[:, t, :], bank[:, 0:TABLE]), done, *free_a)
                    c2 = act.do(lambda e, t=t, bank=bank: e.copy(dirs[:, t, :], bank[:, TABLE:TABLE + D]), done)
                    ring_b.free(i, c2)
                work.free(wi, done)
            hh = v8_pair = area(TILES * GRID).rearrange("p (t n) -> p t n", t=TILES)
            h2 = prod.rearrange("p t n -> p (t n)")[:, 0:TILES * GRID].rearrange("p (t n) -> p t n", t=TILES)

            def bc(i2):
                return comp[:, i2, :].unsqueeze(2).to_broadcast([P, TILES, GRID])
            a = dve.do(lambda e: e.tensor_tensor(hh, par[:, :, 0:GRID], bc(0), ALU.mult), c2, cd)
            a2 = dve.do(lambda e: e.tensor_tensor(h2, par[:, :, GRID:2 * GRID], bc(1), ALU.mult), a)
            a = dve.do(lambda e: e.tensor_tensor(hh, hh, h2, ALU.add), a2)
            a = dve.do(lambda e: e.tensor_tensor(hh, hh, par[:, :, 2 * GRID:3 * GRID], ALU.add), a)
            a = dve.do(lambda e: e.scalar_tensor_tensor(hh, hh, 0.0, par[:, :, 3 * GRID:4 * GRID], ALU.max, ALU.mult), a)
            a = dve.do(lambda e: e.tensor_reduce(col, hh, AX.X, ALU.add), a)
            a = dve.do(lambda e: e.tensor_tensor(col, col, par[:, :, 4 * GRID], ALU.add), a)
            a = dve.do(lambda e: e.tensor_scalar(col, col, ffn_rows[:, R_SCALE:R_SCALE + 1], None, ALU.mult), a)
            base = b * TILES
            ys = []
            for t in range(TILES):
                y = dve.do(lambda e, t=t: e.scalar_tensor_tensor(dirs[:, t, :], dirs[:, t, :], col[:, t:t + 1], H[b][:, t, :], ALU.mult, ALU.add), a)
                s1 = dve.do(lambda e, t=t: e.bn_stats(stats[b][:, t, :], dirs[:, t, :]), y)
                agg = dve.do(lambda e, t=t: e.bn_aggr(mv[b][:, t, :], stats[b][:, t, :]), s1)
            v = pool.do(lambda e: e.tensor_scalar(rstd[b][:, 0, :], mv[b][:, :, 1], LN_EPS, None, ALU.add), agg)
            v = pool.do(lambda e: e.tensor_tensor(rstd[b][:, 1, :], rstd[b][:, 0, :], const("halfneg"), ALU.pow), v)
            for t in range(TILES):
                n = dve.do(lambda e, t=t: e.tensor_scalar(dirs[:, t, :], dirs[:, t, :], mv[b][:, t, 0:1], rstd[b][:, 1, t:t + 1],
                                                          ALU.subtract, ALU.mult), v)
                gm = pool.do(lambda e, t=t: e.tensor_tensor(dirs[:, t, :], dirs[:, t, :], bias_row[:, 4, :], ALU.mult), n, row1_landed)
                bt = pool.do(lambda e, t=t: e.tensor_tensor(dirs[:, t, :], dirs[:, t, :], bias_row[:, 5, :], ALU.add), gm)
                x_ready[b][t] = pool.do(lambda e, t=t: e.tensor_tensor(X[:, base + t, :], X[:, base + t, :], dirs[:, t, :], ALU.add), bt)
            batch_free[b] = lasts()

        w_qkv = W2[:, 0:1536].rearrange("p (c n) -> p c n", c=DC)
        w_proj = W2[:, 1536:2048].rearrange("p (c n) -> p c n", c=DC)

        def attention_inputs(b):
            h_ready, ht_ready = normalise(b)
            biased = add_bias(b, bias_row[:, 1, :], row2_landed[0], h_ready[-1])
            ht, va = HT[b], vaug[b]
            ready = []
            for n in range(SPANS):
                for name, wcol, bcol in (("q", 0, 12), ("k", D, 14)):
                    for m in range(DC):
                        i, bank, free = ring_b.take()
                        for c in range(DC):
                            done = pe.do(lambda e, c=c, m=m, n=n, wcol=wcol, bank=bank: e.matmul(
                                bank, w_qkv[:, c, wcol + m * P:wcol + (m + 1) * P], ht[:, c, n * SPAN:(n + 1) * SPAN],
                                start=c == 0, stop=c == DC - 1), w2_landed[0], ht_ready[2 * n + 1], *free, signal=c == DC - 1)
                        j, f, ffree = work.take()
                        bias = bias_col[:, bcol + m:bcol + m + 1]
                        scale = 0.25 if name == "q" else 1.0
                        fd = dve.do(lambda e, f=f, bank=bank, bias=bias, scale=scale: e.tensor_scalar(
                            f[:, :], bank, bias, scale, ALU.add, ALU.mult), done, cols_landed, *ffree)
                        ring_b.free(i, fd)
                        lo, r1 = split(name, m, n, f[:, :], fd, *parts_free[0], *region_a_free)
                        work.free(j, r1)
                        ready.append(lo)
            for pair in range(TILES // 2):
                i, bank, free = ring_b.take()
                for q in range(2):
                    t = 2 * pair + q
                    for c in range(DC):
                        done = pe.do(lambda e, q=q, t=t, c=c, bank=bank: e.matmul(
                            bank[:, q * D:(q + 1) * D], ht[:, c, t * P:(t + 1) * P], w_qkv[:, c, 2 * D:3 * D],
                            start=(q == 0 and c == 0), stop=c == DC - 1, skip_group_check=True), *free, signal=(q == 1 and c == DC - 1))
                for q in range(2):
                    t = 2 * pair + q
                    vd = dve.do(lambda e, t=t, q=q, bank=bank: e.tensor_tensor(
                        va[:, t, :, 0:HD], bank[:, q * D:(q + 1) * D].rearrange("p (h e) -> p h e", h=HEADS),
                        bias_row[:, 0, :].rearrange("p (h e) -> p h e", h=HEADS), ALU.add), done, row2_landed[0], *v1_free)
                ring_b.free(i, vd)
            return ready, vd, biased

        v1_free = []
        mneg = [sb(f"mneg{i}", [STRIP, 2, P], BF16) for i in range(2)]
        mxt = [sb(f"mx{i}", [P, HPG, TILES, 2]) for i in range(2)]
        mcomb = sb("mcomb", [P, HPG * TILES])
        mneg_free = [[], []]

        def maxima(b, g, slot, stack, landed):
            mx = mxt[slot]
            for j in range(HPG):
                for t in range(TILES):
                    for half in range(t // TPS + 1):
                        n = min(t + 1 - half * TPS, TPS) * P
                        diagonal = half == t // TPS
                        i, bank, free = ring_a.take()
                        done = pe.do(lambda e, j=j, t=t, half=half, n=n, bank=bank: e.matmul(
                            bank[:, 0:n], stack["q"][0:KSTACK, j, t * P:(t + 1) * P],
                            stack["k"][0:KSTACK, j, half * SPAN:half * SPAN + n], start=True, stop=True, skip_group_check=True),
                            landed, *free, signal=not diagonal)
                        if diagonal:
                            done = pe.do(lambda e, n=n, bank=bank: e.matmul(bank[:, n - P:n], ident_bf[:, :], mask_qk_bf[:, :],
                                                                 start=False, stop=True, skip_group_check=True), masks_ready)
                        red = dve.do(lambda e, j=j, t=t, half=half, n=n, bank=bank: e.tensor_reduce(mx[:, j, t, half:half + 1], bank[:, 0:n], AX.X, ALU.max),
                                     done, *mneg_free[slot])
                        ring_a.free(i, red)
                        yield
            m3 = mcomb[:, :].rearrange("p (j t) -> p j t", j=HPG)
            a = dve.do(lambda e: e.tensor_copy(m3[:, :, 0:TPS], mx[:, :, 0:TPS, 0]), red, mcomb_free[0])
            a = dve.do(lambda e: e.tensor_tensor(m3[:, :, TPS:], mx[:, :, TPS:, 0], mx[:, :, TPS:, 1], ALU.max), a)
            i, bank, free = ring_a.take()
            done = pe.do(lambda e: e.transpose(bank[0:STRIP, 0:P], mcomb[:, :], ident), a, *free)
            mcomb_free[0] = done
            ng = mneg[slot]
            a = dve.do(lambda e: e.tensor_scalar(ng[:, 0, :], bank[0:STRIP, 0:P], -1.0, None, ALU.mult), done, *mneg_free[slot])
            a = dve.do(lambda e: e.scalar_tensor_tensor(ng[:, 1, :], bank[0:STRIP, 0:P], -1.0, ng[:, 0, :], ALU.mult, ALU.subtract), a)
            ring_a.free(i, a)
            for s in range(2):
                dst = stack["q"][KSTACK + s:KSTACK + s + 1, :, :].rearrange("p j (t n) -> p (j t) n", n=P)
                m_landed = sp.dma(dst, ng[:, s, :], max_landing[slot], a)
            mneg_free[slot] = [m_landed]
            result[(b, g)] = m_landed
            yield

        mcomb_free = [None]
        result = {}

        def weighted(b, g, stack, landed, m_landed, v_ready):
            for c in range(SPANS):
                bank_i, obank, ofree = ring_c.take()
                held = None

                def values(kb, off, ps, last):
                    for j in range(HPG):
                        w, p, ex = ps[j]
                        done = pe.do(lambda e, j=j, p=p: e.matmul(
                            obank[j * STRIP:(j + 1) * STRIP, off:SPAN], vaug[b][:, kb, g * HPG + j, :], p[:, 0:SPAN - off],
                            start=kb == 0, stop=last, skip_group_check=True), ex, v_ready, first_fill["v1"], *ofree, signal=j == HPG - 1)
                    for j in range(HPG):
                        work.free(ps[j][0], done)
                    return done

                blocks = (c + 1) * TPS
                for kb in range(blocks):
                    off = max(0, kb * P - c * SPAN)
                    ps = []
                    for j in range(HPG):
                        i, bank, free = ring_b.take()
                        n = SPAN - off
                        diagonal = kb * P >= c * SPAN
                        done = pe.do(lambda e, j=j, kb=kb, off=off, n=n, bank=bank: e.matmul(
                            bank[:, 0:n], stack["k"][0:KSTACK + 2, j, kb * P:(kb + 1) * P],
                            stack["q"][0:KSTACK + 2, j, c * SPAN + off:(c + 1) * SPAN], start=True, stop=True, skip_group_check=True),
                            landed, m_landed, first_fill["ones"], *free, signal=not diagonal)
                        if diagonal:
                            done = pe.do(lambda e, bank=bank: e.matmul(bank[:, 0:P], ident_bf[:, :], mask_kq_bf[:, :], start=False, stop=True,
                                                            skip_group_check=True))
                        w, p, wfree = work.take()
                        ex = act.do(lambda e, p=p, n=n, bank=bank: e.activation(p[:, 0:n], bank[:, 0:n], ACT.Exp), done, *wfree)
                        ring_b.free(i, ex)
                        ps.append((w, p, ex))
                    if held:
                        values(*held, False)
                    held = (kb, off, ps)
                    yield
                done = values(*held, True)
                heads_done[(b, g)] = head_outputs(b, g, c, bank_i, obank, done, 0.0)

        heads_done = {}

        def softmax_attention():
            nonlocal region_a_free, v1_free
            v1_free = list(region_b_free)
            for b in range(BATCH):
                first_fill["v1"] = ones_column(vaug[b], *region_b_free, pool.last())
            for s in range(2):
                first_fill["ones"] = dve.do(lambda e, s=s: e.memset(stacks.buffers[s]["k"][KSTACK:KSTACK + 2, :, :], 1.0),
                                             *region_a_free, pool.last())
            seq = [(b, g) for b in range(BATCH) for g in range(GROUPS)]
            inputs = {0: attention_inputs(0)}
            last_b = None
            for n in range(len(seq) + 1):
                steps_a, steps_b = None, None
                if n < len(seq):
                    b, g = seq[n]
                    if b not in inputs:
                        parts_free[0] = [landed]
                        inputs[b] = attention_inputs(b)
                    s, stack, landed = load_stacks(g, inputs[b][0])
                    steps_a = maxima(b, g, s, stack, landed)
                if n:
                    pb, pg, ps, pstack, planded = last_b
                    steps_b = weighted(pb, pg, pstack, planded, result[(pb, pg)], inputs[pb][1])
                while steps_a or steps_b:
                    if steps_b and next(steps_b, "end") == "end":
                        steps_b = None
                    for _ in range(4):
                        if steps_a and next(steps_a, "end") == "end":
                            steps_a = None
                if n:
                    stacks.free(ps, pe.last())
                    if pg == GROUPS - 1:
                        finish_attention(pb, heads_done[(pb, pg)], w_proj, w2_landed[0], inputs[pb][2])
                if n < len(seq):
                    last_b = (b, g, s, stack, landed)
            parts_free[0] = [landed]
            region_a_free = lasts() + [landed, result[seq[-1]]]

        w_x = W1[:, :].rearrange("p (c n) -> p c n", c=DC)
        rowany = sb("rowany", [P, TILES])

        def mask_weights():
            a = None
            for half in range(2):
                w, buf, free = work.take()
                v = buf[:, 0:TPS * CTX].rearrange("p (t k) -> p t k", t=TPS)
                sl = slice(half * TPS, (half + 1) * TPS)
                a = dve.do(lambda e, v=v, sl=sl: e.tensor_scalar(v, mask_i[:, sl, :], 0.0, None, ALU.not_equal), mask_landed, *free)
                r = dve.do(lambda e, v=v, sl=sl: e.tensor_reduce(rowany[:, sl], v, AX.X, ALU.max), a)
                a = dve.do(lambda e, v=v, sl=sl: e.tensor_scalar(maskneg[:, sl, :], v, 1.0, 1e9, ALU.subtract, ALU.mult), r)
                work.free(w, a)
            return a

        def masked_attention(b):
            nonlocal region_a_free, ox_free
            h_ready, ht_ready = normalise(b)
            biased = add_bias(b, bias_row[:, 3, :], row2_landed[0], h_ready[-1])
            free_a = list(region_a_free)
            q_ready, kv_ready = [], []
            for m in range(DC):
                for n in range(SPANS):
                    i, bank, free = ring_b.take()
                    for c in range(DC):
                        done = pe.do(lambda e, c=c, m=m, n=n, bank=bank: e.matmul(
                            bank, w_x[:, c, m * P:(m + 1) * P], HT[b][:, c, n * SPAN:(n + 1) * SPAN],
                            start=c == 0, stop=c == DC - 1), wx_landed[0], ht_ready[2 * n + 1], *free, signal=c == DC - 1)
                    q = dve.do(lambda e, m=m, n=n, bank=bank: e.tensor_scalar(qx[:, m, n * SPAN:(n + 1) * SPAN], bank, bias_col[:, 8 + m:9 + m],
                                                                   0.25, ALU.add, ALU.mult), done, cols_landed, *free_a)
                    ring_b.free(i, q)
                    q_ready.append(q)
            z = pool.do(lambda e: e.memset(vx[:, :, :], 0.0), *free_a)
            for m in range(DC):
                i, bank, free = ring_b.take()
                for c in range(DC):
                    done = pe.do(lambda e, c=c, m=m, bank=bank: e.matmul(bank[:, 0:CTX], w_x[:, c, D + m * P:D + (m + 1) * P], ctx_t[:, b, c, :],
                                                              start=c == 0, stop=c == DC - 1), *free, signal=c == DC - 1)
                for h8 in range(HALF_HEADS):
                    k = dve.do(lambda e, m=m, h8=h8, bank=bank: e.tensor_scalar(
                        kbd[:, 2 * m + h8 // HPG, h8 % HPG, :], bank[:, 0:CTX], bias_col[:, 10 + m:11 + m],
                        const("headmask")[:, h8:h8 + 1], ALU.add, ALU.mult), done, *free_a)
                ring_b.free(i, k)
                kv_ready.append(k)
            i, bank, free = ring_b.take()
            for c in range(DC):
                done = pe.do(lambda e, c=c, bank=bank: e.matmul(bank[0:CTX, 0:D], ctx_t[:, b, c, :], w_x[:, c, 2 * D:3 * D],
                                                     start=c == 0, stop=c == DC - 1), *free, signal=c == DC - 1)
            for odd in range(2):
                src = bank[0:CTX, 0:D].rearrange("p (h o e) -> p h o e", o=2, e=HD)[:, :, odd, :]
                brow = bias_row[0:CTX, 2, :].rearrange("p (h o e) -> p h o e", o=2, e=HD)[:, :, odd, :]
                dst = vx[0:CTX, :, :].rearrange("p (h o) e -> p h o e", o=2)[:, :, odd, odd * HD:(odd + 1) * HD]
                k = dve.do(lambda e, dst=dst, src=src, brow=brow: e.tensor_tensor(dst, src, brow, ALU.add), done, z, row2_landed[0])
            ring_b.free(i, k)
            kv_ready.append(k)
            for _ in context_attention(b, DC, q_ready, kv_ready, 2, True):
                pass
            project_out(b, [ox[:, c, :] for c in range(DC)], w_x[:, :, 3 * D:4 * D], lambda t: [ox_ready[t // TPS]], [biased])
            region_a_free = lasts()
            ox_free = lasts()

        NE = EXPERTS + 1
        wg = carve(region_b, 0, DC * NE * INNER).rearrange("p (c e i) -> p c e i", c=DC, e=NE)
        wu = carve(region_b, DC * NE * INNER, DC * NE * INNER).rearrange("p (c e i) -> p c e i", c=DC, e=NE)
        wd = carve(region_b, 2 * DC * NE * INNER, NE * D).rearrange("p (e n) -> p e n", e=NE)
        gw = W2[:, 0:DC * EXPERTS].rearrange("p (c e) -> p c e", c=DC)

        def load_experts(waits):
            for c in range(DC):
                rs = slice(c * P, (c + 1) * P)
                for w, name, shared in ((wg, "L1_ffn_Wg", "L1_ffn_sg"), (wu, "L1_ffn_Wu", "L1_ffn_su")):
                    load("moe", w[:, c, 0:EXPERTS, :], A[name][:, rs, :].rearrange("e p i -> p e i"), *waits)
                    load("moe", w[:, c, EXPERTS, :], A[shared][rs, :])
            load("moe", wd[:, 0:EXPERTS, :], A["L1_ffn_Wd"].rearrange("e p n -> p e n"))
            return load("moe", wd[:, EXPERTS, :], A["L1_ffn_sd"])

        def moe(b):
            landed, gw_landed = moe_landed
            h_ready, ht_ready = normalise(b)
            base = 0
            free_a = list(region_a_free)
            combt = carve(region_a, b * 512, 512, BF16)
            sel = carve(region_a, 1024, 1024, BF16).rearrange("p (e n) -> p e n", e=EXPERTS)
            at = 2048 + b * 5400
            sc = carve(region_a, at, P).rearrange("p (t e) -> p t e", t=TILES)
            rank = carve(region_a, at + P, P).rearrange("p (t e) -> p t e", t=TILES)
            col = carve(region_a, at + 2 * P, TILES)
            comb3 = carve(region_a, at + 272, TILES * PARTS * EXPERTS).rearrange("p (t s e) -> p t s e", t=TILES, s=PARTS)
            cbf = carve(region_a, at + 272 + 384, P // 2, BF16).rearrange("p (t e) -> p t e", t=TILES)
            g1 = carve(region_a, at + 800, 2048).rearrange("p (t i j) -> p t i j", t=TILES, i=EXPERTS)
            g2 = carve(region_a, at + 800 + 2048, 2048).rearrange("p (t i j) -> p t i j", t=TILES, i=EXPERTS)
            if b == 0:
                first_fill["sel"] = dve.do(lambda e: e.tensor_copy(sel[0:PARTS * EXPERTS], const("parts")[0:PARTS * EXPERTS, :].unsqueeze(2)
                                                                   .to_broadcast([PARTS * EXPERTS, EXPERTS, P])), *free_a)
            i, bank, free = ring_b.take()
            for t in range(TILES):
                for c in range(DC):
                    done = pe.do(lambda e, c=c, t=t, bank=bank: e.matmul(bank[:, t * EXPERTS:(t + 1) * EXPERTS], HT[b][:, c, t * P:(t + 1) * P],
                                                              gw[:, c, :], start=(t == 0 and c == 0), stop=c == 1, skip_group_check=True),
                                 gw_landed, ht_ready[t // 2], *free, signal=(t == TILES - 1 and c == 1))
            a = act.do(lambda e, bank=bank: e.activation(sc.rearrange("p t e -> p (t e)"), bank[:, 0:P], ACT.Exp, scale=-1.0), done, *free_a)
            ring_b.free(i, a)
            a = dve.do(lambda e: e.tensor_scalar(sc, sc, 1.0, None, ALU.add), a)
            a = dve.do(lambda e: e.reciprocal(sc, sc), a)
            me = sc.unsqueeze(3).to_broadcast([P, TILES, EXPERTS, EXPERTS])
            other = sc.unsqueeze(2).to_broadcast([P, TILES, EXPERTS, EXPERTS])
            a = dve.do(lambda e: e.tensor_tensor(g1, other, me, ALU.is_gt), a)
            a2 = dve.do(lambda e: e.tensor_tensor(g2, other, me, ALU.is_equal), a)
            before = const("before").rearrange("p (i j) -> p i j", i=EXPERTS).unsqueeze(1).to_broadcast([P, TILES, EXPERTS, EXPERTS])
            a2 = dve.do(lambda e: e.tensor_tensor(g2, g2, before, ALU.mult), a2)
            a = dve.do(lambda e: e.tensor_tensor(g1, g1, g2, ALU.add), a2)
            a = dve.do(lambda e: e.tensor_reduce(rank, g1, AX.X, ALU.add), a)
            a = dve.do(lambda e: e.scalar_tensor_tensor(sc, rank, float(TOPK) - 0.5, sc, ALU.is_lt, ALU.mult), a)
            a = dve.do(lambda e: e.tensor_reduce(col, sc, AX.X, ALU.add), a)
            a = dve.do(lambda e: e.reciprocal(col, col), a)
            a = dve.do(lambda e: e.tensor_tensor(sc, sc, col.unsqueeze(2).to_broadcast([P, TILES, EXPERTS]), ALU.mult), a)
            for s in range(PARTS):
                a = dve.do(lambda e: e.tensor_copy(cbf, sc), a)
                a = dve.do(lambda e, s=s: e.tensor_copy(comb3[:, :, s, :], cbf), a)
                if s < PARTS - 1:
                    a = dve.do(lambda e: e.tensor_tensor(sc, sc, cbf, ALU.subtract), a)
            comb_ready = []
            for n in range(SPANS):
                i, bank, free = ring_b.take()
                for q in range(TPS):
                    done = pe.do(lambda e, q=q, n=n, bank=bank: e.transpose(
                        bank[0:PARTS * EXPERTS, q * P:(q + 1) * P], comb3[:, n * TPS + q, :, :].rearrange("p s e -> p (s e)"), ident),
                        a, *free, signal=q == TPS - 1)
                cd = act.do(lambda e, n=n, bank=bank: e.copy(combt[0:PARTS * EXPERTS, n * SPAN:(n + 1) * SPAN], bank[0:PARTS * EXPERTS, :]), done, *free_a)
                ring_b.free(i, cd)
                comb_ready.append(cd)
            ht = HT[b]
            for n in range(SPANS):
                cols = slice(n * SPAN, (n + 1) * SPAN)
                outs = [ring_c.take() for _ in range(2)]
                held = {}

                def up(x):
                    banks = []
                    for w in (wg, wu):
                        i, bank, free = ring_a.take() if w is wg else ring_b.take()
                        for c in range(DC):
                            done = pe.do(lambda e, c=c, w=w, bank=bank: e.matmul(bank, w[:, c, x, :], ht[:, c, cols], start=c == 0, stop=c == 1),
                                         landed, ht_ready[2 * n + 1], *free, signal=c == 1)
                        banks.append((i, bank, done))
                    (gi, gbank, gdone), (ui, ubank, udone) = banks
                    k, s, sfree = work.take()
                    a = act.do(lambda e: e.activation(s[:, :], gbank, ACT.Silu), gdone, *sfree)
                    ring_a.free(gi, a)
                    a = dve.do(lambda e: e.tensor_tensor(s[:, :], s[:, :], ubank, ALU.mult), a, udone)
                    ring_b.free(ui, a)
                    if x < EXPERTS:
                        i, bank, free = ring_b.take()
                        done = pe.do(lambda e: e.matmul(bank, sel[0:PARTS * EXPERTS, x, :], combt[0:PARTS * EXPERTS, cols], start=True, stop=True),
                                     first_fill["sel"], comb_ready[n], *free)
                        a = dve.do(lambda e: e.tensor_tensor(s[:, :], s[:, :], bank, ALU.mult), a, done)
                        ring_b.free(i, a)
                    held[x] = (k, s, a)

                def down(x):
                    k, s, ready = held.pop(x)
                    for q in range(TPS):
                        oi, obank, ofree = outs[q // 2]
                        o = q % 2
                        done = pe.do(lambda e, q=q, o=o, obank=obank: e.matmul(
                            obank[:, o * D:(o + 1) * D], s[:, q * P:(q + 1) * P], wd[:, x, :],
                            start=(x == 0 and o == 0), stop=x == NE - 1, skip_group_check=True), ready, *ofree, signal=q == TPS - 1)
                    work.free(k, done)
                    return done

                for x in range(NE + 2):
                    if x < NE:
                        up(x)
                    if x >= 2:
                        done = down(x - 2)
                for o in range(2):
                    oi, obank, _ = outs[o]
                    t0 = b * TILES + n * TPS + 2 * o
                    added = dve.do(lambda e, t0=t0, obank=obank: e.tensor_tensor(X[:, t0:t0 + 2, :], X[:, t0:t0 + 2, :],
                                                                    obank.rearrange("p (t d) -> p t d", t=2), ALU.add), done)
                    ring_c.free(oi, added)
                    x_ready[b][n * TPS + 2 * o] = x_ready[b][n * TPS + 2 * o + 1] = added

        weights_done = [ffn_weights()]
        mask_ready = mask_weights()
        region_a_free = [mask_ready]
        row2_landed, w2_landed, wx_landed = [None], [None], [None]
        if "a" in phases:
            for b in range(BATCH):
                linear_attention(b)
        if "b" in phases:
            for b in range(BATCH):
                feature_attention(b)
        free_rows = lasts()
        if "b" not in phases:
            free_rows += [wa_landed, row1_landed, row0_landed, w0_landed, fm_landed, ctx_landed, cols_landed, x_landed[0], x_landed[1]]
        for i, v in enumerate((A["L1_attn_b_attn"][2 * D:3 * D], A["L1_attn_b_proj"], A["L1_xattn_bv"], A["L1_xattn_bo"])):
            row2_landed[0] = load("row2", bias_row[:, i, :], spread(v, D), *free_rows)
        wx_landed[0] = load("wx", w_x, A["L1_xattn_w"].rearrange("(c p) n -> p c n", p=P), *free_rows)
        if "c" in phases:
            for b in range(BATCH):
                spline_ffn(b)
        region_a_free = lasts()
        if "c" not in phases:
            sp.wait(wa_landed)
        if "d" in phases:
            load("w2", w_qkv, A["L1_attn_w_attn"].rearrange("(c p) n -> p c n", p=P), *lasts())
            w2_landed[0] = load("w2", w_proj, A["L1_attn_w_proj"].rearrange("(c p) n -> p c n", p=P))
            softmax_attention()
        if "f" in phases:
            moe_landed = (load_experts(lasts()), load("gw", gw, A["gate_w_t"].rearrange("(c p) e -> p c e", p=P), *lasts()))
        if "e" in phases:
            for b in range(BATCH):
                masked_attention(b)
        if "f" in phases:
            for b in range(BATCH):
                moe(b)
        out_tiles = out.rearrange("b (t p) d -> p (b t) d", p=P)
        stored = landing("stored")
        for b in range(BATCH):
            for n in range(SPANS):
                t0 = b * TILES + n * TPS
                end = sp.dma(out_tiles[:, t0:t0 + TPS, :], X[:, t0:t0 + TPS, :], stored, *x_ready[b][n * TPS:(n + 1) * TPS])
        sp.wait(end, *lasts())
        for l in loads.values():
            sp.wait(l.last())


def lay_out(I):
    f = {k: np.ascontiguousarray(v) for k, v in I.items()}
    a = {"x": f["x"], "consts": constants()}
    a["ctx_t"] = np.ascontiguousarray(f["ctx_1024"].transpose(0, 2, 1))
    a["mask"] = f["mask_1x1xSxS2_ik0"].reshape(SEQ, CTX)
    a["L0_attn_w"] = np.concatenate([f[f"L0_attn_W{n}"].T for n in "qkvo"], axis=1)
    for n in ("L0_attn_bq", "L0_attn_bk", "L0_attn_bv", "L0_attn_bo", "L0_xattn_fc_b", "L0_ffn_knot_values", "L0_ffn_temperature",
              "L0_ffn_compress_w1", "L0_ffn_compress_b1", "L0_ffn_compress_b2", "L0_ffn_norm_gamma", "L0_ffn_norm_beta",
              "L0_ffn_output_scale", "L1_attn_w_attn", "L1_attn_b_attn", "L1_attn_w_proj", "L1_attn_b_proj", "L1_xattn_bq",
              "L1_xattn_bk", "L1_xattn_bv", "L1_xattn_bo", "L1_ffn_Wg", "L1_ffn_Wu", "L1_ffn_Wd", "L1_ffn_sg", "L1_ffn_su", "L1_ffn_sd"):
        a[n] = f[n]
    bd = np.zeros((2, P, P), np.float32)
    for v in range(2):
        for j in range(HPG):
            r = (v * HPG + j) * HD
            bd[v, r:r + HD, j * STRIP:j * STRIP + HD] = f["L0_xattn_fm_w"].T
            bd[v, r:r + HD, j * STRIP + HD:(j + 1) * STRIP] = f["L0_xattn_fm_w"].T
    a["fm_bd"] = bd
    cols = [f["L0_attn_bq"], f["L0_attn_bk"], np.tile(f["L0_xattn_fm_b"], P // HD), np.zeros(3 * P, np.float32),
            f["L1_xattn_bq"], f["L1_xattn_bk"], f["L1_attn_b_attn"][:2 * D]]
    a["bias_cols"] = np.ascontiguousarray(np.concatenate(cols).reshape(16, P).T)
    a["fm_b_row"] = np.tile(f["L0_xattn_fm_b"], P // HD).reshape(1, P)
    a["sign_row"] = np.where(np.arange(P) % STRIP < HD, 1.0, -1.0).astype(np.float32).reshape(1, P)
    a["fc_w_t"] = np.ascontiguousarray(f["L0_xattn_fc_w"].T)
    a["sig_t"] = np.ascontiguousarray(f["L0_ffn_signatures_raw"].T)
    a["spline_table"] = np.concatenate([f["L0_ffn_spline_w1"].reshape(TILES_FFN, 2 * GRID), f["L0_ffn_spline_b1"],
                                        f["L0_ffn_spline_w2"].reshape(TILES_FFN, GRID), f["L0_ffn_spline_b2"],
                                        f["L0_ffn_directions"]], axis=1)
    a["compress_w2_t"] = np.ascontiguousarray(f["L0_ffn_compress_w2"].T)
    a["L1_xattn_w"] = np.concatenate([f[f"L1_xattn_w{n}"].T for n in "qkvo"], axis=1)
    a["gate_w_t"] = np.ascontiguousarray(f["L1_ffn_gate_w"].T)
    return a


def kernel(**inputs):
    import concourse.bacc as bacc
    from concourse.bass_utils import run_bass_kernel_spmd

    arrays = lay_out({k: np.asarray(v) for k, v in inputs.items()})
    nc = bacc.Bacc("TRN2", target_bir_lowering=False, num_devices=1)
    args = {k: nc.dram_tensor(f"in_{k}", v.shape, mybir.dt.from_np(v.dtype), kind="ExternalInput").ap() for k, v in arrays.items()}
    out = nc.dram_tensor("out", (BATCH, SEQ, D), F32, kind="ExternalOutput").ap()
    build(nc, args, out)
    r = run_bass_kernel_spmd(nc, [{f"in_{k}": v for k, v in arrays.items()}], core_ids=[0])
    return r.results[0]["out"]
```

```python
from contextlib import ExitStack

import numpy as np

import concourse.bass as bass
from concourse import mybir

BATCH, SEQ, D = 2, 1024, 256
CTX = 77
HEADS, HD = 16, 16
P = 128
TILES = SEQ // P
DC = D // P
GROUPS = 4
HPG = HEADS // GROUPS
STRIP = 32
LEAD = 6
HALF_HEADS = P // HD
SPAN = 512
SPANS = SEQ // SPAN
TPS = SPAN // P
PARTS = 3
KSTACK = 6 * HD
EXPERTS, TOPK, INNER = 16, 4, 128
TILES_FFN, CLUSTERS, TPC = 64, 8, 8
GRID, COMP, KNOTS = 16, 64, 8
GATE_COLS = CLUSTERS + TILES_FFN + COMP
TABLE = 2 * GRID + GRID + GRID + 1
LN_EPS = 1e-5
DEN_EPS = 1e-6
MASKED = -1e30

F32, BF16, I32 = mybir.dt.float32, mybir.dt.bfloat16, mybir.dt.int32
ALU = mybir.AluOpType
ACT = mybir.ActivationFunctionType
AX = mybir.AxisListType

Q_PARTS = (0, 1, 2, 0, 1, 0)
K_PARTS = (0, 0, 0, 1, 1, 2)

CONSTS = {}
_at = 0
for _name, _width in (("ident", P), ("causal01", P), ("headmask", HALF_HEADS), ("sign", 1), ("iota8", 8), ("parts", EXPERTS),
                      ("before", EXPERTS * EXPERTS), ("halfneg", TILES), ("mask_qk", P), ("mask_kq", P)):
    CONSTS[_name] = (_at, _width)
    _at += _width
CONST_COLS = _at
KEPT_COLS = CONSTS["mask_qk"][0]


def constants():
    c = np.zeros((P, CONST_COLS), np.float32)

    def put(name, value):
        at, width = CONSTS[name]
        c[:, at:at + width] = value

    r, k = np.arange(P)[:, None], np.arange(P)[None, :]
    put("ident", r == k)
    put("causal01", r <= k)
    put("mask_qk", np.where(k <= r, 0.0, MASKED))
    put("mask_kq", np.where(r <= k, 0.0, MASKED))
    put("headmask", r // HD == np.arange(HALF_HEADS)[None, :])
    put("sign", np.where(r % STRIP < HD, 1.0, -1.0))
    put("iota8", np.arange(8)[None, :])
    put("parts", (r % EXPERTS == np.arange(EXPERTS)[None, :]) & (r < PARTS * EXPERTS))
    i, j = np.arange(EXPERTS)[:, None], np.arange(EXPERTS)[None, :]
    put("before", (j < i).reshape(1, -1))
    put("halfneg", -0.5)
    return c


class Engine:

    def __init__(self, engine, sem):
        self.engine, self.sem, self.count, self.waited = engine, sem, 0, {}

    def wait(self, *tokens):
        for token in tokens:
            if token is None:
                continue
            sem, value = token
            if self.waited.get(id(sem), 0) < value:
                self.waited[id(sem)] = value
                self.engine.wait_ge(sem, value)

    def do(self, emit, *waits, signal=True):
        self.wait(*waits)
        instruction = emit(self.engine)
        if not signal:
            return None
        self.count += 1
        instruction.then_inc(self.sem, 1)
        return self.last()

    def dma(self, out, in_, landing, *waits):
        self.wait(*waits)
        landing.count += 16
        self.engine.dma_start(out, in_).then_inc(landing.sem, 16)
        return landing.last()

    def last(self):
        return (self.sem, self.count)


class Slots:

    def __init__(self, buffers):
        self.buffers, self.readers = buffers, [()] * len(buffers)
        self.idle = list(range(len(buffers)))

    def take(self):
        i = self.idle.pop(0)
        return i, self.buffers[i], self.readers[i]

    def free(self, i, *readers):
        self.readers[i] = readers
        self.idle.append(i)

    def add(self, buffer, *readers):
        self.buffers.append(buffer)
        self.readers.append(readers)
        self.idle.append(len(self.buffers) - 1)

    def hold_back(self, *tokens):
        self.readers = [tuple(r) + tokens for r in self.readers]


def build(nc, A, out):
    with ExitStack() as ctx:
        def sb(name, shape, dt=F32):
            return ctx.enter_context(nc.sbuf_tensor(name, shape, dt))

        sems = {}

        def sem(name):
            sems[name] = ctx.enter_context(nc.semaphore(name))
            return sems[name]

        pe = Engine(nc.tensor, sem("pe_done"))
        act = Engine(nc.scalar, sem("act_done"))
        dve = Engine(nc.vector, sem("dve_done"))
        pool = Engine(nc.gpsimd, sem("pool_done"))
        sp = Engine(nc.sync, sem("sp_done"))

        def landing(name):
            return Engine(None, sem(name))

        psum = ctx.enter_context(nc.psum_tensor("psum", [P, 8, SPAN], F32))
        ring_a = Slots([psum[:, i, :] for i in (0, 1, 2)])
        ring_b = Slots([psum[:, i, :] for i in (3, 4, 5)])
        ring_c = Slots([psum[:, i, :] for i in (6, 7)])

        X = sb("X", [P, BATCH * TILES, D])
        H = [sb(f"H{b}", [P, TILES, D]) for b in range(BATCH)]
        HT = [sb(f"HT{b}", [P, DC, SEQ]) for b in range(BATCH)]
        stack_area = sb("stack_area", [P, 8192])
        area = [sb(f"area{b}", [P, 9728]) for b in range(BATCH)]
        work = Slots([sb(f"work{i}", [P, SPAN]) for i in range(8)])
        W1 = sb("W1", [P, 2048])
        W2 = sb("W2", [P, 2048])
        consts = sb("const_tile", [P, KEPT_COLS])
        ident_bf = sb("ident_bf", [P, P], BF16)
        mask_qk_bf = sb("mask_qk_bf", [P, P], BF16)
        mask_kq_bf = sb("mask_kq_bf", [P, P], BF16)
        bias_row = sb("bias_row", [P, 6, D])
        bias_col = sb("bias_col", [P, 17])
        stats = [sb(f"stats{b}", [P, TILES, 6]) for b in range(BATCH)]
        mv = [sb(f"mv{b}", [P, TILES, 2]) for b in range(BATCH)]
        rstd = [sb(f"rstd{b}", [P, 2, TILES]) for b in range(BATCH)]
        small = sb("small", [P, 456])

        masks_once = stack_area[:, 0:CONST_COLS - KEPT_COLS]

        def const(name):
            at, width = CONSTS[name]
            if at >= KEPT_COLS:
                return masks_once[:, at - KEPT_COLS:at - KEPT_COLS + width]
            return consts[:, at:at + width]

        ident = const("ident")

        def carve(region, at, n, dt=F32):
            view = region[:, at:at + n]
            return view if dt is F32 else view.bitcast(dt)

        parts_dram = {(phase, b, name): nc.dram_tensor(f"parts_{phase}{b}{name}", (DC, PARTS, P, SEQ), BF16, kind="Internal").ap()
                      for phase in "ad" for b in range(BATCH) for name in "qk"}
        stack_words = HPG * SEQ // 2

        def stack_slot(*places):
            return {n: carve(region, at, stack_words, BF16).rearrange("p (j t) -> p j t", j=HPG) for n, (region, at) in zip("qk", places)}

        stack_slots = [stack_slot((stack_area, 0), (stack_area, 2048)), stack_slot((stack_area, 4096), (stack_area, 6144)),
                       stack_slot((area[0], 6880), (area[1], 5344))]
        stacks = Slots(stack_slots[0:2])
        stack_landing = [landing(f"stack_landed{s}") for s in range(3)]
        max_landing = [landing(f"max_landed{s}") for s in range(2)]
        work_stored = [landing(f"work{i}_stored") for i in range(len(work.buffers))]
        parts_stored = {(*key, m): [] for key in parts_dram for m in range(DC)}

        vaug = [carve(area[b], 0, 4096).rearrange("p (t h e) -> p t h e", t=TILES, h=HEADS) for b in range(BATCH)]
        qfeats = [carve(area[b], 4096, 2048).rearrange("p (m t) -> p m t", m=DC) for b in range(BATCH)]
        states = [carve(area[b], 6144, 7 * SPAN).rearrange("p (c n) -> p c n", c=7) for b in range(BATCH)]

        loads = {}

        def load(group, dst, src, *waits):
            if group not in loads:
                loads[group] = landing(f"landed_{group}")
            return sp.dma(dst, src, loads[group], *waits)

        def spread(vector, n, partitions=P):
            return vector.rearrange("(a n) -> a n", a=1).to_broadcast([partitions, n])

        def rows(name, n):
            return spread(A[name], n)

        x_tiles = A["x"].rearrange("b (t p) d -> p (b t) d", p=P)
        def load_x(b):
            return [load(f"x{b}{n}", X[:, t:t + TPS, :], x_tiles[:, t:t + TPS, :]) for n, t in enumerate(range(b * TILES, (b + 1) * TILES, TPS))]

        x_landed = [load_x(0)]
        load("consts", consts[:, :], A["consts"][:, 0:KEPT_COLS])
        consts_landed = load("consts", masks_once, A["consts"][:, KEPT_COLS:])
        w_attn0 = W1[:, :].rearrange("p (c n) -> p c n", c=DC)
        w0_landed = load("w0", w_attn0, A["L0_attn_w"].rearrange("(c p) n -> p c n", p=P))
        for i, n in enumerate(("L0_attn_bk", "L0_attn_bv", "L0_attn_bo")):
            row0_landed = load("row0", bias_row[:, i, :], rows(n, D))
        cols_landed = load("cols", bias_col[:, 0:16], A["bias_cols"])
        x_landed.append(load_x(1))
        w_fc = W2[:, 0:1024].rearrange("p (g n) -> p g n", g=GROUPS)
        wa_landed = load("wa", w_fc, A["fc_w_t"].rearrange("(g p) n -> p g n", p=P))

        casts = [act.do(lambda e, o=o, n=n: e.copy(o[:, :], const(n)), consts_landed)
                 for o, n in ((ident_bf, "ident"), (mask_qk_bf, "mask_qk"), (mask_kq_bf, "mask_kq"))]
        masks_ready = casts[-1]

        x_ready = [[x_landed[b][t // TPS] for t in range(TILES)] for b in range(BATCH)]
        batch_free = [[] for _ in range(BATCH)]
        area_free = [[], []]
        mask_ready = None

        def lasts():
            return [pe.last(), act.last(), dve.last(), pool.last()]

        def pause(steps):
            for _ in range(steps):
                yield

        def normalise(b):
            h, ht, base = H[b], HT[b], b * TILES
            ready, ht_ready, scales = [], [], []
            for half in range(2):
                for t in range(half * 4, half * 4 + 4):
                    s = dve.do(lambda e, t=t: e.bn_stats(stats[b][:, t, :], X[:, base + t, :]), x_ready[b][t], *batch_free[b])
                    done = dve.do(lambda e, t=t: e.bn_aggr(mv[b][:, t, :], stats[b][:, t, :]), s)
                sl = slice(half * 4, half * 4 + 4)
                v = pool.do(lambda e, sl=sl: e.tensor_scalar(rstd[b][:, 0, sl], mv[b][:, sl, 1], LN_EPS, None, ALU.add), done,
                            consts_landed)
                scales.append(pool.do(lambda e, sl=sl: e.tensor_tensor(rstd[b][:, 1, sl], rstd[b][:, 0, sl],
                                                                       const("halfneg")[:, 0:4], ALU.pow), v))
                yield
            for half in range(2):
                for t in range(half * 4, half * 4 + 4):
                    ready.append(dve.do(lambda e, t=t: e.tensor_scalar(
                        h[:, t, :], X[:, base + t, :], mv[b][:, t, 0:1], rstd[b][:, 1, t:t + 1], ALU.subtract, ALU.mult), scales[half]))
                yield
            for pair in range(TILES // 2):
                ht_ready.append(turn(h, ht, b, pair, ready[2 * pair + 1]))
                yield
            return ready, ht_ready

        def turn(src, dst, b, pair, src_ready):
            i, bank, free = ring_a.take()
            for q in range(4):
                t, c = 2 * pair + q // 2, q % 2
                done = pe.do(lambda e, q=q, t=t, c=c, bank=bank: e.transpose(bank[:, q * P:(q + 1) * P], src[:, t, c * P:(c + 1) * P], ident),
                             src_ready, consts_landed, *free, signal=q == 3)
            copied = act.do(lambda e: e.copy(
                dst[:, :, pair * 2 * P:(pair + 1) * 2 * P].rearrange("p c (t n) -> p t c n", t=2),
                bank.rearrange("p (t c n) -> p t c n", t=2, c=DC)), done, *batch_free[b])
            ring_a.free(i, copied)
            return copied

        def add_bias(b, bias, landed, *readers):
            sl = slice(b * TILES, (b + 1) * TILES)
            return pool.do(lambda e: e.tensor_tensor(X[:, sl, :], X[:, sl, :],
                                                     bias.unsqueeze(1).to_broadcast([P, TILES, D]), ALU.add), landed, *readers)

        def project_out(b, chunks, weight, waits_for, extra):
            for pair in range(TILES // 2):
                i, bank, free = ring_a.take()
                for q in range(2):
                    t = 2 * pair + q
                    for c, chunk in enumerate(chunks):
                        done = pe.do(lambda e, q=q, t=t, c=c, chunk=chunk, bank=bank: e.matmul(
                            bank[:, q * D:(q + 1) * D], chunk[:, t * P:(t + 1) * P], weight[:, c, :],
                            start=(q == 0 and c == 0), stop=(c == len(chunks) - 1), skip_group_check=True),
                            *waits_for(t), *free, signal=(q == 1 and c == len(chunks) - 1))
                t0 = b * TILES + 2 * pair
                added = dve.do(lambda e, t0=t0, bank=bank: e.tensor_tensor(
                    X[:, t0:t0 + 2, :], X[:, t0:t0 + 2, :], bank.rearrange("p (t d) -> p t d", t=2), ALU.add), done, *extra)
                ring_a.free(i, added)
                x_ready[b][2 * pair] = x_ready[b][2 * pair + 1] = added
                yield
            batch_free[b] = lasts()

        first_fill = {}
        first_stack = {}

        def split(phase, b, name, m, n, f, f_ready):
            key = (phase, b, name)
            dst = parts_dram[key][m, :, :, n * SPAN:(n + 1) * SPAN].rearrange("s p t -> p s t")
            j, both, both_free = work.take()
            two = both[:, :].bitcast(BF16).rearrange("p (s t) -> p s t", s=2)
            hi = act.do(lambda e: e.copy(two[:, 0, :], f), f_ready, *both_free)
            r, rest, rest_free = work.take()
            r1 = dve.do(lambda e: e.tensor_tensor(rest[:, :], f, two[:, 0, :], ALU.subtract), hi, *rest_free)
            mid = act.do(lambda e: e.copy(two[:, 1, :], rest[:, :]), r1)
            w, last, last_free = work.take()
            low = last[:, 0:SPAN // 2].bitcast(BF16)
            lo = pool.do(lambda e: e.tensor_tensor(low, rest[:, :], two[:, 1, :], ALU.subtract), mid, *last_free)
            work.free(r, lo, mid)
            s1 = sp.dma(dst[:, 0:2, :], two, work_stored[j], mid)
            s2 = sp.dma(dst[:, 2, :], low, work_stored[w], lo)
            parts_stored[(*key, m)] += [s1, s2]
            work.free(j, lo, s1)
            work.free(w, s2)
            return r1

        def load_stacks(phase, b, g):
            s, stack, free = stacks.take()
            rows_of = slice(g % 2 * HPG * HD, (g % 2 + 1) * HPG * HD)
            for name, blocks in (("q", ((0, 3), (0, 2), (0, 1))), ("k", ((0, 1), (0, 1), (0, 1), (1, 1), (1, 1), (2, 1)))):
                src = parts_dram[(phase, b, name)][g // 2, :, rows_of, :].rearrange("s (j d) t -> s d j t", j=HPG)
                at = 0
                for first, count in blocks:
                    for part in range(first, first + count):
                        landed = sp.dma(stack[name][at:at + HD, :, :], src[part], stack_landing[s],
                                        *parts_stored[(phase, b, name, g // 2)], *free)
                        at += HD
            return s, stack, landed

        def ones_column(va, *waits):
            z = pool.do(lambda e: e.memset(va[:, :, :, HD:STRIP], 0.0), *waits)
            return pool.do(lambda e: e.memset(va[:, :, :, HD:HD + 1], 1.0), z)

        h_free = [[], []]

        def head_outputs(b, g, c, bank_i, bank, pv_done, eps):
            r, o, free = work.take()
            copied = act.do(lambda e: e.copy(o[:, :], bank), pv_done, *free)
            ring_c.free(bank_i, copied)
            i, tb, tfree = ring_a.take()
            for t in range(TPS):
                turned = pe.do(lambda e, t=t: e.transpose(tb[:, t * P:(t + 1) * P], o[:, t * P:(t + 1) * P], ident),
                               copied, *tfree, signal=t == TPS - 1)
            work.free(r, turned)
            v = tb.rearrange("p (t j e) -> p t j e", t=TPS, j=HPG)
            den = small[:, 0:16].rearrange("p (t j) -> p t j", t=TPS)
            if eps:
                d = dve.do(lambda e: e.tensor_scalar(den, v[:, :, :, HD], eps, None, ALU.max), turned, dve.last())
                d = dve.do(lambda e: e.reciprocal(den, den), d)
            else:
                d = dve.do(lambda e: e.reciprocal(den, v[:, :, :, HD]), turned, dve.last())
            dst = H[b][:, c * TPS:(c + 1) * TPS, g * HPG * HD:(g + 1) * HPG * HD].rearrange("p t (j e) -> p t j e", j=HPG)
            done = dve.do(lambda e: e.tensor_tensor(dst, v[:, :, :, 0:HD], den.unsqueeze(3).to_broadcast([P, TPS, HPG, HD]),
                                                    ALU.mult), d, *h_free[b])
            ring_a.free(i, done)
            return done

        def linear_inputs(b):
            h_ready, ht_ready = yield from normalise(b)
            biased = add_bias(b, bias_row[:, 2, :], row0_landed, h_ready[-1])
            ht, va, qfeat, state = HT[b], vaug[b], qfeats[b], states[b]
            ktok = H[b]
            ones_ready = ones_column(va, pool.last())
            q_ready = []
            for name, wcol, bcol in (("q", 0, 0), ("k", D, 2)):
                for m in range(DC):
                    for n in range(SPANS):
                        i, bank, free = ring_b.take()
                        for c in range(DC):
                            done = pe.do(lambda e: e.matmul(
                                bank, w_attn0[:, c, wcol + m * P:wcol + (m + 1) * P], ht[:, c, n * SPAN:(n + 1) * SPAN],
                                start=c == 0, stop=c == DC - 1), w0_landed, ht_ready[2 * n + 1], *free, signal=c == DC - 1)
                        yield
                        bias = bias_col[:, bcol + m:bcol + m + 1]
                        j1, low, low_free = work.take()
                        j2, pos, pos_free = work.take()
                        z = act.do(lambda e: e.activation(pos[:, :], bank, ACT.Identity, bias=bias), done, cols_landed, *pos_free)
                        ring_b.free(i, z)
                        t = dve.do(lambda e: e.tensor_scalar(low[:, :], pos[:, :], 0.0, None, ALU.min), z, *low_free)
                        t = act.do(lambda e: e.activation(low[:, :], low[:, :], ACT.Exp), t)
                        f = qfeat[:, m, n * SPAN:(n + 1) * SPAN] if name == "q" else pos[:, :]
                        f_done = dve.do(lambda e: e.scalar_tensor_tensor(f, pos[:, :], 0.0, low[:, :], ALU.max, ALU.add), t)
                        work.free(j1, f_done)
                        yield
                        r1 = split("a", b, name, m, n, f, f_done)
                        work.free(j2, f_done, r1, act.last())
                        if name == "q":
                            q_ready.append(f_done)
                        yield
            if b == 0:
                small_inputs()
                first_stack["a", b] = load_stacks("a", b, 0)
            tok_ready = []
            for t in range(TILES):
                i, bank, free = ring_b.take()
                for c in range(DC):
                    done = pe.do(lambda e: e.matmul(bank, ht[:, c, t * P:(t + 1) * P], w_attn0[:, c, D:3 * D], start=c == 0, stop=c == DC - 1),
                                 w0_landed, ht_ready[t // 2], *free, signal=c == DC - 1)
                yield
                j1, z, zfree = work.take()
                j2, low, low_free = work.take()
                zd = dve.do(lambda e: e.tensor_tensor(z[:, 0:D], bank[:, 0:D], bias_row[:, 0, :], ALU.add), done, row0_landed, *zfree)
                dve.do(lambda e: e.tensor_tensor(va[:, t, :, 0:HD], bank[:, D:2 * D].rearrange("p (h e) -> p h e", h=HEADS),
                                                 bias_row[:, 1, :].rearrange("p (h e) -> p h e", h=HEADS), ALU.add), done)
                vd = dve.last()
                ring_b.free(i, vd)
                l = dve.do(lambda e: e.tensor_scalar(low[:, 0:D], z[:, 0:D], 0.0, None, ALU.min), zd, *low_free)
                l = act.do(lambda e: e.activation(low[:, 0:D], low[:, 0:D], ACT.Exp), l)
                yield
                kd = dve.do(lambda e: e.scalar_tensor_tensor(ktok[:, t, :], z[:, 0:D], 0.0, low[:, 0:D], ALU.max, ALU.add), l, ht_ready[-1])
                work.free(j1, kd)
                work.free(j2, kd)
                tok_ready.append(kd)
            bank_i, sbank, sfree = ring_c.take()
            state_ready = [None]
            copied = None
            for c in range(TILES - 1):
                for half in range(DC):
                    done = pe.do(lambda e: e.matmul(
                        sbank[:, half * D:(half + 1) * D], ktok[:, c, half * P:(half + 1) * P],
                        va[:, c, half * HALF_HEADS:(half + 1) * HALF_HEADS, :].rearrange("p h e -> p (h e)"),
                        start=(c == 0 and half == 0), stop=True, skip_group_check=True),
                        tok_ready[c], ones_ready, copied, *sfree, signal=half == DC - 1)
                copied = dve.do(lambda e: e.tensor_tensor(
                    state[:, c, :].rearrange("p (m h e) -> p m h e", m=DC, h=HALF_HEADS),
                    sbank.rearrange("p (m h e) -> p m h e", m=DC, h=HALF_HEADS),
                    const("headmask").unsqueeze(1).unsqueeze(3).to_broadcast([P, DC, HALF_HEADS, STRIP]), ALU.mult), done)
                state_ready.append(copied)
                yield
                yield
            ring_c.free(bank_i, copied)
            h_free[b] = [done]
            ready[b] = (q_ready, tok_ready, state_ready, biased)

        ready = {}

        def linear_heads(b):
            q_ready, tok_ready, state_ready, biased = ready[b]
            va, qfeat, state = vaug[b], qfeats[b], states[b]
            loaded = first_stack["a", b]
            for g in range(GROUPS):
                s, stack, landed = loaded
                if g + 1 < GROUPS:
                    loaded = load_stacks("a", b, g + 1)
                outs, pending = {}, {}

                def scores(t):
                    i, bank, free = ring_b.take()
                    for j in range(HPG):
                        done = pe.do(lambda e: e.matmul(
                            bank[:, j * P:(j + 1) * P], stack["k"][0:KSTACK, j, t * P:(t + 1) * P],
                            stack["q"][0:KSTACK, j, t * P:(t + 1) * P], start=j == 0, stop=True, skip_group_check=True),
                            landed, *free, signal=j == HPG - 1)
                    w, a, afree = work.take()
                    masked = dve.do(lambda e: e.tensor_tensor(
                        a[:, :].rearrange("p (j n) -> p j n", j=HPG), bank.rearrange("p (j n) -> p j n", j=HPG),
                        const("causal01").unsqueeze(1).to_broadcast([P, HPG, P]), ALU.mult), done, *afree)
                    ring_b.free(i, masked)
                    pending[t] = (w, a, masked)

                def sums(t):
                    c, q = t // TPS, t % TPS
                    w, a, masked = pending.pop(t)
                    if q == 0:
                        outs[c] = ring_c.take()
                    bank_i, bank, free = outs[c]
                    if t:
                        pe.do(lambda e: e.matmul(bank[:, q * P:(q + 1) * P], state[:, t - 1, g * P:(g + 1) * P],
                                                 qfeat[:, g // 2, t * P:(t + 1) * P], start=q == 0, stop=False, skip_group_check=True),
                              state_ready[t], *q_ready, *free, signal=False)
                    for j in range(HPG):
                        done = pe.do(lambda e: e.matmul(
                            bank[j * STRIP:(j + 1) * STRIP, q * P:(q + 1) * P], va[:, t, g * HPG + j, :],
                            a[:, j * P:(j + 1) * P], start=t == 0, stop=True, skip_group_check=True),
                            masked, tok_ready[t], *free, signal=j == HPG - 1)
                    work.free(w, done)
                    if q == TPS - 1:
                        heads_done[b] = head_outputs(b, g, c, bank_i, bank, done, DEN_EPS)

                yield from staged(range(TILES), scores, sums)
                stacks.free(s, pe.last())
            area_free[b] = lasts()

        heads_done = {}

        def finish_attention(b, weight, weight_landed, biased):
            turned = []
            for pair in range(TILES // 2):
                turned.append(turn(H[b], HT[b], b, pair, heads_done[b]))
                yield
            yield from project_out(b, [HT[b][:, c, :] for c in range(DC)], weight, lambda t: [turned[t // 2], weight_landed], [biased])

        qx = [carve(area[b], 0, 4096).rearrange("p (g t) -> p g t", g=GROUPS) for b in range(BATCH)]
        qx2 = [carve(area[b], 0, 2048).rearrange("p (g t) -> p g t", g=DC) for b in range(BATCH)]
        kbd, vx = {}, {}
        for b in range(BATCH):
            for phase, at in (("b", 4096), ("e", 2048)):
                kbd[phase, b] = carve(area[b], at, GROUPS * HPG * CTX).rearrange("p (g j k) -> p g j k", g=GROUPS, j=HPG)
                vx[phase, b] = carve(area[b], at + GROUPS * HPG * CTX, HEADS * STRIP).rearrange("p (h e) -> p h e", h=HEADS)
        hx = [H[b][:, :, :].rearrange("p t d -> p (t d)").rearrange("p (c t) -> p c t", c=DC) for b in range(BATCH)]
        ox = [[hx[b][:, 0, :], hx[b][:, 1, :], HT[b][:, 0, :], HT[b][:, 1, :]] for b in range(BATCH)]
        pt = Slots([carve(stack_area, 2048 * s, 2048).rearrange("p (j t) -> p j t", j=HPG) for s in range(2)])
        ctx_t = sb("ctx_t", [P, BATCH, DC, CTX])
        ctx_landed = load("ctx", ctx_t[:, :, :, :], A["ctx_t"].rearrange("b (c p) k -> p b c k", p=P))
        fmbd = sb("fmbd", [P, 2, P])
        fm_row = sb("fm_row", [CTX, 2, HPG * STRIP])
        load("fm", fmbd[:, :, :], A["fm_bd"].rearrange("v p n -> p v n"))
        load("fm", fm_row[:, 0, :], A["fm_b_row"].to_broadcast([CTX, P]))
        fm_landed = load("fm", fm_row[:, 1, :], A["sign_row"].to_broadcast([CTX, P]))
        load("row1", bias_row[:, 3, :], rows("L0_xattn_fc_b", D))
        load("row1", bias_row[:, 4, :], rows("L0_ffn_norm_gamma", D))
        row1_landed = load("row1", bias_row[:, 5, :], rows("L0_ffn_norm_beta", D))
        mask_i = stack_area[:, 1024:1024 + TILES * CTX].bitcast(I32).rearrange("p (t k) -> p t k", t=TILES)
        maskneg = sb("maskneg", [P, TILES, CTX], BF16)
        mask_landed = load("mask", mask_i, A["mask"].rearrange("(t p) k -> p t k", p=P))
        fm_b_signed = pool.do(lambda e: e.tensor_tensor(bias_col[:, 16:17], bias_col[:, 4:5], const("sign"), ALU.mult),
                              cols_landed, consts_landed)

        def staged(items, first, second, lag=2):
            items = list(items)
            for n in range(len(items) + lag):
                if n < len(items):
                    first(items[n])
                if n >= lag:
                    second(items[n - lag])
                yield

        def context_attention(b, phase):
            masked = phase == "e"
            queries, q_ready, kv_ready, ox_free, _ = ready[b]
            keys, values = kbd[phase, b], vx[phase, b]
            hold, spans, outs, turned = {}, {}, {}, {}

            def soft(item):
                c, g, q = item
                t = c * TPS + q
                i, bank, free = ring_b.take()
                s = bank[:, 0:HPG * CTX]
                done = pe.do(lambda e: e.matmul(
                    s, queries[:, g // 2 if masked else g, t * P:(t + 1) * P], keys[:, g, :, :].rearrange("p j k -> p (j k)"),
                    start=True, stop=not masked, skip_group_check=True), *q_ready, *kv_ready, *free, signal=not masked)
                s3 = s.rearrange("p (j k) -> p j k", j=HPG)
                if masked:
                    done = pe.do(lambda e: e.matmul(s3, ident_bf[:, :], maskneg[:, t, :].unsqueeze(1).to_broadcast([P, HPG, CTX]),
                                                    start=False, stop=True, skip_group_check=True), masks_ready, mask_ready)
                at = 32 + 8 * (soft_count[0] % 8)
                soft_count[0] += 1
                mx, den = small[:, at:at + HPG], small[:, at + 4:at + 8]
                m = dve.do(lambda e: e.tensor_reduce(mx, s3, AX.X, ALU.max), done, small_free.get(at))
                w, ex, wfree = work.take()
                ex3 = ex[:, 0:HPG * CTX].rearrange("p (j k) -> p j k", j=HPG)
                d = dve.do(lambda e: e.tensor_tensor(ex3, s3, mx.unsqueeze(2).to_broadcast([P, HPG, CTX]), ALU.subtract), m, *wfree)
                ring_b.free(i, d)
                scale = rowany[:, t:t + 1] if masked else 1.0
                x = act.do(lambda e: e.activation(ex[:, 0:HPG * CTX], ex[:, 0:HPG * CTX], ACT.Exp, scale=scale), d)
                hold[item] = (w, ex, ex3, den, x, at)

            def divide(item):
                w, ex, ex3, den, x, at = hold[item]
                r = dve.do(lambda e: e.tensor_reduce(den, ex3, AX.X, ALU.add), x)
                r = dve.do(lambda e: e.reciprocal(den, den), r)
                n = pool.do(lambda e: e.tensor_tensor(ex3, ex3, den.unsqueeze(2).to_broadcast([P, HPG, CTX]), ALU.mult), r)
                small_free[at] = n
                hold[item] = (w, ex, n)

            def turn_p(item):
                c, g, q = item
                if q == 0:
                    spans[c, g] = pt.take()
                pi, p_t, pt_free = spans[c, g]
                w, ex, n = hold.pop(item)
                i, bank, free = ring_a.take()
                for j in range(HPG):
                    done = pe.do(lambda e: e.transpose(bank[0:CTX, j * P:(j + 1) * P], ex[:, j * CTX:(j + 1) * CTX], ident),
                                 n, *free, signal=j == HPG - 1)
                work.free(w, done)
                turned[c, g] = act.do(lambda e: e.copy(p_t[0:CTX, :, q * P:(q + 1) * P], bank[0:CTX, :].rearrange("p (j n) -> p j n", j=HPG)),
                                      done, *pt_free)
                ring_a.free(i, turned[c, g])

            def sums(c, g):
                pi, p_t, _ = spans[c, g]
                if not masked or g % 2 == 0:
                    outs[c] = ring_c.take()
                oi, obank, ofree = outs[c]
                for j in range(HPG):
                    head = g * HPG + j
                    strip = (head % HALF_HEADS) // 2 if masked else j
                    done = pe.do(lambda e: e.matmul(
                        obank[strip * STRIP:(strip + 1) * STRIP, :], values[0:CTX, head, :], p_t[0:CTX, j, :],
                        start=(not masked or head % 2 == 0), stop=(not masked or head % 2 == 1), skip_group_check=True),
                        turned[c, g], *kv_ready, *ofree, signal=j == HPG - 1)
                pt.free(pi, done)
                if not masked or g % 2 == 1:
                    slot = g // 2 if masked else g
                    ox_ready[b, c] = act.do(lambda e: e.copy(ox[b][slot][:, c * SPAN:(c + 1) * SPAN], obank), done, *ox_free)
                    ring_c.free(oi, ox_ready[b, c])

            items = [(c, g, q) for c in range(SPANS) for g in range(GROUPS) for q in range(TPS)]
            for n in range(len(items) + 7):
                if n < len(items):
                    soft(items[n])
                if 2 <= n < len(items) + 2:
                    divide(items[n - 2])
                if 4 <= n < len(items) + 4:
                    turn_p(items[n - 4])
                if n >= 7 and (n - 7) % TPS == TPS - 1:
                    sums(*items[n - 7][0:2])
                yield
            area_free[b] = lasts()

        small_free = {}
        soft_count = [0]
        ox_ready = {}

        def feature_inputs(b):
            h_ready, ht_ready = yield from normalise(b)
            biased = add_bias(b, bias_row[:, 3, :], row1_landed, h_ready[-1])
            free_a = list(area_free[b])
            q, keys, values = qx[b], kbd["b", b], vx["b", b]
            q_ready = []
            for g in range(GROUPS):
                for n in range(SPANS):
                    i, bank, free = ring_b.take()
                    done = pe.do(lambda e: e.matmul(bank, fmbd[:, g % 2, :], HT[b][:, g // 2, n * SPAN:(n + 1) * SPAN],
                                                    start=True, stop=True), fm_landed, ht_ready[2 * n + 1], *free)
                    yield
                    qd = act.do(lambda e: e.activation(q[:, g, n * SPAN:(n + 1) * SPAN], bank, ACT.Exp, bias=bias_col[:, 16:17],
                                                       scale=const("sign")), done, fm_b_signed, *free_a)
                    ring_b.free(i, qd)
                    q_ready.append(qd)
            z = pool.do(lambda e: e.memset(keys[:, :, :, :], 0.0), *free_a)
            kv_ready = []
            for g in range(GROUPS):
                i, bank, free = ring_b.take()
                done = pe.do(lambda e: e.matmul(bank[:, 0:CTX], fmbd[:, g % 2, :], ctx_t[:, b, g // 2, :], start=True, stop=True),
                             fm_landed, ctx_landed, *free)
                i2, bank2, free2 = ring_b.take()
                done2 = pe.do(lambda e: e.matmul(bank2[0:CTX, 0:P], ctx_t[:, b, g // 2, :], fmbd[:, g % 2, :], start=True, stop=True), *free2)
                yield
                for j in range(HPG):
                    st = slice(j * STRIP, (j + 1) * STRIP)
                    k = act.do(lambda e: e.activation(keys[st, g, j, :], bank[st, 0:CTX], ACT.Exp, bias=bias_col[st, 16:17],
                                                      scale=const("sign")[st, :]), done, z)
                ring_b.free(i, k)
                j1, tmp, tfree = work.take()
                s = dve.do(lambda e: e.tensor_tensor(tmp[0:CTX, 0:P], bank2[0:CTX, 0:P], fm_row[:, 0, :], ALU.add), done2, fm_landed, *tfree)
                ring_b.free(i2, s)
                s = dve.do(lambda e: e.tensor_tensor(tmp[0:CTX, 0:P], tmp[0:CTX, 0:P], fm_row[:, 1, :], ALU.mult), s)
                s = act.do(lambda e: e.activation(values[0:CTX, g * HPG:(g + 1) * HPG, :].rearrange("p h e -> p (h e)"), tmp[0:CTX, 0:P],
                                                  ACT.Exp), s, *free_a)
                work.free(j1, s)
                kv_ready.append(s)
                yield
                kv_ready.append(dve.do(lambda e: e.tensor_scalar(keys[:, g, :, :], keys[:, g, :, :], 1.0 / 16.0, None, ALU.mult), k))
            ready[b] = (q, q_ready, kv_ready, [pe.last()], biased)

        def finish_context(b, chunks, weight, weight_landed, biased):
            yield from project_out(b, chunks, weight, lambda t: [ox_ready[b, t // TPS], weight_landed], [biased])

        gate_w = W2[:, 1024:1024 + DC * GATE_COLS].rearrange("p (c n) -> p c n", c=DC)
        table = W2[:, 1300:1300 + TABLE + D]
        raw_t = W2[:, 1640:1640 + DC * TILES_FFN].rearrange("p (c n) -> p c n", c=DC)
        ffn_rows = sb("ffn_rows", [P, 3 * COMP + 2 + KNOTS + 2])
        load("ffn", raw_t, A["sig_t"].rearrange("(c p) n -> p c n", p=P))
        load("ffn", gate_w[:, :, CLUSTERS + TILES_FFN:], A["L0_ffn_compress_w1"].rearrange("(c p) n -> p c n", p=P))
        load("ffn", table[0:TILES_FFN, :], A["spline_table"])
        R_B1, R_W2, R_B2, R_KN, R_TEMP, R_SCALE = 0, COMP, 3 * COMP, 3 * COMP + 2, 3 * COMP + 2 + KNOTS, 3 * COMP + 3 + KNOTS
        load("ffn", ffn_rows[:, R_B1:R_B1 + COMP], rows("L0_ffn_compress_b1", COMP))
        load("ffn", ffn_rows[:, R_W2:R_W2 + 2 * COMP], A["compress_w2_t"].rearrange("(a i) n -> a (i n)", a=1).to_broadcast([P, 2 * COMP]))
        load("ffn", ffn_rows[:, R_B2:R_B2 + 2], rows("L0_ffn_compress_b2", 2))
        load("ffn", ffn_rows[:, R_KN:R_KN + KNOTS], rows("L0_ffn_knot_values", KNOTS))
        load("ffn", ffn_rows[:, R_TEMP:R_TEMP + 1], rows("L0_ffn_temperature", 1))
        ffn_landed = load("ffn", ffn_rows[:, R_SCALE:R_SCALE + 1], rows("L0_ffn_output_scale", 1))

        def ffn_weights():
            q = small[:, 128:256].rearrange("p (c n) -> p c n", c=DC)
            n = small[:, 256:384].rearrange("p (c n) -> p c n", c=DC)
            a = dve.do(lambda e: e.tensor_scalar(q, raw_t, 0.3, None, ALU.is_gt), ffn_landed)
            bb = dve.do(lambda e: e.tensor_scalar(n, raw_t, -0.3, None, ALU.is_lt), ffn_landed)
            a = dve.do(lambda e: e.tensor_tensor(q, q, n, ALU.subtract), a, bb)
            a = dve.do(lambda e: e.tensor_tensor(q, q, raw_t, ALU.subtract), a)
            sig = gate_w[:, :, CLUSTERS:CLUSTERS + TILES_FFN]
            a = dve.do(lambda e: e.tensor_tensor(sig, raw_t, q, ALU.add), a)
            cs = small[:, 384:400].rearrange("p (c n) -> p c n", c=DC)
            a = dve.do(lambda e: e.tensor_reduce(cs, sig.rearrange("p c (n k) -> p c n k", k=TPC), AX.X, ALU.add), a)
            pos = small[:, 400:416].rearrange("p (c n) -> p c n", c=DC)
            neg = small[:, 416:432].rearrange("p (c n) -> p c n", c=DC)
            a1 = dve.do(lambda e: e.tensor_scalar(pos, cs, 0.0, None, ALU.is_gt), a)
            a2 = dve.do(lambda e: e.tensor_scalar(neg, cs, 0.0, None, ALU.is_lt), a)
            a = dve.do(lambda e: e.tensor_tensor(gate_w[:, :, 0:CLUSTERS], pos, neg, ALU.subtract), a2)
            a = dve.do(lambda e: e.tensor_tensor(small[:, 440:440 + KNOTS - 1], ffn_rows[:, R_KN + 1:R_KN + KNOTS],
                                                 ffn_rows[:, R_KN:R_KN + KNOTS - 1], ALU.subtract), a)
            a = dve.do(lambda e: e.tensor_scalar(small[:, 448:449], ffn_rows[:, R_TEMP:R_TEMP + 1], 1e-6, None, ALU.add), a)
            a = dve.do(lambda e: e.reciprocal(small[:, 449:450], small[:, 448:449]), a)
            return dve.do(lambda e: e.tensor_scalar(small[:, 450:451], small[:, 449:450], -1.0, None, ALU.mult), a)

        def calibrate(dst, s, scratch, ready):
            u, low, diff, step = scratch
            a = act.do(lambda e: e.activation(u, s, ACT.Exp, scale=small[:, 450:451]), ready)
            yield
            a = dve.do(lambda e: e.tensor_scalar(u, u, 1.0, None, ALU.add), a)
            a = dve.do(lambda e: e.reciprocal(u, u), a)
            a = dve.do(lambda e: e.tensor_scalar(u, u, float(KNOTS - 1), None, ALU.mult), a)
            a = dve.do(lambda e: e.tensor_scalar(low, u, 1.0, None, ALU.is_ge), a)
            yield
            for k in range(2, KNOTS - 1):
                a = dve.do(lambda e, k=k: e.scalar_tensor_tensor(low, u, float(k), low, ALU.is_ge, ALU.add), a)
            a = dve.do(lambda e: e.tensor_tensor(u, u, low, ALU.subtract), a)
            a = dve.do(lambda e: e.tensor_scalar(dst, low, 0.0, ffn_rows[:, R_KN:R_KN + 1], ALU.is_equal, ALU.mult), a)
            a = dve.do(lambda e: e.tensor_scalar(diff, low, 0.0, small[:, 440:441], ALU.is_equal, ALU.mult), a)
            for k in range(1, KNOTS - 1):
                for acc, col in ((dst, ffn_rows[:, R_KN + k:R_KN + k + 1]), (diff, small[:, 440 + k:441 + k])):
                    a = dve.do(lambda e, k=k, col=col: e.tensor_scalar(step, low, float(k), col, ALU.is_equal, ALU.mult), a)
                    a = dve.do(lambda e, acc=acc: e.tensor_tensor(acc, acc, step, ALU.add), a)
                yield
            a = dve.do(lambda e: e.tensor_tensor(diff, diff, u, ALU.mult), a)
            return dve.do(lambda e: e.tensor_tensor(dst, dst, diff, ALU.add), a)

        def first_max(onehot, g, scratch, col, ready):
            eq = scratch
            a = dve.do(lambda e: e.tensor_reduce(col, g, AX.X, ALU.max), ready)
            a = dve.do(lambda e: e.tensor_tensor(eq, g, col.unsqueeze(2).to_broadcast([P, TILES, 8]), ALU.is_equal), a)
            a = dve.do(lambda e: e.tensor_scalar(onehot, const("iota8").unsqueeze(1).to_broadcast([P, TILES, 8]), -8.0, None, ALU.add), a)
            a2 = dve.do(lambda e: e.tensor_tensor(eq, eq, onehot, ALU.mult), a)
            a3 = dve.do(lambda e: e.tensor_reduce(col, eq, AX.X, ALU.min), a2)
            return dve.do(lambda e: e.tensor_tensor(onehot, onehot, col.unsqueeze(2).to_broadcast([P, TILES, 8]), ALU.is_equal), a3)

        def spline_ffn(b):
            weights_ready = weights_done[0]
            h_ready, ht_ready = yield from normalise(b)
            at = [0]

            def take(n):
                at[0] += n
                return carve(area[b], at[0] - n, n)
            S = take(TILES * GATE_COLS).rearrange("p (t n) -> p t n", t=TILES)
            free_a = list(area_free[b])
            s_ready = []
            for t in range(TILES):
                i, bank, free = ring_b.take()
                for c in range(DC):
                    done = pe.do(lambda e, c=c, t=t, bank=bank: e.matmul(bank[:, 0:GATE_COLS], HT[b][:, c, t * P:(t + 1) * P], gate_w[:, c, :],
                                                              start=c == 0, stop=c == DC - 1), weights_ready, ht_ready[t // 2], *free, signal=c == 1)
                s = act.do(lambda e, t=t, bank=bank: e.copy(S[:, t, :], bank[:, 0:GATE_COLS]), done, *free_a)
                ring_b.free(i, s)
                yield
            cs, ts, zc = S[:, :, 0:CLUSTERS], S[:, :, CLUSTERS:CLUSTERS + TILES_FFN], S[:, :, CLUSTERS + TILES_FFN:]
            n8 = TILES * 8
            v8 = [take(n8).rearrange("p (t n) -> p t n", t=TILES) for _ in range(8)]
            gate, oc, ol, sel = v8[4], v8[5], v8[6], v8[7]
            col = take(TILES)
            w = dve.do(lambda e: e.tensor_tensor(zc, zc, ffn_rows[:, R_B1:R_B1 + COMP].unsqueeze(1).to_broadcast([P, TILES, COMP]), ALU.add), s)
            gl = act.do(lambda e: e.activation(zc, zc, ACT.Gelu), w)
            big = take(TILES * COMP)
            big3 = big.rearrange("p (t n) -> p t n", t=TILES)
            comp = take(2 * TILES).rearrange("p (i t) -> p i t", i=2)
            yield
            a = yield from calibrate(gate, cs, v8[0:4], s)
            a = first_max(oc, gate, v8[0], col, a)
            big4 = big.rearrange("p (t c k) -> p t c k", t=TILES, c=CLUSTERS)
            a = dve.do(lambda e: e.tensor_tensor(big4, ts.rearrange("p t (c k) -> p t c k", c=CLUSTERS),
                                                 oc.unsqueeze(3).to_broadcast([P, TILES, CLUSTERS, TPC]), ALU.mult), a)
            a = dve.do(lambda e: e.tensor_reduce(sel, big.rearrange("p (t c k) -> p t k c", t=TILES, c=CLUSTERS), AX.X, ALU.add), a)
            a = yield from calibrate(gate, sel, v8[0:4], a)
            a = first_max(ol, gate, v8[0], col, a)
            a = dve.do(lambda e: e.tensor_tensor(big4, oc.unsqueeze(3).to_broadcast([P, TILES, CLUSTERS, TPC]),
                                                 ol.unsqueeze(2).to_broadcast([P, TILES, CLUSTERS, TPC]), ALU.mult), a)
            onehot_ready = a
            yield
            prod = take(TILES * COMP).rearrange("p (t n) -> p t n", t=TILES)
            a = gl
            for i2 in range(2):
                w2 = ffn_rows[:, R_W2 + i2 * COMP:R_W2 + (i2 + 1) * COMP].unsqueeze(1).to_broadcast([P, TILES, COMP])
                a = dve.do(lambda e, w2=w2: e.tensor_tensor(prod, zc, w2, ALU.mult), a)
                a = dve.do(lambda e, i2=i2: e.tensor_reduce(comp[:, i2, :], prod, AX.X, ALU.add), a)
            for i2 in range(2):
                cd = act.do(lambda e, i2=i2: e.activation(comp[:, i2, :], comp[:, i2, :], ACT.Tanh, bias=ffn_rows[:, R_B2 + i2:R_B2 + i2 + 1]), a)
            par = take(TILES * TABLE).rearrange("p (t n) -> p t n", t=TILES)
            dirs = take(TILES * D).rearrange("p (t n) -> p t n", t=TILES)
            yield from pause(2)
            for pair in range(TILES // TPS):
                i, bank, free = ring_a.take()
                for q in range(TPS):
                    done = pe.do(lambda e, q=q, pair=pair, bank=bank: e.transpose(bank[0:TILES_FFN, q * P:(q + 1) * P], big3[:, pair * TPS + q, :], ident),
                                 onehot_ready, *free, signal=q == TPS - 1)
                wi, oh, ofree = work.take()
                turned = act.do(lambda e, oh=oh, bank=bank: e.copy(oh[0:TILES_FFN, :], bank[0:TILES_FFN, :]), done, *ofree)
                ring_a.free(i, turned)
                yield
                for q in range(TPS):
                    t = pair * TPS + q
                    i, bank, free = ring_b.take()
                    done = pe.do(lambda e, q=q, oh=oh, bank=bank: e.matmul(bank[:, 0:TABLE + D], oh[0:TILES_FFN, q * P:(q + 1) * P], table[0:TILES_FFN, :],
                                                            start=True, stop=True), turned, *free)
                    c1 = act.do(lambda e, t=t, bank=bank: e.copy(par[:, t, :], bank[:, 0:TABLE]), done, *free_a)
                    c2 = act.do(lambda e, t=t, bank=bank: e.copy(dirs[:, t, :], bank[:, TABLE:TABLE + D]), done)
                    ring_b.free(i, c2)
                    yield
                work.free(wi, done)
            hh = take(TILES * GRID).rearrange("p (t n) -> p t n", t=TILES)
            h2 = prod.rearrange("p t n -> p (t n)")[:, 0:TILES * GRID].rearrange("p (t n) -> p t n", t=TILES)

            def bc(i2):
                return comp[:, i2, :].unsqueeze(2).to_broadcast([P, TILES, GRID])
            a = dve.do(lambda e: e.tensor_tensor(hh, par[:, :, 0:GRID], bc(0), ALU.mult), c2, cd)
            a2 = dve.do(lambda e: e.tensor_tensor(h2, par[:, :, GRID:2 * GRID], bc(1), ALU.mult), a)
            a = dve.do(lambda e: e.tensor_tensor(hh, hh, h2, ALU.add), a2)
            a = dve.do(lambda e: e.tensor_tensor(hh, hh, par[:, :, 2 * GRID:3 * GRID], ALU.add), a)
            a = dve.do(lambda e: e.scalar_tensor_tensor(hh, hh, 0.0, par[:, :, 3 * GRID:4 * GRID], ALU.max, ALU.mult), a)
            a = dve.do(lambda e: e.tensor_reduce(col, hh, AX.X, ALU.add), a)
            a = dve.do(lambda e: e.tensor_tensor(col, col, par[:, :, 4 * GRID], ALU.add), a)
            a = dve.do(lambda e: e.tensor_scalar(col, col, ffn_rows[:, R_SCALE:R_SCALE + 1], None, ALU.mult), a)
            base = b * TILES
            ys = []
            for t in range(TILES):
                y = dve.do(lambda e, t=t: e.scalar_tensor_tensor(dirs[:, t, :], dirs[:, t, :], col[:, t:t + 1], H[b][:, t, :], ALU.mult, ALU.add), a)
                s1 = dve.do(lambda e, t=t: e.bn_stats(stats[b][:, t, :], dirs[:, t, :]), y)
                agg = dve.do(lambda e, t=t: e.bn_aggr(mv[b][:, t, :], stats[b][:, t, :]), s1)
                yield
            v = pool.do(lambda e: e.tensor_scalar(rstd[b][:, 0, :], mv[b][:, :, 1], LN_EPS, None, ALU.add), agg)
            v = pool.do(lambda e: e.tensor_tensor(rstd[b][:, 1, :], rstd[b][:, 0, :], const("halfneg"), ALU.pow), v)
            yield
            for t in range(TILES):
                n = dve.do(lambda e, t=t: e.scalar_tensor_tensor(dirs[:, t, :], dirs[:, t, :], mv[b][:, t, 0:1], bias_row[:, 4, :],
                                                                 ALU.subtract, ALU.mult), v, row1_landed)
                bt = dve.do(lambda e, t=t: e.scalar_tensor_tensor(dirs[:, t, :], dirs[:, t, :], rstd[b][:, 1, t:t + 1], bias_row[:, 5, :],
                                                                  ALU.mult, ALU.add), n)
                x_ready[b][t] = pool.do(lambda e, t=t: e.tensor_tensor(X[:, base + t, :], X[:, base + t, :], dirs[:, t, :], ALU.add), bt)
                yield
            batch_free[b] = lasts()
            area_free[b] = lasts()

        w_qkv = carve(area[0], 5344, 1536).rearrange("p (c n) -> p c n", c=DC)
        w_proj = carve(area[0], 9216, 512).rearrange("p (c n) -> p c n", c=DC)

        def attention_inputs(b):
            h_ready, ht_ready = yield from normalise(b)
            biased = add_bias(b, bias_row[:, 1, :], row2_landed[0], h_ready[-1])
            ht, va = HT[b], vaug[b]
            ones_ready = ones_column(va, pool.last(), *area_free[b])
            for n in range(SPANS):
                for name, wcol, bcol in (("q", 0, 12), ("k", D, 14)):
                    for m in range(DC):
                        i, bank, free = ring_b.take()
                        for c in range(DC):
                            done = pe.do(lambda e: e.matmul(
                                bank, w_qkv[:, c, wcol + m * P:wcol + (m + 1) * P], ht[:, c, n * SPAN:(n + 1) * SPAN],
                                start=c == 0, stop=c == DC - 1), w2_landed[0], ht_ready[2 * n + 1], *free, signal=c == DC - 1)
                        yield
                        j, f, ffree = work.take()
                        bias = bias_col[:, bcol + m:bcol + m + 1]
                        scale = 0.25 if name == "q" else 1.0
                        fd = dve.do(lambda e: e.tensor_scalar(f[:, :], bank, bias, scale, ALU.add, ALU.mult), done, cols_landed, *ffree)
                        ring_b.free(i, fd)
                        r1 = split("d", b, name, m, n, f[:, :], fd)
                        work.free(j, r1, act.last())
                        yield
            if b == 0:
                first_stack["d", b] = load_stacks("d", b, 0)
            for pair in range(TILES // 2):
                i, bank, free = ring_b.take()
                for q in range(2):
                    t = 2 * pair + q
                    for c in range(DC):
                        done = pe.do(lambda e: e.matmul(
                            bank[:, q * D:(q + 1) * D], ht[:, c, t * P:(t + 1) * P], w_qkv[:, c, 2 * D:3 * D],
                            start=(q == 0 and c == 0), stop=c == DC - 1, skip_group_check=True), *free, signal=(q == 1 and c == DC - 1))
                yield
                for q in range(2):
                    t = 2 * pair + q
                    vd = dve.do(lambda e: e.tensor_tensor(
                        va[:, t, :, 0:HD], bank[:, q * D:(q + 1) * D].rearrange("p (h e) -> p h e", h=HEADS),
                        bias_row[:, 0, :].rearrange("p (h e) -> p h e", h=HEADS), ALU.add), done, row2_landed[0], *area_free[b])
                ring_b.free(i, vd)
            h_free[b] = [ht_ready[-1]]
            inputs[b] = (vd, ones_ready, biased)

        inputs = {}
        mneg = [sb(f"mneg{i}", [STRIP, 2, P], BF16) for i in range(2)]
        mxt = [sb(f"mx{i}", [P, HPG, TILES, 2]) for i in range(2)]
        mcomb = sb("mcomb", [P, HPG * TILES])
        mneg_free = [[], []]

        def maxima(b, g, slot, stack, landed):
            mx = mxt[slot]
            for j in range(HPG):
                for t in range(TILES):
                    for half in range(t // TPS + 1):
                        n = min(t + 1 - half * TPS, TPS) * P
                        diagonal = half == t // TPS
                        i, bank, free = ring_a.take()
                        done = pe.do(lambda e, j=j, t=t, half=half, n=n, bank=bank: e.matmul(
                            bank[:, 0:n], stack["q"][0:KSTACK, j, t * P:(t + 1) * P],
                            stack["k"][0:KSTACK, j, half * SPAN:half * SPAN + n], start=True, stop=True, skip_group_check=True),
                            landed, *free, signal=not diagonal)
                        if diagonal:
                            done = pe.do(lambda e, n=n, bank=bank: e.matmul(bank[:, n - P:n], ident_bf[:, :], mask_qk_bf[:, :],
                                                                 start=False, stop=True, skip_group_check=True), masks_ready)
                        red = dve.do(lambda e, j=j, t=t, half=half, n=n, bank=bank: e.tensor_reduce(mx[:, j, t, half:half + 1], bank[:, 0:n], AX.X, ALU.max),
                                     done, *mneg_free[slot])
                        ring_a.free(i, red)
                        yield
            m3 = mcomb[:, :].rearrange("p (j t) -> p j t", j=HPG)
            a = dve.do(lambda e: e.tensor_copy(m3[:, :, 0:TPS], mx[:, :, 0:TPS, 0]), red, mcomb_free[0])
            a = dve.do(lambda e: e.tensor_tensor(m3[:, :, TPS:], mx[:, :, TPS:, 0], mx[:, :, TPS:, 1], ALU.max), a)
            i, bank, free = ring_a.take()
            done = pe.do(lambda e: e.transpose(bank[0:STRIP, 0:P], mcomb[:, :], ident), a, *free)
            mcomb_free[0] = done
            ng = mneg[slot]
            a = dve.do(lambda e: e.tensor_scalar(ng[:, 0, :], bank[0:STRIP, 0:P], -1.0, None, ALU.mult), done, *mneg_free[slot])
            a = dve.do(lambda e: e.scalar_tensor_tensor(ng[:, 1, :], bank[0:STRIP, 0:P], -1.0, ng[:, 0, :], ALU.mult, ALU.subtract), a)
            ring_a.free(i, a)
            for s in range(2):
                dst = stack["q"][KSTACK + s:KSTACK + s + 1, :, :].rearrange("p j (t n) -> p (j t) n", n=P)
                m_landed = sp.dma(dst, ng[:, s, :], max_landing[slot], a)
            mneg_free[slot] = [m_landed]
            result[(b, g)] = m_landed
            yield

        mcomb_free = [None]
        result = {}

        def weighted(b, g, stack, landed, m_landed):
            v_ready, ones_ready, _ = inputs[b]
            for c in range(SPANS):
                bank_i, obank, ofree = ring_c.take()
                held = None

                def values(kb, off, ps, last):
                    for j in range(HPG):
                        w, p, ex = ps[j]
                        done = pe.do(lambda e, j=j, p=p: e.matmul(
                            obank[j * STRIP:(j + 1) * STRIP, off:SPAN], vaug[b][:, kb, g * HPG + j, :], p[:, 0:SPAN - off],
                            start=kb == 0, stop=last, skip_group_check=True), ex, v_ready, ones_ready, *ofree, signal=j == HPG - 1)
                    for j in range(HPG):
                        work.free(ps[j][0], done)
                    return done

                blocks = (c + 1) * TPS
                for kb in range(blocks):
                    off = max(0, kb * P - c * SPAN)
                    ps = []
                    for j in range(HPG):
                        i, bank, free = ring_b.take()
                        n = SPAN - off
                        diagonal = kb * P >= c * SPAN
                        done = pe.do(lambda e, j=j, kb=kb, off=off, n=n, bank=bank: e.matmul(
                            bank[:, 0:n], stack["k"][0:KSTACK + 2, j, kb * P:(kb + 1) * P],
                            stack["q"][0:KSTACK + 2, j, c * SPAN + off:(c + 1) * SPAN], start=True, stop=True, skip_group_check=True),
                            landed, m_landed, first_fill["ones"], *free, signal=not diagonal)
                        if diagonal:
                            done = pe.do(lambda e, bank=bank: e.matmul(bank[:, 0:P], ident_bf[:, :], mask_kq_bf[:, :], start=False, stop=True,
                                                            skip_group_check=True))
                        w, p, wfree = work.take()
                        ex = act.do(lambda e, p=p, n=n, bank=bank: e.activation(p[:, 0:n], bank[:, 0:n], ACT.Exp), done, *wfree)
                        ring_b.free(i, ex)
                        ps.append((w, p, ex))
                        if j < HPG - 1:
                            yield
                    if held:
                        values(*held, False)
                    held = (kb, off, ps)
                    yield
                done = values(*held, True)
                heads_done[b] = head_outputs(b, g, c, bank_i, obank, done, 0.0)

        def softmax_attention(other_inputs, after_first):
            for s in range(len(stacks.buffers)):
                first_fill["ones"] = act.do(lambda e: e.copy(
                    stacks.buffers[s]["k"][KSTACK:KSTACK + 2, :, :].rearrange("p j t -> p (j t)"),
                    const("sign")[KSTACK:KSTACK + 2, :].to_broadcast([2, HPG * SEQ])), *lasts())
            seq = [(b, g) for b in range(BATCH) for g in range(GROUPS)]
            loaded = {0: first_stack["d", 0]}
            side = other_inputs
            previous = None
            for n in range(len(seq) + 1):
                steps_a, steps_b = None, None
                if n == GROUPS - 1:
                    drain(side)
                if n + 1 < len(seq):
                    loaded[n + 1] = load_stacks("d", *seq[n + 1])
                if n < len(seq):
                    (b, g), (s, stack, landed) = seq[n], loaded[n]
                    steps_a = maxima(b, g, n % 2, stack, landed)
                if n:
                    pb, pg, ps, pstack, planded = previous
                    steps_b = weighted(pb, pg, pstack, planded, result[(pb, pg)])
                for _ in range(LEAD):
                    next(steps_a or side, None)
                while steps_a or steps_b:
                    if steps_b and next(steps_b, "end") == "end":
                        steps_b = None
                    if steps_a and next(steps_a, "end") == "end":
                        steps_a = None
                    next(side, None)
                    if not steps_b:
                        next(side, None)
                if n:
                    stacks.free(ps, pe.last())
                    if pg == GROUPS - 1:
                        area_free[pb] = lasts()
                        if pb == 0:
                            side = after_first()
                if n < len(seq):
                    previous = (b, g, s, stack, landed)
            yield from side

        w_x = W1[:, :].rearrange("p (c n) -> p c n", c=DC)
        rowany = sb("rowany", [P, TILES])

        def mask_weights():
            a = None
            for half in range(2):
                w, buf, free = work.take()
                v = buf[:, 0:TPS * CTX].rearrange("p (t k) -> p t k", t=TPS)
                sl = slice(half * TPS, (half + 1) * TPS)
                a = dve.do(lambda e, v=v, sl=sl: e.tensor_scalar(v, mask_i[:, sl, :], 0.0, None, ALU.not_equal), mask_landed, *free)
                r = dve.do(lambda e, v=v, sl=sl: e.tensor_reduce(rowany[:, sl], v, AX.X, ALU.max), a)
                a = dve.do(lambda e, v=v, sl=sl: e.tensor_scalar(maskneg[:, sl, :], v, 1.0, 1e9, ALU.subtract, ALU.mult), r)
                work.free(w, a)
            return a

        def masked_inputs(b):
            h_ready, ht_ready = yield from normalise(b)
            biased = add_bias(b, bias_row[:, 3, :], row3_landed, h_ready[-1])
            free_a = list(area_free[b])
            queries, keys, values = qx2[b], kbd["e", b], vx["e", b]
            q_ready, kv_ready = [], []
            for m in range(DC):
                for n in range(SPANS):
                    i, bank, free = ring_b.take()
                    for c in range(DC):
                        done = pe.do(lambda e, c=c, m=m, n=n, bank=bank: e.matmul(
                            bank, w_x[:, c, m * P:(m + 1) * P], HT[b][:, c, n * SPAN:(n + 1) * SPAN],
                            start=c == 0, stop=c == DC - 1), wx_landed[0], ht_ready[2 * n + 1], *free, signal=c == DC - 1)
                    q = dve.do(lambda e, m=m, n=n, bank=bank: e.tensor_scalar(queries[:, m, n * SPAN:(n + 1) * SPAN], bank, bias_col[:, 8 + m:9 + m],
                                                                   0.25, ALU.add, ALU.mult), done, cols_landed, *free_a)
                    ring_b.free(i, q)
                    q_ready.append(q)
                    yield
            z = pool.do(lambda e: e.memset(values[:, :, :], 0.0), *free_a)
            for m in range(DC):
                i, bank, free = ring_b.take()
                for c in range(DC):
                    done = pe.do(lambda e, c=c, m=m, bank=bank: e.matmul(bank[:, 0:CTX], w_x[:, c, D + m * P:D + (m + 1) * P], ctx_t[:, b, c, :],
                                                              start=c == 0, stop=c == DC - 1), *free, signal=c == DC - 1)
                for h8 in range(HALF_HEADS):
                    k = dve.do(lambda e, m=m, h8=h8, bank=bank: e.tensor_scalar(
                        keys[:, 2 * m + h8 // HPG, h8 % HPG, :], bank[:, 0:CTX], bias_col[:, 10 + m:11 + m],
                        const("headmask")[:, h8:h8 + 1], ALU.add, ALU.mult), done, *free_a)
                ring_b.free(i, k)
                kv_ready.append(k)
            i, bank, free = ring_b.take()
            for c in range(DC):
                done = pe.do(lambda e, c=c, bank=bank: e.matmul(bank[0:CTX, 0:D], ctx_t[:, b, c, :], w_x[:, c, 2 * D:3 * D],
                                                     start=c == 0, stop=c == DC - 1), *free, signal=c == DC - 1)
            for odd in range(2):
                src = bank[0:CTX, 0:D].rearrange("p (h o e) -> p h o e", o=2, e=HD)[:, :, odd, :]
                brow = bias_row[0:CTX, 2, :].rearrange("p (h o e) -> p h o e", o=2, e=HD)[:, :, odd, :]
                dst = values[0:CTX, :, :].rearrange("p (h o) e -> p h o e", o=2)[:, :, odd, odd * HD:(odd + 1) * HD]
                k = dve.do(lambda e, dst=dst, src=src, brow=brow: e.tensor_tensor(dst, src, brow, ALU.add), done, z, row2_landed[0])
            ring_b.free(i, k)
            kv_ready.append(k)
            ready[b] = (queries, q_ready, kv_ready, [pe.last()], biased)

        NE = EXPERTS + 1
        wd_shared = carve(area[0], 8144, D)
        wg = carve(area[0], 3792, DC * NE * INNER).rearrange("p (c e i) -> p c e i", c=DC, e=NE)
        wu = carve(area[1], 3792, DC * NE * INNER).rearrange("p (c e i) -> p c e i", c=DC, e=NE)
        sel = carve(area[1], 8144, 1024, BF16).rearrange("p (e n) -> p e n", e=EXPERTS)
        wd = carve(stack_area, 4096, EXPERTS * D).rearrange("p (e n) -> p e n", e=EXPERTS)
        gw = sb("gate_weights", [P, DC, EXPERTS])

        def load_experts(waits):
            for c in range(DC):
                rs = slice(c * P, (c + 1) * P)
                for w, name, shared in ((wg, "L1_ffn_Wg", "L1_ffn_sg"), (wu, "L1_ffn_Wu", "L1_ffn_su")):
                    load("moe", w[:, c, 0:EXPERTS, :], A[name][:, rs, :].rearrange("e p i -> p e i"), *waits)
                    load("moe", w[:, c, EXPERTS, :], A[shared][rs, :])
            load("moe", wd[:, 0:EXPERTS, :], A["L1_ffn_Wd"].rearrange("e p n -> p e n"))
            return load("moe", wd_shared, A["L1_ffn_sd"])

        def moe_inputs(b):
            h_ready, ht_ready = yield from normalise(b)
            free_a = list(area_free[b])
            combt = carve(area[b], 0, 512, BF16)
            sc = carve(area[b], 512, P).rearrange("p (t e) -> p t e", t=TILES)
            rank = carve(area[b], 640, P).rearrange("p (t e) -> p t e", t=TILES)
            col = carve(area[b], 768, TILES)
            comb3 = carve(area[b], 784, TILES * PARTS * EXPERTS).rearrange("p (t s e) -> p t s e", t=TILES, s=PARTS)
            cbf = carve(area[b], 1168, P // 2, BF16).rearrange("p (t e) -> p t e", t=TILES)
            g1 = carve(area[b], 1232, 1024).rearrange("p (t i j) -> p t i j", t=TPS, i=EXPERTS)
            g2 = carve(area[b], 2256, 1024).rearrange("p (t i j) -> p t i j", t=TPS, i=EXPERTS)
            i, bank, free = ring_b.take()
            for t in range(TILES):
                for c in range(DC):
                    done = pe.do(lambda e: e.matmul(bank[:, t * EXPERTS:(t + 1) * EXPERTS], HT[b][:, c, t * P:(t + 1) * P],
                                                    gw[:, c, :], start=(t == 0 and c == 0), stop=c == 1, skip_group_check=True),
                                 gw_landed, ht_ready[t // 2], *free, signal=(t == TILES - 1 and c == 1))
            a = act.do(lambda e, bank=bank: e.activation(sc.rearrange("p t e -> p (t e)"), bank[:, 0:P], ACT.Exp, scale=-1.0), done, *free_a)
            ring_b.free(i, a)
            yield
            yield
            a = dve.do(lambda e: e.tensor_scalar(sc, sc, 1.0, None, ALU.add), a)
            a = dve.do(lambda e: e.reciprocal(sc, sc), a)
            yield
            before = const("before").rearrange("p (i j) -> p i j", i=EXPERTS).unsqueeze(1).to_broadcast([P, TPS, EXPERTS, EXPERTS])
            for half in range(SPANS):
                ts = slice(half * TPS, (half + 1) * TPS)
                me = sc[:, ts, :].unsqueeze(3).to_broadcast([P, TPS, EXPERTS, EXPERTS])
                other = sc[:, ts, :].unsqueeze(2).to_broadcast([P, TPS, EXPERTS, EXPERTS])
                a1 = dve.do(lambda e: e.tensor_tensor(g1, other, me, ALU.is_gt), a)
                yield
                a2 = dve.do(lambda e: e.tensor_tensor(g2, other, me, ALU.is_equal), a1)
                yield
                a2 = dve.do(lambda e: e.tensor_tensor(g2, g2, before, ALU.mult), a2)
                yield
                a2 = dve.do(lambda e: e.tensor_tensor(g1, g1, g2, ALU.add), a2)
                yield
                a = dve.do(lambda e: e.tensor_reduce(rank[:, ts, :], g1, AX.X, ALU.add), a2)
                yield
            a = dve.do(lambda e: e.scalar_tensor_tensor(sc, rank, float(TOPK) - 0.5, sc, ALU.is_lt, ALU.mult), a)
            a = dve.do(lambda e: e.tensor_reduce(col, sc, AX.X, ALU.add), a)
            a = dve.do(lambda e: e.reciprocal(col, col), a)
            a = dve.do(lambda e: e.tensor_tensor(sc, sc, col.unsqueeze(2).to_broadcast([P, TILES, EXPERTS]), ALU.mult), a)
            for s in range(PARTS):
                a = dve.do(lambda e: e.tensor_copy(cbf, sc), a)
                a = dve.do(lambda e, s=s: e.tensor_copy(comb3[:, :, s, :], cbf), a)
                if s < PARTS - 1:
                    a = dve.do(lambda e: e.tensor_tensor(sc, sc, cbf, ALU.subtract), a)
                yield
            yield from pause(2)
            comb_ready = []
            for n in range(SPANS):
                i, bank, free = ring_b.take()
                for q in range(TPS):
                    done = pe.do(lambda e, q=q, n=n, bank=bank: e.transpose(
                        bank[0:PARTS * EXPERTS, q * P:(q + 1) * P], comb3[:, n * TPS + q, :, :].rearrange("p s e -> p (s e)"), ident),
                        a, *free, signal=q == TPS - 1)
                cd = act.do(lambda e, n=n, bank=bank: e.copy(combt[0:PARTS * EXPERTS, n * SPAN:(n + 1) * SPAN], bank[0:PARTS * EXPERTS, :]), done, *free_a)
                ring_b.free(i, cd)
                comb_ready.append(cd)
                yield
            ready[b] = (ht_ready, comb_ready)

        def moe(b):
            ht_ready, comb_ready = ready[b]
            combt = carve(area[b], 0, 512, BF16)
            landed = moe_landed[0]
            ht = HT[b]
            for n in range(SPANS):
                cols = slice(n * SPAN, (n + 1) * SPAN)
                outs = [ring_c.take() for _ in range(2)]
                held = {}

                def up(x):
                    banks = []
                    for w in (wg, wu):
                        i, bank, free = ring_a.take() if w is wg else ring_b.take()
                        for c in range(DC):
                            done = pe.do(lambda e, c=c, w=w, bank=bank: e.matmul(bank, w[:, c, x, :], ht[:, c, cols], start=c == 0, stop=c == 1),
                                         landed, ht_ready[2 * n + 1], *free, signal=c == 1)
                        banks.append((i, bank, done))
                    (gi, gbank, gdone), (ui, ubank, udone) = banks
                    k, s, sfree = work.take()
                    a = act.do(lambda e: e.activation(s[:, :], gbank, ACT.Silu), gdone, *sfree)
                    ring_a.free(gi, a)
                    a = dve.do(lambda e: e.tensor_tensor(s[:, :], s[:, :], ubank, ALU.mult), a, udone)
                    ring_b.free(ui, a)
                    if x < EXPERTS:
                        i, bank, free = ring_b.take()
                        done = pe.do(lambda e: e.matmul(bank, sel[0:PARTS * EXPERTS, x, :], combt[0:PARTS * EXPERTS, cols], start=True, stop=True),
                                     sel_ready[0], comb_ready[n], *free)
                        a = dve.do(lambda e: e.tensor_tensor(s[:, :], s[:, :], bank, ALU.mult), a, done)
                        ring_b.free(i, a)
                    held[x] = (k, s, a)

                def down(x):
                    k, s, ready = held.pop(x)
                    for q in range(TPS):
                        oi, obank, ofree = outs[q // 2]
                        o = q % 2
                        done = pe.do(lambda e, q=q, o=o, obank=obank: e.matmul(
                            obank[:, o * D:(o + 1) * D], s[:, q * P:(q + 1) * P], wd_shared if x == EXPERTS else wd[:, x, :],
                            start=(x == 0 and o == 0), stop=x == NE - 1, skip_group_check=True), ready, *ofree, signal=q == TPS - 1)
                    work.free(k, done)
                    return done

                for x in range(NE + 2):
                    if x < NE:
                        up(x)
                    if x >= 2:
                        done = down(x - 2)
                    yield
                for o in range(2):
                    oi, obank, _ = outs[o]
                    t0 = b * TILES + n * TPS + 2 * o
                    added = dve.do(lambda e, t0=t0, obank=obank: e.tensor_tensor(X[:, t0:t0 + 2, :], X[:, t0:t0 + 2, :],
                                                                    obank.rearrange("p (t d) -> p t d", t=2), ALU.add), done)
                    ring_c.free(oi, added)
                    x_ready[b][n * TPS + 2 * o] = x_ready[b][n * TPS + 2 * o + 1] = added

        row2_landed, w2_landed, wx_landed, moe_landed, sel_ready = [None], [None], [None], [None], [None]
        gw_landed = load("gw", gw[:, :, :], A["gate_w_t"].rearrange("(c p) e -> p c e", p=P))

        def drain(stage):
            for _ in stage:
                pass

        def weave(main, side, times=1):
            for _ in main:
                for _ in range(times):
                    next(side, None)
            drain(side)

        def chain(*stages):
            for stage in stages:
                yield from stage

        w_out0 = w_attn0[:, :, 3 * D:4 * D]
        w_outx = w_x[:, :, 3 * D:4 * D]
        ox_e = [[hx[b][:, c, :] for c in range(DC)] for b in range(BATCH)]
        def advance(main, side):
            for _ in main:
                next(side, None)

        def with_tokens_of_all(slots):
            slots.hold_back(*lasts())
            yield

        weights_done = []

        def small_inputs():
            nonlocal mask_ready
            weights_done.append(ffn_weights())
            mask_ready = mask_weights()
            stacks.hold_back(masks_ready, mask_ready)
            pt.hold_back(mask_ready)

        drain(linear_inputs(0))
        other = linear_inputs(1)
        advance(linear_heads(0), other)
        pt.hold_back(*lasts())
        advance(chain(finish_attention(0, w_out0, w0_landed, ready[0][3]), feature_inputs(0), context_attention(0, "b")), other)
        drain(other)
        stacks.idle.reverse()
        stacks.hold_back(pe.last())
        first_stack["a", 1] = load_stacks("a", 1, 0)
        for i, v in enumerate((A["L1_attn_b_attn"][2 * D:3 * D], A["L1_attn_b_proj"], A["L1_xattn_bv"])):
            row2_landed[0] = load("row2", bias_row[:, i, :], spread(v, D), *lasts())
        load("w2", w_qkv, A["L1_attn_w_attn"].rearrange("(c p) n -> p c n", p=P))
        w2_landed[0] = load("w2", w_proj, A["L1_attn_w_proj"].rearrange("(c p) n -> p c n", p=P))
        stacks.hold_back(pe.last())
        other = chain(finish_context(0, ox[0], w_fc, wa_landed, ready[0][4]), spline_ffn(0), attention_inputs(0))
        advance(chain(linear_heads(1), with_tokens_of_all(pt), finish_attention(1, w_out0, w0_landed, ready[1][3]), feature_inputs(1),
                      context_attention(1, "b")), other)
        row3_landed = load("row3", bias_row[:, 3, :], spread(A["L1_xattn_bo"], D), *lasts())
        wx_landed[0] = load("wx", w_x, A["L1_xattn_w"].rearrange("(c p) n -> p c n", p=P))
        drain(other)
        stacks.hold_back(*lasts())
        stacks.add(stack_slots[2], *lasts())
        drain(softmax_attention(
            chain(finish_context(1, ox[1], w_fc, wa_landed, ready[1][4]), spline_ffn(1), attention_inputs(1)),
            lambda: chain(finish_attention(0, w_proj, w2_landed[0], inputs[0][2]), masked_inputs(0))))
        pt.hold_back(*lasts())
        moe_landed[0] = load_experts(lasts())
        sel_ready[0] = dve.do(lambda e: e.tensor_copy(sel[0:PARTS * EXPERTS], const("parts")[0:PARTS * EXPERTS, :].unsqueeze(2)
                                                      .to_broadcast([PARTS * EXPERTS, EXPERTS, P])), *lasts())
        weave(context_attention(0, "e"), chain(finish_attention(1, w_proj, w2_landed[0], inputs[1][2]), masked_inputs(1)))
        weave(context_attention(1, "e"), chain(finish_context(0, ox_e[0], w_outx, wx_landed[0], ready[0][4]), moe_inputs(0)))
        weave(moe(0), chain(finish_context(1, ox_e[1], w_outx, wx_landed[0], ready[1][4]), moe_inputs(1)))
        drain(moe(1))
        out_tiles = out.rearrange("b (t p) d -> p (b t) d", p=P)
        stored = landing("stored")
        for b in range(BATCH):
            for n in range(SPANS):
                t0 = b * TILES + n * TPS
                end = sp.dma(out_tiles[:, t0:t0 + TPS, :], X[:, t0:t0 + TPS, :], stored, *x_ready[b][n * TPS:(n + 1) * TPS])
        sp.wait(end, *lasts())
        for l in loads.values():
            sp.wait(l.last())


def lay_out(I):
    f = {k: np.ascontiguousarray(v) for k, v in I.items()}
    a = {"x": f["x"], "consts": constants()}
    a["ctx_t"] = np.ascontiguousarray(f["ctx_1024"].transpose(0, 2, 1))
    a["mask"] = f["mask_1x1xSxS2_ik0"].reshape(SEQ, CTX)
    a["L0_attn_w"] = np.concatenate([f[f"L0_attn_W{n}"].T for n in "qkvo"], axis=1)
    for n in ("L0_attn_bq", "L0_attn_bk", "L0_attn_bv", "L0_attn_bo", "L0_xattn_fc_b", "L0_ffn_knot_values", "L0_ffn_temperature",
              "L0_ffn_compress_w1", "L0_ffn_compress_b1", "L0_ffn_compress_b2", "L0_ffn_norm_gamma", "L0_ffn_norm_beta",
              "L0_ffn_output_scale", "L1_attn_w_attn", "L1_attn_b_attn", "L1_attn_w_proj", "L1_attn_b_proj", "L1_xattn_bq",
              "L1_xattn_bk", "L1_xattn_bv", "L1_xattn_bo", "L1_ffn_Wg", "L1_ffn_Wu", "L1_ffn_Wd", "L1_ffn_sg", "L1_ffn_su", "L1_ffn_sd"):
        a[n] = f[n]
    bd = np.zeros((2, P, P), np.float32)
    for v in range(2):
        for j in range(HPG):
            r = (v * HPG + j) * HD
            bd[v, r:r + HD, j * STRIP:j * STRIP + HD] = f["L0_xattn_fm_w"].T
            bd[v, r:r + HD, j * STRIP + HD:(j + 1) * STRIP] = f["L0_xattn_fm_w"].T
    a["fm_bd"] = bd
    cols = [f["L0_attn_bq"], f["L0_attn_bk"], np.tile(f["L0_xattn_fm_b"], P // HD), np.zeros(3 * P, np.float32),
            f["L1_xattn_bq"], f["L1_xattn_bk"], f["L1_attn_b_attn"][:2 * D]]
    a["bias_cols"] = np.ascontiguousarray(np.concatenate(cols).reshape(16, P).T)
    a["fm_b_row"] = np.tile(f["L0_xattn_fm_b"], P // HD).reshape(1, P)
    a["sign_row"] = np.where(np.arange(P) % STRIP < HD, 1.0, -1.0).astype(np.float32).reshape(1, P)
    a["fc_w_t"] = np.ascontiguousarray(f["L0_xattn_fc_w"].T)
    a["sig_t"] = np.ascontiguousarray(f["L0_ffn_signatures_raw"].T)
    a["spline_table"] = np.concatenate([f["L0_ffn_spline_w1"].reshape(TILES_FFN, 2 * GRID), f["L0_ffn_spline_b1"],
                                        f["L0_ffn_spline_w2"].reshape(TILES_FFN, GRID), f["L0_ffn_spline_b2"],
                                        f["L0_ffn_directions"]], axis=1)
    a["compress_w2_t"] = np.ascontiguousarray(f["L0_ffn_compress_w2"].T)
    a["L1_xattn_w"] = np.concatenate([f[f"L1_xattn_w{n}"].T for n in "qkvo"], axis=1)
    a["gate_w_t"] = np.ascontiguousarray(f["L1_ffn_gate_w"].T)
    return a


def kernel(**inputs):
    import concourse.bacc as bacc
    from concourse.bass_utils import run_bass_kernel_spmd

    arrays = lay_out({k: np.asarray(v) for k, v in inputs.items()})
    nc = bacc.Bacc("TRN2", target_bir_lowering=False, num_devices=1)
    args = {k: nc.dram_tensor(f"in_{k}", v.shape, mybir.dt.from_np(v.dtype), kind="ExternalInput").ap() for k, v in arrays.items()}
    out = nc.dram_tensor("out", (BATCH, SEQ, D), F32, kind="ExternalOutput").ap()
    build(nc, args, out)
    r = run_bass_kernel_spmd(nc, [{f"in_{k}": v for k, v in arrays.items()}], core_ids=[0])
    return r.results[0]["out"]
```

```python
from contextlib import ExitStack

import numpy as np

import concourse.bass as bass
from concourse import mybir

BATCH, SEQ, D = 2, 1024, 256
CTX = 77
HEADS, HD = 16, 16
P = 128
TILES = SEQ // P
DC = D // P
GROUPS = 4
HPG = HEADS // GROUPS
STRIP = 32
HALF_HEADS = P // HD
SPAN = 512
SPANS = SEQ // SPAN
TPS = SPAN // P
PARTS = 3
KSTACK = 6 * HD
EXPERTS, TOPK, INNER = 16, 4, 128
TILES_FFN, CLUSTERS, TPC = 64, 8, 8
GRID, COMP, KNOTS = 16, 64, 8
GATE_COLS = CLUSTERS + TILES_FFN + COMP
TABLE = 2 * GRID + GRID + GRID + 1
LN_EPS = 1e-5
DEN_EPS = 1e-6
MASKED = -1e30

INPUTS_LEAD = 24
MAXIMA_LEAD = 6
EXTRA_EVERY = 5
RESIDUAL_PAUSE = 6
ONEHOT_PAUSE = 2
ROUTING_PAUSE = 4
DIVIDE_LAG = 2
TURN_LAG = {"b": 4, "e": 5}
SUMS_LAG = 4
SPLIT_EARLY = 5
SPLIT_AHEAD = 2

F32, BF16, I32 = mybir.dt.float32, mybir.dt.bfloat16, mybir.dt.int32
F32R = mybir.dt.float32r
ALU = mybir.AluOpType
ACT = mybir.ActivationFunctionType
AX = mybir.AxisListType

Q_PARTS = (0, 1, 2, 0, 1, 0)
K_PARTS = (0, 0, 0, 1, 1, 2)

CONSTS = {}
_at = 0
for _name, _width in (("ident", P), ("causal01", P), ("headmask", HALF_HEADS), ("sign", 1), ("iota8", 8), ("parts", EXPERTS),
                      ("before", EXPERTS * EXPERTS), ("halfneg", TILES), ("mask_qk", P), ("mask_kq", P)):
    CONSTS[_name] = (_at, _width)
    _at += _width
CONST_COLS = _at
KEPT_COLS = CONSTS["mask_qk"][0]


def constants():
    c = np.zeros((P, CONST_COLS), np.float32)

    def put(name, value):
        at, width = CONSTS[name]
        c[:, at:at + width] = value

    r, k = np.arange(P)[:, None], np.arange(P)[None, :]
    put("ident", r == k)
    put("causal01", r <= k)
    put("mask_qk", np.where(k <= r, 0.0, MASKED))
    put("mask_kq", np.where(r <= k, 0.0, MASKED))
    put("headmask", r // HD == np.arange(HALF_HEADS)[None, :])
    put("sign", np.where(r % STRIP < HD, 1.0, -1.0))
    put("iota8", np.arange(8)[None, :])
    put("parts", (r % EXPERTS == np.arange(EXPERTS)[None, :]) & (r < PARTS * EXPERTS))
    i, j = np.arange(EXPERTS)[:, None], np.arange(EXPERTS)[None, :]
    put("before", (j < i).reshape(1, -1))
    put("halfneg", -0.5)
    return c


class Engine:

    def __init__(self, engine, sem):
        self.engine, self.sem, self.count, self.waited = engine, sem, 0, {}

    def wait(self, *tokens):
        for token in tokens:
            if token is None:
                continue
            sem, value = token
            if self.waited.get(id(sem), 0) < value:
                self.waited[id(sem)] = value
                self.engine.wait_ge(sem, value)

    def do(self, emit, *waits, signal=True):
        self.wait(*waits)
        instruction = emit(self.engine)
        if not signal:
            return None
        self.count += 1
        instruction.then_inc(self.sem, 1)
        return self.last()

    def dma(self, out, in_, landing, *waits):
        self.wait(*waits)
        landing.count += 16
        self.engine.dma_start(out, in_).then_inc(landing.sem, 16)
        return landing.last()

    def last(self):
        return (self.sem, self.count)


class Slots:

    def __init__(self, buffers):
        self.buffers, self.readers = buffers, [()] * len(buffers)
        self.idle = list(range(len(buffers)))

    def take(self):
        i = self.idle.pop(0)
        return i, self.buffers[i], self.readers[i]

    def free(self, i, *readers):
        self.readers[i] = readers
        self.idle.append(i)

    def add(self, buffer, *readers):
        self.buffers.append(buffer)
        self.readers.append(readers)
        self.idle.append(len(self.buffers) - 1)

    def hold_back(self, *tokens):
        self.readers = [tuple(r) + tokens for r in self.readers]


def build(nc, A, out):
    with ExitStack() as ctx:
        def sb(name, shape, dt=F32):
            return ctx.enter_context(nc.sbuf_tensor(name, shape, dt))

        def sb2(name, shape):
            with nc.sbuf_tensor(f"{name}_r", shape, F32R) as rounded:
                pass
            return sb(name, shape), rounded

        sems = {}

        def sem(name):
            sems[name] = ctx.enter_context(nc.semaphore(name))
            return sems[name]

        pe = Engine(nc.tensor, sem("pe_done"))
        act = Engine(nc.scalar, sem("act_done"))
        dve = Engine(nc.vector, sem("dve_done"))
        pool = Engine(nc.gpsimd, sem("pool_done"))
        sp = Engine(nc.sync, sem("sp_done"))

        def landing(name):
            return Engine(None, sem(name))

        psum = ctx.enter_context(nc.psum_tensor("psum", [P, 8, SPAN], F32))
        ring_a = Slots([psum[:, i, :] for i in (0, 1, 2)])
        ring_b = Slots([psum[:, i, :] for i in (3, 4, 5)])
        ring_c = Slots([psum[:, i, :] for i in (6, 7)])

        X = sb("X", [P, BATCH * TILES, D])
        H, H_r = zip(*(sb2(f"H{b}", [P, TILES, D]) for b in range(BATCH)))
        HT, HT_r = zip(*(sb2(f"HT{b}", [P, DC, SEQ]) for b in range(BATCH)))
        stack_area, stack_area_r = sb2("stack_area", [P, 8192])
        area, area_r = zip(*(sb2(f"area{b}", [P, 9728]) for b in range(BATCH)))
        work_bufs, work_r = zip(*(sb2(f"work{i}", [P, SPAN]) for i in range(8)))
        work = Slots(list(work_bufs))
        W1 = sb("W1", [P, 2048])
        W2, W2_r = sb2("W2", [P, 2048])
        consts = sb("const_tile", [P, KEPT_COLS])
        ident_bf = sb("ident_bf", [P, P], BF16)
        mask_qk_bf = sb("mask_qk_bf", [P, P], BF16)
        mask_kq_bf = sb("mask_kq_bf", [P, P], BF16)
        bias_row = sb("bias_row", [P, 6, D])
        bias_col = sb("bias_col", [P, 17])
        stats = [sb(f"stats{b}", [P, TILES, 6]) for b in range(BATCH)]
        mv = [sb(f"mv{b}", [P, TILES, 2]) for b in range(BATCH)]
        rstd = [sb(f"rstd{b}", [P, 2, TILES]) for b in range(BATCH)]
        small = sb("small", [P, 456])

        masks_once = stack_area[:, 0:CONST_COLS - KEPT_COLS]

        def const(name):
            at, width = CONSTS[name]
            if at >= KEPT_COLS:
                return masks_once[:, at - KEPT_COLS:at - KEPT_COLS + width]
            return consts[:, at:at + width]

        ident = const("ident")

        def carve(region, at, n, dt=F32):
            view = region[:, at:at + n]
            return view if dt is F32 else view.bitcast(dt)

        parts_dram = {(phase, b, name): nc.dram_tensor(f"parts_{phase}{b}{name}", (DC, PARTS, P, SEQ), BF16, kind="Internal").ap()
                      for phase in "ad" for b in range(BATCH) for name in "qk"}
        stack_words = HPG * SEQ // 2

        def stack_slot(*places):
            return {n: carve(region, at, stack_words, BF16).rearrange("p (j t) -> p j t", j=HPG) for n, (region, at) in zip("qk", places)}

        stack_slots = [stack_slot((stack_area, 0), (stack_area, 2048)), stack_slot((stack_area, 4096), (stack_area, 6144)),
                       stack_slot((area[0], 6880), (area[1], 5344))]
        stacks = Slots(stack_slots[0:2])
        stack_landing = [landing(f"stack_landed{s}") for s in range(3)]
        max_landing = [landing(f"max_landed{s}") for s in range(2)]
        work_stored = [landing(f"work{i}_stored") for i in range(len(work.buffers))]
        parts_stored = {(*key, m): [] for key in parts_dram for m in range(DC)}

        vaug = [carve(area[b], 0, 4096).rearrange("p (t h e) -> p t h e", t=TILES, h=HEADS) for b in range(BATCH)]
        qfeats = [carve(area[b], 4096, 2048).rearrange("p (m t) -> p m t", m=DC) for b in range(BATCH)]
        states = [carve(area[b], 6144, 7 * SPAN).rearrange("p (c n) -> p c n", c=7) for b in range(BATCH)]

        loads = {}

        def load(group, dst, src, *waits):
            if group not in loads:
                loads[group] = landing(f"landed_{group}")
            return sp.dma(dst, src, loads[group], *waits)

        def spread(vector, n, partitions=P):
            return vector.rearrange("(a n) -> a n", a=1).to_broadcast([partitions, n])

        def rows(name, n):
            return spread(A[name], n)

        x_tiles = A["x"].rearrange("b (t p) d -> p (b t) d", p=P)
        def load_x(b):
            return [load(f"x{b}{n}", X[:, t:t + TPS, :], x_tiles[:, t:t + TPS, :]) for n, t in enumerate(range(b * TILES, (b + 1) * TILES, TPS))]

        x_landed = [load_x(0)]
        load("consts", consts[:, :], A["consts"][:, 0:KEPT_COLS])
        consts_landed = load("consts", masks_once, A["consts"][:, KEPT_COLS:])
        w_attn0 = W1[:, :].rearrange("p (c n) -> p c n", c=DC)
        w0_landed = load("w0", w_attn0, A["L0_attn_w"].rearrange("(c p) n -> p c n", p=P))
        for i, n in enumerate(("L0_attn_bk", "L0_attn_bv", "L0_attn_bo")):
            row0_landed = load("row0", bias_row[:, i, :], rows(n, D))
        cols_landed = load("cols", bias_col[:, 0:16], A["bias_cols"])
        x_landed.append(load_x(1))
        w_fc = W2[:, 0:1024].rearrange("p (g n) -> p g n", g=GROUPS)
        wa_landed = load("wa", w_fc, A["fc_w_t"].rearrange("(g p) n -> p g n", p=P))

        casts = [act.do(lambda e, o=o, n=n: e.copy(o[:, :], const(n)), consts_landed)
                 for o, n in ((ident_bf, "ident"), (mask_qk_bf, "mask_qk"), (mask_kq_bf, "mask_kq"))]
        masks_ready = casts[-1]

        x_ready = [[x_landed[b][t // TPS] for t in range(TILES)] for b in range(BATCH)]
        batch_free = [[] for _ in range(BATCH)]
        area_free = [[], []]
        mask_ready = None

        def lasts():
            return [pe.last(), act.last(), dve.last(), pool.last()]

        def pause(steps):
            for _ in range(steps):
                yield

        def normalise(b):
            yield from pause(RESIDUAL_PAUSE)
            h, ht, base = H[b], HT[b], b * TILES
            ready, ht_ready, scales = [], [], []
            for half in range(2):
                ts = range(half * 4, half * 4 + 4)
                taken = [dve.do(lambda e: e.bn_stats(stats[b][:, t, :], X[:, base + t, :]), x_ready[b][t], *batch_free[b]) for t in ts]
                for t, s in zip(ts, taken):
                    done = dve.do(lambda e: e.bn_aggr(mv[b][:, t, :], stats[b][:, t, :]), s)
                sl = slice(half * 4, half * 4 + 4)
                v = pool.do(lambda e, sl=sl: e.tensor_scalar(rstd[b][:, 0, sl], mv[b][:, sl, 1], LN_EPS, None, ALU.add), done,
                            consts_landed)
                scales.append(pool.do(lambda e, sl=sl: e.tensor_tensor(rstd[b][:, 1, sl], rstd[b][:, 0, sl],
                                                                       const("halfneg")[:, 0:4], ALU.pow), v))
                yield
            for half in range(2):
                for t in range(half * 4, half * 4 + 4):
                    ready.append(dve.do(lambda e, t=t: e.tensor_scalar(
                        h[:, t, :], X[:, base + t, :], mv[b][:, t, 0:1], rstd[b][:, 1, t:t + 1], ALU.subtract, ALU.mult), scales[half]))
                yield
            for pair in range(TILES // 2):
                ht_ready.append(turn(h, ht, b, pair, ready[2 * pair + 1]))
                yield
            return ready, ht_ready

        def turn(src, dst, b, pair, src_ready):
            i, bank, free = ring_a.take()
            for q in range(4):
                t, c = 2 * pair + q // 2, q % 2
                done = pe.do(lambda e, q=q, t=t, c=c, bank=bank: e.transpose(bank[:, q * P:(q + 1) * P], src[:, t, c * P:(c + 1) * P], ident),
                             src_ready, consts_landed, *free, signal=q == 3)
            copied = act.do(lambda e: e.copy(
                dst[:, :, pair * 2 * P:(pair + 1) * 2 * P].rearrange("p c (t n) -> p t c n", t=2),
                bank.rearrange("p (t c n) -> p t c n", t=2, c=DC)), done, *batch_free[b])
            ring_a.free(i, copied)
            return copied

        def add_bias(b, bias, landed, *readers):
            sl = slice(b * TILES, (b + 1) * TILES)
            return pool.do(lambda e: e.tensor_tensor(X[:, sl, :], X[:, sl, :],
                                                     bias.unsqueeze(1).to_broadcast([P, TILES, D]), ALU.add), landed, *readers)

        def project_out(b, chunks, weight, waits_for, extra):
            for pair in range(TILES // 2):
                i, bank, free = ring_a.take()
                for q in range(2):
                    t = 2 * pair + q
                    for c, chunk in enumerate(chunks):
                        done = pe.do(lambda e, q=q, t=t, c=c, chunk=chunk, bank=bank: e.matmul(
                            bank[:, q * D:(q + 1) * D], chunk[:, t * P:(t + 1) * P], weight[:, c, :],
                            start=(q == 0 and c == 0), stop=(c == len(chunks) - 1), skip_group_check=True),
                            *waits_for(t), *free, signal=(q == 1 and c == len(chunks) - 1))
                t0 = b * TILES + 2 * pair
                added = dve.do(lambda e, t0=t0, bank=bank: e.tensor_tensor(
                    X[:, t0:t0 + 2, :], X[:, t0:t0 + 2, :], bank.rearrange("p (t d) -> p t d", t=2), ALU.add), done, *extra)
                ring_a.free(i, added)
                x_ready[b][2 * pair] = x_ready[b][2 * pair + 1] = added
                yield
            batch_free[b] = lasts()

        max_rows_ones = []
        first_stack = {}

        def split(phase, b, name, m, n, f, f_ready, rest_slot, last_slot):
            key = (phase, b, name)
            dst = parts_dram[key][m, :, :, n * SPAN:(n + 1) * SPAN].rearrange("s p t -> p s t")
            (r, rest, rest_free), (w, last, last_free) = rest_slot, last_slot
            j, both, both_free = work.take()
            two = both[:, :].bitcast(BF16).rearrange("p (s t) -> p s t", s=2)
            hi = act.do(lambda e: e.copy(two[:, 0, :], f), f_ready, *both_free)
            r1 = dve.do(lambda e: e.tensor_tensor(rest[:, :], f, two[:, 0, :], ALU.subtract), hi, *rest_free)
            mid = act.do(lambda e: e.copy(two[:, 1, :], rest[:, :]), r1)
            low = last[:, 0:SPAN // 2].bitcast(BF16)
            lo = pool.do(lambda e: e.tensor_tensor(low, rest[:, :], two[:, 1, :], ALU.subtract), mid, *last_free)
            work.free(r, lo)
            s1 = sp.dma(dst[:, 0:2, :], two, work_stored[j], mid)
            s2 = sp.dma(dst[:, 2, :], low, work_stored[w], lo)
            parts_stored[(*key, m)] += [s1, s2]
            work.free(j, lo, s1)
            work.free(w, s2)

        def load_stacks(phase, b, g):
            s, stack, free = stacks.take()
            rows_of = slice(g % 2 * HPG * HD, (g % 2 + 1) * HPG * HD)
            for name, row_parts in (("q", Q_PARTS), ("k", K_PARTS)):
                src = parts_dram[(phase, b, name)][g // 2, :, rows_of, :].rearrange("s (j d) t -> s d j t", j=HPG)
                for block, part in enumerate(row_parts):
                    landed = sp.dma(stack[name][block * HD:(block + 1) * HD, :, :], src[part], stack_landing[s],
                                    *parts_stored[(phase, b, name, g // 2)], *free)
            return s, stack, landed

        def ones_column(va, *waits):
            z = pool.do(lambda e: e.memset(va[:, :, :, HD:STRIP], 0.0), *waits)
            return pool.do(lambda e: e.memset(va[:, :, :, HD:HD + 1], 1.0), z)

        h_free = [[], []]

        def head_outputs(b, g, c, bank_i, bank, pv_done, eps):
            r, o, free = work.take()
            copied = act.do(lambda e: e.copy(o[:, :], bank), pv_done, *free)
            ring_c.free(bank_i, copied)
            yield
            i, tb, tfree = ring_a.take()
            for t in range(TPS):
                turned = pe.do(lambda e, t=t: e.transpose(tb[:, t * P:(t + 1) * P], o[:, t * P:(t + 1) * P], ident),
                               copied, *tfree, signal=t == TPS - 1)
            work.free(r, turned)
            v = tb.rearrange("p (t j e) -> p t j e", t=TPS, j=HPG)
            den = small[:, 0:16].rearrange("p (t j) -> p t j", t=TPS)
            if eps:
                d = dve.do(lambda e: e.tensor_scalar(den, v[:, :, :, HD], eps, None, ALU.max), turned, dve.last())
                d = dve.do(lambda e: e.reciprocal(den, den), d)
            else:
                d = dve.do(lambda e: e.reciprocal(den, v[:, :, :, HD]), turned, dve.last())
            dst = H[b][:, c * TPS:(c + 1) * TPS, g * HPG * HD:(g + 1) * HPG * HD].rearrange("p t (j e) -> p t j e", j=HPG)
            done = dve.do(lambda e: e.tensor_tensor(dst, v[:, :, :, 0:HD], den.unsqueeze(3).to_broadcast([P, TPS, HPG, HD]),
                                                    ALU.mult), d, *h_free[b])
            ring_a.free(i, done)
            heads_done[b] = done

        def linear_inputs(b):
            h_ready, ht_ready = yield from normalise(b)
            biased = add_bias(b, bias_row[:, 2, :], row0_landed, h_ready[-1])
            ht, va, qfeat, state = HT[b], vaug[b], qfeats[b], states[b]
            ktok = H[b]
            ones_ready = ones_column(va, pool.last())
            q_ready, unsplit = [], []
            for name, wcol, bcol in (("q", 0, 0), ("k", D, 2)):
                for m in range(DC):
                    for n in range(SPANS):
                        i, bank, free = ring_b.take()
                        for c in range(DC):
                            done = pe.do(lambda e: e.matmul(
                                bank, w_attn0[:, c, wcol + m * P:wcol + (m + 1) * P], ht[:, c, n * SPAN:(n + 1) * SPAN],
                                start=c == 0, stop=c == DC - 1), w0_landed, ht_ready[2 * n + 1], *free, signal=c == DC - 1)
                        yield
                        bias = bias_col[:, bcol + m:bcol + m + 1]
                        low_slot, f_slot = work.take(), work.take()
                        low = low_slot[1]
                        f = qfeat[:, m, n * SPAN:(n + 1) * SPAN] if name == "q" else f_slot[1][:, :]
                        t = act.do(lambda e: e.activation(low[:, :], bank, ACT.Exp, bias=bias), done, cols_landed, *low_slot[2])
                        z = dve.do(lambda e: e.tensor_scalar(f, bank, bias, 0.0, ALU.add, ALU.max), t, *f_slot[2])
                        ring_b.free(i, z)
                        f_done = dve.do(lambda e: e.scalar_tensor_tensor(f, low[:, :], 1.0, f, ALU.min, ALU.add), z)
                        if unsplit:
                            yield
                            split(*unsplit.pop())
                        unsplit.append(("a", b, name, m, n, f, f_done, (low_slot[0], low, (f_done,)), f_slot))
                        if name == "q":
                            q_ready.append(f_done)
                        yield
            split(*unsplit.pop())
            if b == 0:
                small_inputs()
                first_stack["a", b] = load_stacks("a", b, 0)
            tok_ready = []
            for t in range(TILES):
                i, bank, free = ring_b.take()
                for c in range(DC):
                    done = pe.do(lambda e: e.matmul(bank, ht[:, c, t * P:(t + 1) * P], w_attn0[:, c, D:3 * D], start=c == 0, stop=c == DC - 1),
                                 w0_landed, ht_ready[t // 2], *free, signal=c == DC - 1)
                yield
                j1, z, zfree = work.take()
                j2, low, low_free = work.take()
                zd = dve.do(lambda e: e.tensor_tensor(z[:, 0:D], bank[:, 0:D], bias_row[:, 0, :], ALU.add), done, row0_landed, *zfree)
                dve.do(lambda e: e.tensor_tensor(va[:, t, :, 0:HD], bank[:, D:2 * D].rearrange("p (h e) -> p h e", h=HEADS),
                                                 bias_row[:, 1, :].rearrange("p (h e) -> p h e", h=HEADS), ALU.add), done)
                vd = dve.last()
                ring_b.free(i, vd)
                l = dve.do(lambda e: e.tensor_scalar(low[:, 0:D], z[:, 0:D], 0.0, None, ALU.min), zd, *low_free)
                l = act.do(lambda e: e.activation(low[:, 0:D], low[:, 0:D], ACT.Exp), l)
                yield
                kd = dve.do(lambda e: e.scalar_tensor_tensor(ktok[:, t, :], z[:, 0:D], 0.0, low[:, 0:D], ALU.max, ALU.add), l, ht_ready[-1])
                work.free(j1, kd)
                work.free(j2, kd)
                tok_ready.append(kd)
            bank_i, sbank, sfree = ring_c.take()
            state_ready = [None]
            copied = None
            for c in range(TILES - 1):
                for half in range(DC):
                    done = pe.do(lambda e: e.matmul(
                        sbank[:, half * D:(half + 1) * D], ktok[:, c, half * P:(half + 1) * P],
                        va[:, c, half * HALF_HEADS:(half + 1) * HALF_HEADS, :].rearrange("p h e -> p (h e)"),
                        start=(c == 0 and half == 0), stop=True, skip_group_check=True),
                        tok_ready[c], ones_ready, copied, *sfree, signal=half == DC - 1)
                copied = dve.do(lambda e: e.tensor_tensor(
                    state[:, c, :].rearrange("p (m h e) -> p m h e", m=DC, h=HALF_HEADS),
                    sbank.rearrange("p (m h e) -> p m h e", m=DC, h=HALF_HEADS),
                    const("headmask").unsqueeze(1).unsqueeze(3).to_broadcast([P, DC, HALF_HEADS, STRIP]), ALU.mult), done)
                state_ready.append(copied)
                yield
                yield
            ring_c.free(bank_i, copied)
            h_free[b] = [done]
            ready[b] = (q_ready, tok_ready, state_ready, biased)

        ready = {}

        def linear_heads(b):
            q_ready, tok_ready, state_ready, biased = ready[b]
            va, qfeat, state = vaug[b], qfeats[b], states[b]
            loaded = first_stack["a", b]
            for g in range(GROUPS):
                s, stack, landed = loaded
                if g + 1 < GROUPS:
                    loaded = load_stacks("a", b, g + 1)
                outs, pending, finishing, summed = {}, {}, [], []

                def scores(t):
                    i, bank, free = ring_b.take()
                    for j in range(HPG):
                        done = pe.do(lambda e: e.matmul(
                            bank[:, j * P:(j + 1) * P], stack["k"][0:KSTACK, j, t * P:(t + 1) * P],
                            stack["q"][0:KSTACK, j, t * P:(t + 1) * P], start=j == 0, stop=True, skip_group_check=True),
                            landed, *free, signal=j == HPG - 1)
                    w, a, afree = work.take()
                    masked = dve.do(lambda e: e.tensor_tensor(
                        a[:, :].rearrange("p (j n) -> p j n", j=HPG), bank.rearrange("p (j n) -> p j n", j=HPG),
                        const("causal01").unsqueeze(1).to_broadcast([P, HPG, P]), ALU.mult), done, *afree)
                    ring_b.free(i, masked)
                    pending[t] = (w, a, masked)

                def sums(t):
                    c, q = t // TPS, t % TPS
                    w, a, masked = pending.pop(t)
                    if q == 0:
                        outs[c] = ring_c.take()
                    bank_i, bank, free = outs[c]
                    if t:
                        pe.do(lambda e: e.matmul(bank[:, q * P:(q + 1) * P], state[:, t - 1, g * P:(g + 1) * P],
                                                 qfeat[:, g // 2, t * P:(t + 1) * P], start=q == 0, stop=False, skip_group_check=True),
                              state_ready[t], *q_ready, *free, signal=False)
                    for j in range(HPG):
                        done = pe.do(lambda e: e.matmul(
                            bank[j * STRIP:(j + 1) * STRIP, q * P:(q + 1) * P], va[:, t, g * HPG + j, :],
                            a[:, j * P:(j + 1) * P], start=t == 0, stop=True, skip_group_check=True),
                            masked, tok_ready[t], *free, signal=j == HPG - 1)
                    work.free(w, done)
                    if q == TPS - 1:
                        finishing.append(head_outputs(b, g, c, bank_i, bank, done, DEN_EPS))
                        next(finishing[-1])

                for _ in staged(range(TILES), scores, sums):
                    if summed:
                        drain(summed.pop())
                    summed += finishing
                    finishing.clear()
                    yield
                drain(chain(*summed))
                stacks.free(s, pe.last())
            area_free[b] = lasts()

        heads_done = {}

        def finish_attention(b, weight, weight_landed, biased):
            turned = []
            for pair in range(TILES // 2):
                turned.append(turn(H[b], HT[b], b, pair, heads_done[b]))
                yield
            yield from project_out(b, [HT[b][:, c, :] for c in range(DC)], weight, lambda t: [turned[t // 2], weight_landed], [biased])

        qx = [carve(area[b], 0, 4096).rearrange("p (g t) -> p g t", g=GROUPS) for b in range(BATCH)]
        qx2 = [carve(area[b], 0, 2048).rearrange("p (g t) -> p g t", g=DC) for b in range(BATCH)]
        kbd, vx = {}, {}
        for b in range(BATCH):
            for phase, at in (("b", 4096), ("e", 2048)):
                kbd[phase, b] = carve(area[b], at, GROUPS * HPG * CTX).rearrange("p (g j k) -> p g j k", g=GROUPS, j=HPG)
                vx[phase, b] = carve(area[b], at + GROUPS * HPG * CTX, HEADS * STRIP).rearrange("p (h e) -> p h e", h=HEADS)
        hx, hx_r = [[h[b][:, :, :].rearrange("p t d -> p (t d)").rearrange("p (c t) -> p c t", c=DC) for b in range(BATCH)]
                    for h in (H, H_r)]
        ox = [[hx[b][:, 0, :], hx[b][:, 1, :], HT[b][:, 0, :], HT[b][:, 1, :]] for b in range(BATCH)]
        pt = Slots([carve(stack_area, 2048 * s, 2048).rearrange("p (j t) -> p j t", j=HPG) for s in range(2)])
        ctx_t = sb("ctx_t", [P, BATCH, DC, CTX])
        ctx_landed = load("ctx", ctx_t[:, :, :, :], A["ctx_t"].rearrange("b (c p) k -> p b c k", p=P))
        fmbd = sb("fmbd", [P, 2, P])
        fm_row = sb("fm_row", [CTX, 2, HPG * STRIP])
        load("fm", fmbd[:, :, :], A["fm_bd"].rearrange("v p n -> p v n"))
        load("fm", fm_row[:, 0, :], A["fm_b_row"].to_broadcast([CTX, P]))
        fm_landed = load("fm", fm_row[:, 1, :], A["sign_row"].to_broadcast([CTX, P]))
        load("row1", bias_row[:, 3, :], rows("L0_xattn_fc_b", D))
        load("row1", bias_row[:, 4, :], rows("L0_ffn_norm_gamma", D))
        row1_landed = load("row1", bias_row[:, 5, :], rows("L0_ffn_norm_beta", D))
        mask_i = stack_area[:, 1024:1024 + TILES * CTX].bitcast(I32).rearrange("p (t k) -> p t k", t=TILES)
        maskneg = sb("maskneg", [P, TILES, CTX], BF16)
        mask_landed = load("mask", mask_i, A["mask"].rearrange("(t p) k -> p t k", p=P))
        fm_b_signed = pool.do(lambda e: e.tensor_tensor(bias_col[:, 16:17], bias_col[:, 4:5], const("sign"), ALU.mult),
                              cols_landed, consts_landed)

        def staged(items, first, second, lag=2):
            items = list(items)
            for n in range(len(items) + lag):
                if n < len(items):
                    first(items[n])
                if n >= lag:
                    second(items[n - lag])
                yield

        def context_attention(b, phase):
            masked = phase == "e"
            queries, q_ready, kv_ready, ox_free, _ = ready[b]
            keys, values = kbd[phase, b], vx[phase, b]
            hold, spans, outs, turned = {}, {}, {}, {}

            def score(item):
                c, g, q = item
                t = c * TPS + q
                i, bank, free = ring_b.take()
                s = bank[:, 0:HPG * CTX]
                done = pe.do(lambda e: e.matmul(
                    s, queries[:, g // 2 if masked else g, t * P:(t + 1) * P], keys[:, g, :, :].rearrange("p j k -> p (j k)"),
                    start=True, stop=not masked, skip_group_check=True), *q_ready, *kv_ready, *free, signal=not masked)
                s3 = s.rearrange("p (j k) -> p j k", j=HPG)
                if masked:
                    done = pe.do(lambda e: e.matmul(s3, ident_bf[:, :], maskneg[:, t, :].unsqueeze(1).to_broadcast([P, HPG, CTX]),
                                                    start=False, stop=True, skip_group_check=True), masks_ready, mask_ready)
                at = 32 + 8 * (soft_count[0] % 8)
                soft_count[0] += 1
                mx, den = small[:, at:at + HPG], small[:, at + 4:at + 8]
                m = dve.do(lambda e: e.tensor_reduce(mx, s3, AX.X, ALU.max), done, small_free.get(at))
                hold[item] = (i, s3, mx, den, m, at)

            def exponential(item):
                i, s3, mx, den, m, at = hold[item]
                t = item[0] * TPS + item[2]
                w, ex, wfree = work.take()
                ex3 = ex[:, 0:HPG * CTX].rearrange("p (j k) -> p j k", j=HPG)
                d = dve.do(lambda e: e.tensor_tensor(ex3, s3, mx.unsqueeze(2).to_broadcast([P, HPG, CTX]), ALU.subtract), m, *wfree)
                ring_b.free(i, d)
                scale = rowany[:, t:t + 1] if masked else 1.0
                x = act.do(lambda e: e.activation(ex[:, 0:HPG * CTX], ex[:, 0:HPG * CTX], ACT.Exp, scale=scale), d)
                hold[item] = (w, ex, ex3, den, x, at)

            def total(item):
                w, ex, ex3, den, x, at = hold[item]
                hold[item] = (w, ex, ex3, den, dve.do(lambda e: e.tensor_reduce(den, ex3, AX.X, ALU.add), x), at)

            def divide(item):
                w, ex, ex3, den, r, at = hold[item]
                r = dve.do(lambda e: e.reciprocal(den, den), r)
                n = pool.do(lambda e: e.tensor_tensor(ex3, ex3, den.unsqueeze(2).to_broadcast([P, HPG, CTX]), ALU.mult), r)
                small_free[at] = n
                hold[item] = (w, ex, n)

            def turn_p(item):
                c, g, q = item
                if q == 0:
                    spans[c, g] = pt.take()
                pi, p_t, pt_free = spans[c, g]
                w, ex, n = hold.pop(item)
                i, bank, free = ring_a.take()
                for j in range(HPG):
                    done = pe.do(lambda e: e.transpose(bank[0:CTX, j * P:(j + 1) * P], ex[:, j * CTX:(j + 1) * CTX], ident),
                                 n, *free, signal=j == HPG - 1)
                work.free(w, done)
                turned[c, g] = act.do(lambda e: e.copy(p_t[0:CTX, :, q * P:(q + 1) * P], bank[0:CTX, :].rearrange("p (j n) -> p j n", j=HPG)),
                                      done, *pt_free)
                ring_a.free(i, turned[c, g])

            def sums(c, g):
                pi, p_t, _ = spans[c, g]
                if not masked or g % 2 == 0:
                    outs[c] = ring_c.take()
                oi, obank, ofree = outs[c]
                for j in range(HPG):
                    head = g * HPG + j
                    strip = (head % HALF_HEADS) // 2 if masked else j
                    done = pe.do(lambda e: e.matmul(
                        obank[strip * STRIP:(strip + 1) * STRIP, :], values[0:CTX, head, :], p_t[0:CTX, j, :],
                        start=(not masked or head % 2 == 0), stop=(not masked or head % 2 == 1), skip_group_check=True),
                        turned[c, g], *kv_ready, *ofree, signal=j == HPG - 1)
                pt.free(pi, done)
                if not masked or g % 2 == 1:
                    slot = g // 2 if masked else g
                    ox_ready[b, c] = act.do(lambda e: e.copy(ox[b][slot][:, c * SPAN:(c + 1) * SPAN], obank), done, *ox_free)
                    ring_c.free(oi, ox_ready[b, c])

            items = [(c, g, q) for c in range(SPANS) for g in range(GROUPS) for q in range(TPS)]
            turn_lag = TURN_LAG[phase]
            sums_lag = turn_lag + SUMS_LAG
            for n in range(len(items) + sums_lag):
                if n < len(items):
                    score(items[n])
                if DIVIDE_LAG <= n < len(items) + DIVIDE_LAG:
                    total(items[n - DIVIDE_LAG])
                if n < len(items):
                    exponential(items[n])
                if DIVIDE_LAG <= n < len(items) + DIVIDE_LAG:
                    divide(items[n - DIVIDE_LAG])
                if turn_lag <= n < len(items) + turn_lag:
                    turn_p(items[n - turn_lag])
                if n >= sums_lag and (n - sums_lag) % TPS == TPS - 1:
                    sums(*items[n - sums_lag][0:2])
                yield
            area_free[b] = lasts()

        small_free = {}
        soft_count = [0]
        ox_ready = {}

        def feature_inputs(b):
            h_ready, ht_ready = yield from normalise(b)
            biased = add_bias(b, bias_row[:, 3, :], row1_landed, h_ready[-1])
            free_a = list(area_free[b])
            q, keys, values = qx[b], kbd["b", b], vx["b", b]
            q_ready = []
            for g in range(GROUPS):
                for n in range(SPANS):
                    i, bank, free = ring_b.take()
                    done = pe.do(lambda e: e.matmul(bank, fmbd[:, g % 2, :], HT[b][:, g // 2, n * SPAN:(n + 1) * SPAN],
                                                    start=True, stop=True), fm_landed, ht_ready[2 * n + 1], *free)
                    yield
                    qd = act.do(lambda e: e.activation(q[:, g, n * SPAN:(n + 1) * SPAN], bank, ACT.Exp, bias=bias_col[:, 16:17],
                                                       scale=const("sign")), done, fm_b_signed, *free_a)
                    ring_b.free(i, qd)
                    q_ready.append(qd)
            z = pool.do(lambda e: e.memset(keys[:, :, :, :], 0.0), *free_a)
            kv_ready = []
            for g in range(GROUPS):
                i, bank, free = ring_b.take()
                done = pe.do(lambda e: e.matmul(bank[:, 0:CTX], fmbd[:, g % 2, :], ctx_t[:, b, g // 2, :], start=True, stop=True),
                             fm_landed, ctx_landed, *free)
                i2, bank2, free2 = ring_b.take()
                done2 = pe.do(lambda e: e.matmul(bank2[0:CTX, 0:P], ctx_t[:, b, g // 2, :], fmbd[:, g % 2, :], start=True, stop=True), *free2)
                yield
                for j in range(HPG):
                    st = slice(j * STRIP, (j + 1) * STRIP)
                    k = act.do(lambda e: e.activation(keys[st, g, j, :], bank[st, 0:CTX], ACT.Exp, bias=bias_col[st, 16:17],
                                                      scale=const("sign")[st, :]), done, z)
                ring_b.free(i, k)
                j1, tmp, tfree = work.take()
                s = dve.do(lambda e: e.tensor_tensor(tmp[0:CTX, 0:P], bank2[0:CTX, 0:P], fm_row[:, 0, :], ALU.add), done2, fm_landed, *tfree)
                ring_b.free(i2, s)
                s = dve.do(lambda e: e.tensor_tensor(tmp[0:CTX, 0:P], tmp[0:CTX, 0:P], fm_row[:, 1, :], ALU.mult), s)
                s = act.do(lambda e: e.activation(values[0:CTX, g * HPG:(g + 1) * HPG, :].rearrange("p h e -> p (h e)"), tmp[0:CTX, 0:P],
                                                  ACT.Exp), s, *free_a)
                work.free(j1, s)
                kv_ready.append(s)
                yield
                kv_ready.append(dve.do(lambda e: e.tensor_scalar(keys[:, g, :, :], keys[:, g, :, :], 1.0 / 16.0, None, ALU.mult), k))
            ready[b] = (q, q_ready, kv_ready, [pe.last()], biased)

        def finish_context(b, chunks, weight, weight_landed, biased):
            yield from project_out(b, chunks, weight, lambda t: [ox_ready[b, t // TPS], weight_landed], [biased])

        gate_w = W2[:, 1024:1024 + DC * GATE_COLS].rearrange("p (c n) -> p c n", c=DC)
        table = W2[:, 1300:1300 + TABLE + D]
        raw_t = W2[:, 1640:1640 + DC * TILES_FFN].rearrange("p (c n) -> p c n", c=DC)
        ffn_rows = sb("ffn_rows", [P, 3 * COMP + 2 + KNOTS + 2])
        load("ffn", raw_t, A["sig_t"].rearrange("(c p) n -> p c n", p=P))
        load("ffn", gate_w[:, :, CLUSTERS + TILES_FFN:], A["L0_ffn_compress_w1"].rearrange("(c p) n -> p c n", p=P))
        load("ffn", table[0:TILES_FFN, :], A["spline_table"])
        R_B1, R_W2, R_B2, R_KN, R_TEMP, R_SCALE = 0, COMP, 3 * COMP, 3 * COMP + 2, 3 * COMP + 2 + KNOTS, 3 * COMP + 3 + KNOTS
        load("ffn", ffn_rows[:, R_B1:R_B1 + COMP], rows("L0_ffn_compress_b1", COMP))
        load("ffn", ffn_rows[:, R_W2:R_W2 + 2 * COMP], A["compress_w2_t"].rearrange("(a i) n -> a (i n)", a=1).to_broadcast([P, 2 * COMP]))
        load("ffn", ffn_rows[:, R_B2:R_B2 + 2], rows("L0_ffn_compress_b2", 2))
        load("ffn", ffn_rows[:, R_KN:R_KN + KNOTS], rows("L0_ffn_knot_values", KNOTS))
        load("ffn", ffn_rows[:, R_TEMP:R_TEMP + 1], rows("L0_ffn_temperature", 1))
        ffn_landed = load("ffn", ffn_rows[:, R_SCALE:R_SCALE + 1], rows("L0_ffn_output_scale", 1))

        def ffn_weights():
            q = small[:, 128:256].rearrange("p (c n) -> p c n", c=DC)
            n = small[:, 256:384].rearrange("p (c n) -> p c n", c=DC)
            a = dve.do(lambda e: e.tensor_scalar(q, raw_t, 0.3, None, ALU.is_gt), ffn_landed)
            bb = dve.do(lambda e: e.tensor_scalar(n, raw_t, -0.3, None, ALU.is_lt), ffn_landed)
            a = dve.do(lambda e: e.tensor_tensor(q, q, n, ALU.subtract), a, bb)
            a = dve.do(lambda e: e.tensor_tensor(q, q, raw_t, ALU.subtract), a)
            sig = gate_w[:, :, CLUSTERS:CLUSTERS + TILES_FFN]
            a = dve.do(lambda e: e.tensor_tensor(sig, raw_t, q, ALU.add), a)
            cs = small[:, 384:400].rearrange("p (c n) -> p c n", c=DC)
            a = dve.do(lambda e: e.tensor_reduce(cs, sig.rearrange("p c (n k) -> p c n k", k=TPC), AX.X, ALU.add), a)
            pos = small[:, 400:416].rearrange("p (c n) -> p c n", c=DC)
            neg = small[:, 416:432].rearrange("p (c n) -> p c n", c=DC)
            a1 = dve.do(lambda e: e.tensor_scalar(pos, cs, 0.0, None, ALU.is_gt), a)
            a2 = dve.do(lambda e: e.tensor_scalar(neg, cs, 0.0, None, ALU.is_lt), a)
            a = dve.do(lambda e: e.tensor_tensor(gate_w[:, :, 0:CLUSTERS], pos, neg, ALU.subtract), a2)
            a = dve.do(lambda e: e.tensor_tensor(small[:, 440:440 + KNOTS - 1], ffn_rows[:, R_KN + 1:R_KN + KNOTS],
                                                 ffn_rows[:, R_KN:R_KN + KNOTS - 1], ALU.subtract), a)
            a = dve.do(lambda e: e.tensor_scalar(small[:, 448:449], ffn_rows[:, R_TEMP:R_TEMP + 1], 1e-6, None, ALU.add), a)
            a = dve.do(lambda e: e.reciprocal(small[:, 449:450], small[:, 448:449]), a)
            return dve.do(lambda e: e.tensor_scalar(small[:, 450:451], small[:, 449:450], -1.0, None, ALU.mult), a)

        def calibrate(dst, s, scratch, ready):
            u, low, diff, wide1, wide2 = scratch
            a = act.do(lambda e: e.activation(u, s, ACT.Exp, scale=small[:, 450:451]), ready)
            yield
            a = dve.do(lambda e: e.tensor_scalar(u, u, 1.0, None, ALU.add), a)
            a = dve.do(lambda e: e.reciprocal(u, u), a)
            a = dve.do(lambda e: e.tensor_scalar(u, u, float(KNOTS - 1), None, ALU.mult), a)
            yield

            def per_knot(row, first, last):
                return row[:, first:last].unsqueeze(1).unsqueeze(1).to_broadcast([P, TILES, 8, last - first])

            def per_score(v, n):
                return v.unsqueeze(3).to_broadcast([P, TILES, 8, n])
            inner, cells = KNOTS - 2, KNOTS - 1
            a = dve.do(lambda e: e.tensor_tensor(wide1[:, :, :, 0:inner], per_score(u, inner), per_knot(const("iota8"), 1, KNOTS - 1), ALU.is_ge), a)
            a = dve.do(lambda e: e.tensor_reduce(low, wide1[:, :, :, 0:inner], AX.X, ALU.add), a)
            a = dve.do(lambda e: e.tensor_tensor(u, u, low, ALU.subtract), a)
            yield
            a = dve.do(lambda e: e.tensor_tensor(wide1[:, :, :, 0:cells], per_score(low, cells), per_knot(const("iota8"), 0, cells), ALU.is_equal), a)
            of_diffs = pool.do(lambda e: e.tensor_tensor(wide2[:, :, :, 0:cells], wide1[:, :, :, 0:cells],
                                                         per_knot(small[:, 440:448], 0, cells), ALU.mult), a)
            a = dve.do(lambda e: e.tensor_tensor(wide1[:, :, :, 0:cells], wide1[:, :, :, 0:cells],
                                                 per_knot(ffn_rows[:, R_KN:R_KN + KNOTS], 0, cells), ALU.mult), of_diffs)
            a = dve.do(lambda e: e.tensor_reduce(dst, wide1[:, :, :, 0:cells], AX.X, ALU.add), a)
            yield
            a = dve.do(lambda e: e.tensor_reduce(diff, wide2[:, :, :, 0:cells], AX.X, ALU.add), a)
            a = dve.do(lambda e: e.tensor_tensor(diff, diff, u, ALU.mult), a)
            return dve.do(lambda e: e.tensor_tensor(dst, dst, diff, ALU.add), a)

        def first_max(onehot, g, scratch, col, ready):
            eq = scratch
            a = dve.do(lambda e: e.tensor_reduce(col, g, AX.X, ALU.max), ready)
            a = dve.do(lambda e: e.tensor_tensor(eq, g, col.unsqueeze(2).to_broadcast([P, TILES, 8]), ALU.is_equal), a)
            a = dve.do(lambda e: e.tensor_scalar(onehot, const("iota8").unsqueeze(1).to_broadcast([P, TILES, 8]), -8.0, None, ALU.add), a)
            a2 = dve.do(lambda e: e.tensor_tensor(eq, eq, onehot, ALU.mult), a)
            a3 = dve.do(lambda e: e.tensor_reduce(col, eq, AX.X, ALU.min), a2)
            return dve.do(lambda e: e.tensor_tensor(onehot, onehot, col.unsqueeze(2).to_broadcast([P, TILES, 8]), ALU.is_equal), a3)

        def spline_ffn(b):
            weights_ready = weights_done[0]
            h_ready, ht_ready = yield from normalise(b)
            add_bias(b, bias_row[:, 5, :], row1_landed, h_ready[-1])
            at = [0]

            def take(n):
                at[0] += n
                return carve(area[b], at[0] - n, n)
            S = take(TILES * GATE_COLS).rearrange("p (t n) -> p t n", t=TILES)
            free_a = list(area_free[b])
            for t in range(TILES):
                i, bank, free = ring_b.take()
                for c in range(DC):
                    done = pe.do(lambda e, c=c, t=t, bank=bank: e.matmul(bank[:, 0:GATE_COLS], HT[b][:, c, t * P:(t + 1) * P], gate_w[:, c, :],
                                                              start=c == 0, stop=c == DC - 1), weights_ready, ht_ready[t // 2], *free, signal=c == 1)
                s = act.do(lambda e, t=t, bank=bank: e.copy(S[:, t, :], bank[:, 0:GATE_COLS]), done, *free_a)
                ring_b.free(i, s)
                yield
            cs, ts, zc = S[:, :, 0:CLUSTERS], S[:, :, CLUSTERS:CLUSTERS + TILES_FFN], S[:, :, CLUSTERS + TILES_FFN:]
            n8 = TILES * 8
            v8 = [take(n8).rearrange("p (t n) -> p t n", t=TILES) for _ in range(8)]
            gate, oc, ol, sel = v8[4], v8[5], v8[6], v8[7]
            col = take(TILES)
            w = dve.do(lambda e: e.tensor_tensor(zc, zc, ffn_rows[:, R_B1:R_B1 + COMP].unsqueeze(1).to_broadcast([P, TILES, COMP]), ALU.add), s)
            gl = act.do(lambda e: e.activation(zc, zc, ACT.Gelu), w)
            big = take(TILES * COMP)
            prod = take(TILES * COMP).rearrange("p (t n) -> p t n", t=TILES)
            big3 = big.rearrange("p (t n) -> p t n", t=TILES)
            comp = take(2 * TILES).rearrange("p (i t) -> p i t", i=2)
            yield
            wides = [v.rearrange("p (t i k) -> p t i k", t=TILES, i=8) for v in (big, prod.rearrange("p t n -> p (t n)"))]
            a = yield from calibrate(gate, cs, (*v8[0:3], *wides), s)
            a = first_max(oc, gate, v8[0], col, a)
            big4 = big.rearrange("p (t c k) -> p t c k", t=TILES, c=CLUSTERS)
            a = dve.do(lambda e: e.tensor_tensor(big4, ts.rearrange("p t (c k) -> p t c k", c=CLUSTERS),
                                                 oc.unsqueeze(3).to_broadcast([P, TILES, CLUSTERS, TPC]), ALU.mult), a)
            a = dve.do(lambda e: e.tensor_reduce(sel, big.rearrange("p (t c k) -> p t k c", t=TILES, c=CLUSTERS), AX.X, ALU.add), a)
            a = yield from calibrate(gate, sel, (*v8[0:3], *wides), a)
            a = first_max(ol, gate, v8[0], col, a)
            a = dve.do(lambda e: e.tensor_tensor(big4, oc.unsqueeze(3).to_broadcast([P, TILES, CLUSTERS, TPC]),
                                                 ol.unsqueeze(2).to_broadcast([P, TILES, CLUSTERS, TPC]), ALU.mult), a)
            onehot_ready = a
            yield
            a = gl
            for i2 in range(2):
                w2 = ffn_rows[:, R_W2 + i2 * COMP:R_W2 + (i2 + 1) * COMP].unsqueeze(1).to_broadcast([P, TILES, COMP])
                a = dve.do(lambda e, w2=w2: e.tensor_tensor(prod, zc, w2, ALU.mult), a)
                a = dve.do(lambda e, i2=i2: e.tensor_reduce(comp[:, i2, :], prod, AX.X, ALU.add), a)
            for i2 in range(2):
                cd = act.do(lambda e, i2=i2: e.activation(comp[:, i2, :], comp[:, i2, :], ACT.Tanh, bias=ffn_rows[:, R_B2 + i2:R_B2 + i2 + 1]), a)
            par = take(TILES * TABLE).rearrange("p (t n) -> p t n", t=TILES)
            dirs = take(TILES * D).rearrange("p (t n) -> p t n", t=TILES)
            yield from pause(ONEHOT_PAUSE)
            for pair in range(TILES // TPS):
                i, bank, free = ring_a.take()
                for q in range(TPS):
                    done = pe.do(lambda e, q=q, pair=pair, bank=bank: e.transpose(bank[0:TILES_FFN, q * P:(q + 1) * P], big3[:, pair * TPS + q, :], ident),
                                 onehot_ready, *free, signal=q == TPS - 1)
                wi, oh, ofree = work.take()
                turned = act.do(lambda e, oh=oh, bank=bank: e.copy(oh[0:TILES_FFN, :], bank[0:TILES_FFN, :]), done, *ofree)
                ring_a.free(i, turned)
                yield
                for q in range(TPS):
                    t = pair * TPS + q
                    i, bank, free = ring_b.take()
                    done = pe.do(lambda e, q=q, oh=oh, bank=bank: e.matmul(bank[:, 0:TABLE + D], oh[0:TILES_FFN, q * P:(q + 1) * P], table[0:TILES_FFN, :],
                                                            start=True, stop=True), turned, *free)
                    act.do(lambda e, t=t, bank=bank: e.copy(par[:, t, :], bank[:, 0:TABLE]), done, *free_a)
                    c2 = act.do(lambda e, t=t, bank=bank: e.copy(dirs[:, t, :], bank[:, TABLE:TABLE + D]), done)
                    ring_b.free(i, c2)
                    yield
                work.free(wi, done)
            hh = take(TILES * GRID).rearrange("p (t n) -> p t n", t=TILES)
            h2 = prod.rearrange("p t n -> p (t n)")[:, 0:TILES * GRID].rearrange("p (t n) -> p t n", t=TILES)

            def bc(i2):
                return comp[:, i2, :].unsqueeze(2).to_broadcast([P, TILES, GRID])
            a = dve.do(lambda e: e.tensor_tensor(hh, par[:, :, 0:GRID], bc(0), ALU.mult), c2, cd)
            a2 = dve.do(lambda e: e.tensor_tensor(h2, par[:, :, GRID:2 * GRID], bc(1), ALU.mult), a)
            a = dve.do(lambda e: e.tensor_tensor(hh, hh, h2, ALU.add), a2)
            a = dve.do(lambda e: e.tensor_tensor(hh, hh, par[:, :, 2 * GRID:3 * GRID], ALU.add), a)
            a = dve.do(lambda e: e.scalar_tensor_tensor(hh, hh, 0.0, par[:, :, 3 * GRID:4 * GRID], ALU.max, ALU.mult), a)
            a = dve.do(lambda e: e.tensor_reduce(col, hh, AX.X, ALU.add), a)
            a = dve.do(lambda e: e.tensor_tensor(col, col, par[:, :, 4 * GRID], ALU.add), a)
            a = dve.do(lambda e: e.tensor_scalar(col, col, ffn_rows[:, R_SCALE:R_SCALE + 1], None, ALU.mult), a)
            base = b * TILES
            for pair in range(TILES // 2):
                ts = (2 * pair, 2 * pair + 1)
                ys = [dve.do(lambda e: e.scalar_tensor_tensor(dirs[:, t, :], dirs[:, t, :], col[:, t:t + 1], H[b][:, t, :], ALU.mult, ALU.add), a)
                      for t in ts]
                taken = [dve.do(lambda e: e.bn_stats(stats[b][:, t, :], dirs[:, t, :]), y) for t, y in zip(ts, ys)]
                for t, s1 in zip(ts, taken):
                    agg = dve.do(lambda e: e.bn_aggr(mv[b][:, t, :], stats[b][:, t, :]), s1)
                yield
                yield
            v = pool.do(lambda e: e.tensor_scalar(rstd[b][:, 0, :], mv[b][:, :, 1], LN_EPS, None, ALU.add), agg)
            v = pool.do(lambda e: e.tensor_tensor(rstd[b][:, 1, :], rstd[b][:, 0, :], const("halfneg"), ALU.pow), v)
            yield
            shift = dve.do(lambda e: e.scalar_tensor_tensor(col, mv[b][:, :, 0], -1.0, rstd[b][:, 1, :], ALU.mult, ALU.mult), v)
            for t in range(TILES):
                n = act.do(lambda e: e.activation(dirs[:, t, :], dirs[:, t, :], ACT.Identity, bias=col[:, t:t + 1],
                                                  scale=rstd[b][:, 1, t:t + 1]), shift)
                gm = dve.do(lambda e: e.tensor_tensor(dirs[:, t, :], dirs[:, t, :], bias_row[:, 4, :], ALU.mult), n, row1_landed)
                x_ready[b][t] = pool.do(lambda e: e.tensor_tensor(X[:, base + t, :], X[:, base + t, :], dirs[:, t, :], ALU.add), gm)
                yield
            batch_free[b] = lasts()
            area_free[b] = lasts()

        w_qkv = carve(area[0], 5344, 1536).rearrange("p (c n) -> p c n", c=DC)
        w_proj = carve(area[0], 9216, 512).rearrange("p (c n) -> p c n", c=DC)

        def attention_inputs(b):
            h_ready, ht_ready = yield from normalise(b)
            biased = add_bias(b, bias_row[:, 1, :], row2_landed[0], h_ready[-1])
            ht, va = HT[b], vaug[b]
            ones_ready = ones_column(va, pool.last(), *area_free[b])
            for n in range(SPANS):
                for name, wcol, bcol in (("q", 0, 12), ("k", D, 14)):
                    for m in range(DC):
                        i, bank, free = ring_b.take()
                        for c in range(DC):
                            done = pe.do(lambda e: e.matmul(
                                bank, w_qkv[:, c, wcol + m * P:wcol + (m + 1) * P], ht[:, c, n * SPAN:(n + 1) * SPAN],
                                start=c == 0, stop=c == DC - 1), w2_landed[0], ht_ready[2 * n + 1], *free, signal=c == DC - 1)
                        yield
                        f_slot, rest_slot = work.take(), work.take()
                        _, f, ffree = f_slot
                        bias = bias_col[:, bcol + m:bcol + m + 1]
                        scale = 0.25 if name == "q" else 1.0
                        fd = dve.do(lambda e: e.tensor_scalar(f[:, :], bank, bias, scale, ALU.add, ALU.mult), done, cols_landed, *ffree)
                        ring_b.free(i, fd)
                        split("d", b, name, m, n, f[:, :], fd, rest_slot, f_slot)
                        yield
            if b == 0:
                first_stack["d", b] = load_stacks("d", b, 0)
            for pair in range(TILES // 2):
                i, bank, free = ring_b.take()
                for q in range(2):
                    t = 2 * pair + q
                    for c in range(DC):
                        done = pe.do(lambda e: e.matmul(
                            bank[:, q * D:(q + 1) * D], ht[:, c, t * P:(t + 1) * P], w_qkv[:, c, 2 * D:3 * D],
                            start=(q == 0 and c == 0), stop=c == DC - 1, skip_group_check=True), *free, signal=(q == 1 and c == DC - 1))
                yield
                for q in range(2):
                    t = 2 * pair + q
                    vd = dve.do(lambda e: e.tensor_tensor(
                        va[:, t, :, 0:HD], bank[:, q * D:(q + 1) * D].rearrange("p (h e) -> p h e", h=HEADS),
                        bias_row[:, 0, :].rearrange("p (h e) -> p h e", h=HEADS), ALU.add), done, row2_landed[0], *area_free[b])
                ring_b.free(i, vd)
            h_free[b] = [ht_ready[-1]]
            inputs[b] = (vd, ones_ready, biased)

        inputs = {}
        mneg = [sb(f"mneg{i}", [STRIP, 2, P], BF16) for i in range(2)]
        mxt = [sb(f"mx{i}", [P, HPG, TILES, 2]) for i in range(2)]
        mcomb = sb("mcomb", [P, HPG * TILES])
        mneg_free = [[], []]

        def maxima(b, g, slot, stack, landed):
            mx = mxt[slot]
            for j in range(HPG):
                for t in range(TILES):
                    for half in range(t // TPS + 1):
                        n = min(t + 1 - half * TPS, TPS) * P
                        diagonal = half == t // TPS
                        i, bank, free = ring_a.take()
                        done = pe.do(lambda e, j=j, t=t, half=half, n=n, bank=bank: e.matmul(
                            bank[:, 0:n], stack["q"][0:KSTACK, j, t * P:(t + 1) * P],
                            stack["k"][0:KSTACK, j, half * SPAN:half * SPAN + n], start=True, stop=True, skip_group_check=True),
                            landed, *free, signal=not diagonal)
                        if diagonal:
                            done = pe.do(lambda e, n=n, bank=bank: e.matmul(bank[:, n - P:n], ident_bf[:, :], mask_qk_bf[:, :],
                                                                 start=False, stop=True, skip_group_check=True), masks_ready)
                        red = dve.do(lambda e, j=j, t=t, half=half, n=n, bank=bank: e.tensor_reduce(mx[:, j, t, half:half + 1], bank[:, 0:n], AX.X, ALU.max),
                                     done, *mneg_free[slot])
                        ring_a.free(i, red)
                        yield
            yield
            m3 = mcomb[:, :].rearrange("p (j t) -> p j t", j=HPG)
            a = dve.do(lambda e: e.tensor_copy(m3[:, :, 0:TPS], mx[:, :, 0:TPS, 0]), red, mcomb_free[0])
            a = dve.do(lambda e: e.tensor_tensor(m3[:, :, TPS:], mx[:, :, TPS:, 0], mx[:, :, TPS:, 1], ALU.max), a)
            yield
            i, bank, free = ring_a.take()
            done = pe.do(lambda e: e.transpose(bank[0:STRIP, 0:P], mcomb[:, :], ident), a, *free)
            mcomb_free[0] = done
            ng = mneg[slot]
            a = dve.do(lambda e: e.tensor_scalar(ng[:, 0, :], bank[0:STRIP, 0:P], -1.0, None, ALU.mult), done, *mneg_free[slot])
            a = dve.do(lambda e: e.scalar_tensor_tensor(ng[:, 1, :], bank[0:STRIP, 0:P], -1.0, ng[:, 0, :], ALU.mult, ALU.subtract), a)
            ring_a.free(i, a)
            for s in range(2):
                dst = stack["q"][KSTACK + s:KSTACK + s + 1, :, :].rearrange("p j (t n) -> p (j t) n", n=P)
                m_landed = sp.dma(dst, ng[:, s, :], max_landing[slot], a)
            mneg_free[slot] = [m_landed]
            result[(b, g)] = m_landed
            yield

        mcomb_free = [None]
        result = {}

        def weighted(b, g, stack, landed, m_landed):
            v_ready, ones_ready, _ = inputs[b]
            finishing = []
            for c in range(SPANS):
                bank_i, obank, ofree = ring_c.take()
                held = None

                def values(kb, off, ps, last, obank=obank, ofree=ofree):
                    for j in range(HPG):
                        w, p, ex = ps[j]
                        done = pe.do(lambda e, j=j, p=p: e.matmul(
                            obank[j * STRIP:(j + 1) * STRIP, off:SPAN], vaug[b][:, kb, g * HPG + j, :], p[:, 0:SPAN - off],
                            start=kb == 0, stop=last, skip_group_check=True), ex, v_ready, ones_ready, *ofree, signal=j == HPG - 1)
                    for j in range(HPG):
                        work.free(ps[j][0], done)
                    return done

                blocks = (c + 1) * TPS
                for kb in range(blocks):
                    off = max(0, kb * P - c * SPAN)
                    ps = []
                    for j in range(HPG):
                        i, bank, free = ring_b.take()
                        n = SPAN - off
                        diagonal = kb * P >= c * SPAN
                        done = pe.do(lambda e, j=j, kb=kb, off=off, n=n, bank=bank: e.matmul(
                            bank[:, 0:n], stack["k"][0:KSTACK + 2, j, kb * P:(kb + 1) * P],
                            stack["q"][0:KSTACK + 2, j, c * SPAN + off:(c + 1) * SPAN], start=True, stop=True, skip_group_check=True),
                            landed, m_landed, max_rows_ones[-1], *free, signal=not diagonal)
                        if diagonal:
                            done = pe.do(lambda e, bank=bank: e.matmul(bank[:, 0:P], ident_bf[:, :], mask_kq_bf[:, :], start=False, stop=True,
                                                            skip_group_check=True))
                        w, p, wfree = work.take()
                        ex = act.do(lambda e, p=p, n=n, bank=bank: e.activation(p[:, 0:n], bank[:, 0:n], ACT.Exp), done, *wfree)
                        ring_b.free(i, ex)
                        ps.append((w, p, ex))
                        if j < HPG - 1:
                            yield
                    if held:
                        values(*held, False)
                    held = (kb, off, ps)
                    if kb == 0 and finishing:
                        drain(finishing.pop())
                    yield
                done = values(*held, True)
                finishing.append(head_outputs(b, g, c, bank_i, obank, done, 0.0))
                next(finishing[-1])
            yield
            drain(finishing.pop())

        def softmax_attention(other_inputs, after_first):
            for s in range(len(stacks.buffers)):
                max_rows_ones.append(act.do(lambda e: e.copy(
                    stacks.buffers[s]["k"][KSTACK:KSTACK + 2, :, :].rearrange("p j t -> p (j t)"),
                    const("sign")[KSTACK:KSTACK + 2, :].to_broadcast([2, HPG * SEQ])), *lasts()))
            seq = [(b, g) for b in range(BATCH) for g in range(GROUPS)]
            loaded = {0: first_stack["d", 0]}
            side = other_inputs
            previous = None
            for n in range(len(seq) + 1):
                steps_a, steps_b = None, None
                if n == GROUPS - 1:
                    drain(side)
                if n + 1 < len(seq):
                    loaded[n + 1] = load_stacks("d", *seq[n + 1])
                if n < len(seq):
                    (b, g), (s, stack, landed) = seq[n], loaded[n]
                    steps_a = maxima(b, g, n % 2, stack, landed)
                if n:
                    pb, pg, ps, pstack, planded = previous
                    steps_b = weighted(pb, pg, pstack, planded, result[(pb, pg)])
                for _ in range(MAXIMA_LEAD):
                    next(steps_a or side, None)
                while steps_a or steps_b:
                    if steps_b and next(steps_b, "end") == "end":
                        steps_b = None
                    if steps_a and next(steps_a, "end") == "end":
                        steps_a = None
                    next(side, None)
                    if not steps_b:
                        next(side, None)
                if n:
                    stacks.free(ps, pe.last())
                    if pg == GROUPS - 1:
                        area_free[pb] = lasts()
                        if pb == 0:
                            side = after_first()
                if n < len(seq):
                    previous = (b, g, s, stack, landed)
            yield from side

        w_x = W1[:, :].rearrange("p (c n) -> p c n", c=DC)
        rowany = sb("rowany", [P, TILES])

        def mask_weights():
            a = None
            for half in range(2):
                w, buf, free = work.take()
                v = buf[:, 0:TPS * CTX].rearrange("p (t k) -> p t k", t=TPS)
                sl = slice(half * TPS, (half + 1) * TPS)
                a = dve.do(lambda e, v=v, sl=sl: e.tensor_scalar(v, mask_i[:, sl, :], 0.0, None, ALU.not_equal), mask_landed, *free)
                r = dve.do(lambda e, v=v, sl=sl: e.tensor_reduce(rowany[:, sl], v, AX.X, ALU.max), a)
                a = dve.do(lambda e, v=v, sl=sl: e.tensor_scalar(maskneg[:, sl, :], v, 1.0, 1e9, ALU.subtract, ALU.mult), r)
                work.free(w, a)
            return a

        def masked_inputs(b):
            h_ready, ht_ready = yield from normalise(b)
            biased = add_bias(b, bias_row[:, 3, :], row3_landed, h_ready[-1])
            free_a = list(area_free[b])
            queries, keys, values = qx2[b], kbd["e", b], vx["e", b]
            q_ready, kv_ready = [], []
            for m in range(DC):
                for n in range(SPANS):
                    i, bank, free = ring_b.take()
                    for c in range(DC):
                        done = pe.do(lambda e, c=c, m=m, n=n, bank=bank: e.matmul(
                            bank, w_x[:, c, m * P:(m + 1) * P], HT[b][:, c, n * SPAN:(n + 1) * SPAN],
                            start=c == 0, stop=c == DC - 1), wx_landed[0], ht_ready[2 * n + 1], *free, signal=c == DC - 1)
                    q = dve.do(lambda e, m=m, n=n, bank=bank: e.tensor_scalar(queries[:, m, n * SPAN:(n + 1) * SPAN], bank, bias_col[:, 8 + m:9 + m],
                                                                   0.25, ALU.add, ALU.mult), done, cols_landed, *free_a)
                    ring_b.free(i, q)
                    q_ready.append(q)
                    yield
            z = pool.do(lambda e: e.memset(values[:, :, :], 0.0), *free_a)
            for m in range(DC):
                i, bank, free = ring_b.take()
                for c in range(DC):
                    done = pe.do(lambda e, c=c, m=m, bank=bank: e.matmul(bank[:, 0:CTX], w_x[:, c, D + m * P:D + (m + 1) * P], ctx_t[:, b, c, :],
                                                              start=c == 0, stop=c == DC - 1), *free, signal=c == DC - 1)
                for h8 in range(HALF_HEADS):
                    k = dve.do(lambda e, m=m, h8=h8, bank=bank: e.tensor_scalar(
                        keys[:, 2 * m + h8 // HPG, h8 % HPG, :], bank[:, 0:CTX], bias_col[:, 10 + m:11 + m],
                        const("headmask")[:, h8:h8 + 1], ALU.add, ALU.mult), done, *free_a)
                ring_b.free(i, k)
                kv_ready.append(k)
            i, bank, free = ring_b.take()
            for c in range(DC):
                done = pe.do(lambda e, c=c, bank=bank: e.matmul(bank[0:CTX, 0:D], ctx_t[:, b, c, :], w_x[:, c, 2 * D:3 * D],
                                                     start=c == 0, stop=c == DC - 1), *free, signal=c == DC - 1)
            for odd in range(2):
                src = bank[0:CTX, 0:D].rearrange("p (h o e) -> p h o e", o=2, e=HD)[:, :, odd, :]
                brow = bias_row[0:CTX, 2, :].rearrange("p (h o e) -> p h o e", o=2, e=HD)[:, :, odd, :]
                dst = values[0:CTX, :, :].rearrange("p (h o) e -> p h o e", o=2)[:, :, odd, odd * HD:(odd + 1) * HD]
                k = dve.do(lambda e, dst=dst, src=src, brow=brow: e.tensor_tensor(dst, src, brow, ALU.add), done, z, row2_landed[0])
            ring_b.free(i, k)
            kv_ready.append(k)
            ready[b] = (queries, q_ready, kv_ready, [pe.last()], biased)

        NE = EXPERTS + 1
        wd_shared, wd_shared_r = [carve(a[0], 8144, D) for a in (area, area_r)]
        wg, wg_r = [carve(a[0], 3792, DC * NE * INNER).rearrange("p (c e i) -> p c e i", c=DC, e=NE) for a in (area, area_r)]
        wu, wu_r = [carve(a[1], 3792, DC * NE * INNER).rearrange("p (c e i) -> p c e i", c=DC, e=NE) for a in (area, area_r)]
        sel = carve(area[1], 8144, 1024, BF16).rearrange("p (e n) -> p e n", e=EXPERTS)
        wd, wd_r = [carve(a, 4096, EXPERTS * D).rearrange("p (e n) -> p e n", e=EXPERTS) for a in (stack_area, stack_area_r)]
        gw = sb("gate_weights", [P, DC, EXPERTS])

        matrix = DC * INNER
        upper_places = [carve(region, first + n * matrix, matrix) for region, first, last in (
            (W2_r, 0, 2048), (area_r[0], 8400, 9728), (area_r[1], 9168, 9728), (stack_area_r, 0, 4096), (area_r[0], 1232, 3792),
            (area_r[1], 1232, 3792))
            for n in range((last - first) // matrix)]
        upper_w = {}

        def split_expert(x, waits=()):
            for k, (name, w, w_lo) in enumerate((
                    ("g", wg[:, :, x, :], wg_r[:, :, x, :]), ("u", wu[:, :, x, :], wu_r[:, :, x, :]),
                    ("d", wd_shared, wd_shared_r) if x == EXPERTS else ("d", wd[:, x, :], wd_r[:, x, :]))):
                w_hi = upper_places[3 * x + k]
                if name != "d":
                    w_hi = w_hi.rearrange("p (c i) -> p c i", c=DC)
                hi = act.do(lambda e: e.copy(w_hi, w), moe_landed[0], *waits)
                lo = dve.do(lambda e: e.tensor_tensor(w_lo, w, w_hi, ALU.subtract), hi)
                upper_w[x, name] = (w_hi, w_lo, lo)

        def load_experts(waits):
            for c in range(DC):
                rs = slice(c * P, (c + 1) * P)
                for w, name, shared in ((wg, "L1_ffn_Wg", "L1_ffn_sg"), (wu, "L1_ffn_Wu", "L1_ffn_su")):
                    load("moe", w[:, c, 0:EXPERTS, :], A[name][:, rs, :].rearrange("e p i -> p e i"), *waits)
                    load("moe", w[:, c, EXPERTS, :], A[shared][rs, :])
            load("moe", wd[:, 0:EXPERTS, :], A["L1_ffn_Wd"].rearrange("e p n -> p e n"))
            return load("moe", wd_shared, A["L1_ffn_sd"])

        def moe_inputs(b):
            h_ready, ht_ready = yield from normalise(b)
            free_a = list(area_free[b])
            combt = carve(area[b], 0, 512, BF16)
            sc = carve(area[b], 512, P).rearrange("p (t e) -> p t e", t=TILES)
            rank = carve(area[b], 640, P).rearrange("p (t e) -> p t e", t=TILES)
            col = carve(area[b], 768, TILES)
            comb3 = carve(area[b], 784, TILES * PARTS * EXPERTS).rearrange("p (t s e) -> p t s e", t=TILES, s=PARTS)
            cbf = carve(area[b], 1168, P // 2, BF16).rearrange("p (t e) -> p t e", t=TILES)
            i, bank, free = ring_b.take()
            for t in range(TILES):
                for c in range(DC):
                    done = pe.do(lambda e: e.matmul(bank[:, t * EXPERTS:(t + 1) * EXPERTS], HT[b][:, c, t * P:(t + 1) * P],
                                                    gw[:, c, :], start=(t == 0 and c == 0), stop=c == 1, skip_group_check=True),
                                 gw_landed, ht_ready[t // 2], *free, signal=(t == TILES - 1 and c == 1))
            scored = done
            a = act.do(lambda e, bank=bank: e.activation(sc.rearrange("p t e -> p (t e)"), bank[:, 0:P], ACT.Exp, scale=-1.0), done, *free_a)
            ring_b.free(i, a)
            yield
            yield
            a = dve.do(lambda e: e.tensor_scalar(sc, sc, 1.0, None, ALU.add), a)
            a = dve.do(lambda e: e.reciprocal(sc, sc), a)
            yield
            before = const("before").rearrange("p (i j) -> p i j", i=EXPERTS).unsqueeze(1).to_broadcast([P, 2, EXPERTS, EXPERTS])
            for pair in range(TILES // 2):
                ts = slice(2 * pair, 2 * pair + 2)
                me = sc[:, ts, :].unsqueeze(3).to_broadcast([P, 2, EXPERTS, EXPERTS])
                other = sc[:, ts, :].unsqueeze(2).to_broadcast([P, 2, EXPERTS, EXPERTS])
                (w1, g1, free1), (w2, g2, free2) = work.take(), work.take()
                g1, g2 = [g[:, :].rearrange("p (t i j) -> p t i j", t=2, i=EXPERTS) for g in (g1, g2)]
                a1 = dve.do(lambda e: e.tensor_tensor(g1, other, me, ALU.is_gt), a, *free1)
                a2 = dve.do(lambda e: e.tensor_tensor(g2, other, me, ALU.is_equal), a1, *free2)
                a2 = dve.do(lambda e: e.tensor_tensor(g2, g2, before, ALU.mult), a2)
                a2 = dve.do(lambda e: e.tensor_tensor(g1, g1, g2, ALU.add), a2)
                a = dve.do(lambda e: e.tensor_reduce(rank[:, ts, :], g1, AX.X, ALU.add), a2)
                work.free(w1, a)
                work.free(w2, a)
                yield
            a = dve.do(lambda e: e.scalar_tensor_tensor(sc, rank, float(TOPK) - 0.5, sc, ALU.is_lt, ALU.mult), a)
            a = dve.do(lambda e: e.tensor_reduce(col, sc, AX.X, ALU.add), a)
            a = dve.do(lambda e: e.reciprocal(col, col), a)
            a = dve.do(lambda e: e.tensor_tensor(sc, sc, col.unsqueeze(2).to_broadcast([P, TILES, EXPERTS]), ALU.mult), a)
            for s in range(PARTS):
                a = dve.do(lambda e: e.tensor_copy(cbf, sc), a)
                a = dve.do(lambda e, s=s: e.tensor_copy(comb3[:, :, s, :], cbf), a)
                if s < PARTS - 1:
                    a = dve.do(lambda e: e.tensor_tensor(sc, sc, cbf, ALU.subtract), a)
                yield
            yield from pause(ROUTING_PAUSE)
            comb_ready = []
            for n in range(SPANS):
                i, bank, free = ring_b.take()
                for q in range(TPS):
                    done = pe.do(lambda e, q=q, n=n, bank=bank: e.transpose(
                        bank[0:PARTS * EXPERTS, q * P:(q + 1) * P], comb3[:, n * TPS + q, :, :].rearrange("p s e -> p (s e)"), ident),
                        a, *free, signal=q == TPS - 1)
                cd = act.do(lambda e, n=n, bank=bank: e.copy(combt[0:PARTS * EXPERTS, n * SPAN:(n + 1) * SPAN], bank[0:PARTS * EXPERTS, :]), done, *free_a)
                ring_b.free(i, cd)
                comb_ready.append(cd)
                yield
            parts_ready = []
            for n in range(SPANS):
                for c in range(DC):
                    cols = slice(n * SPAN, (n + 1) * SPAN)
                    hi = act.do(lambda e: e.copy(hx_r[b][:, c, cols], HT[b][:, c, cols]), ht_ready[-1])
                    lo = dve.do(lambda e: e.tensor_tensor(HT_r[b][:, c, cols], HT[b][:, c, cols], hx_r[b][:, c, cols], ALU.subtract),
                                hi, scored)
                yield
                parts_ready.append(lo)
            ready[b] = (parts_ready, comb_ready)

        def moe(b):
            parts_ready, comb_ready = ready[b]
            combt = carve(area[b], 0, 512, BF16)
            ht_hi, ht_lo = hx_r[b], HT_r[b]
            for n in range(SPANS):
                cols = slice(n * SPAN, (n + 1) * SPAN)
                outs = [ring_c.take() for _ in range(2)]
                held = {}

                def up(x):
                    banks = []
                    for name in "gu":
                        w_hi, w_lo, w_ready = upper_w[x, name]
                        i, bank, free = ring_a.take() if name == "g" else ring_b.take()
                        products = [(w, h, c) for c in range(DC) for w, h in ((w_hi, ht_hi), (w_hi, ht_lo), (w_lo, ht_hi))]
                        for k, (w, h, c) in enumerate(products):
                            done = pe.do(lambda e: e.matmul(bank, w[:, c, :], h[:, c, cols], start=k == 0, stop=k == len(products) - 1),
                                         w_ready, parts_ready[n], *free, signal=k == len(products) - 1)
                        banks.append((i, bank, done))
                    (gi, gbank, gdone), (ui, ubank, udone) = banks
                    k, s, sfree = work.take()
                    a = act.do(lambda e: e.activation(s[:, :], gbank, ACT.Silu), gdone, *sfree)
                    ring_a.free(gi, a)
                    a = dve.do(lambda e: e.tensor_tensor(s[:, :], s[:, :], ubank, ALU.mult), a, udone)
                    ring_b.free(ui, a)
                    if x < EXPERTS:
                        i, bank, free = ring_b.take()
                        done = pe.do(lambda e: e.matmul(bank, sel[0:PARTS * EXPERTS, x, :], combt[0:PARTS * EXPERTS, cols], start=True, stop=True),
                                     sel_ready[0], comb_ready[n], *free)
                        a = dve.do(lambda e: e.tensor_tensor(s[:, :], s[:, :], bank, ALU.mult), a, done)
                        ring_b.free(i, a)
                    k2, _, hi_free = work.take()
                    hi, lo = work_r[k2], work_r[k]
                    h = act.do(lambda e: e.copy(hi[:, :], s[:, :]), a, *hi_free)
                    a = pool.do(lambda e: e.tensor_tensor(lo[:, :], s[:, :], hi[:, :], ALU.subtract), h)
                    held[x] = (k, lo, k2, hi, a)

                def down(x):
                    k, lo, k2, hi, ready = held.pop(x)
                    w_hi, w_lo, w_ready = upper_w[x, "d"]
                    for q in range(TPS):
                        oi, obank, ofree = outs[q // 2]
                        o = q % 2
                        for m, (act_part, w) in enumerate(((hi, w_hi), (hi, w_lo), (lo, w_hi))):
                            done = pe.do(lambda e: e.matmul(
                                obank[:, o * D:(o + 1) * D], act_part[:, q * P:(q + 1) * P], w,
                                start=(x == 0 and o == 0 and m == 0), stop=(x == NE - 1 and m == 2), skip_group_check=True),
                                ready, w_ready, *ofree, signal=(q == TPS - 1 and m == 2))
                    work.free(k, done)
                    work.free(k2, done)
                    return done

                for x in range(NE + 2):
                    if x < NE:
                        if x + SPLIT_AHEAD < NE and (x + SPLIT_AHEAD, "g") not in upper_w:
                            split_expert(x + SPLIT_AHEAD, places_free)
                        up(x)
                    if x >= 2:
                        done = down(x - 2)
                    yield
                for o in range(2):
                    oi, obank, _ = outs[o]
                    t0 = b * TILES + n * TPS + 2 * o
                    added = dve.do(lambda e, t0=t0, obank=obank: e.tensor_tensor(X[:, t0:t0 + 2, :], X[:, t0:t0 + 2, :],
                                                                    obank.rearrange("p (t d) -> p t d", t=2), ALU.add), done)
                    ring_c.free(oi, added)
                    x_ready[b][n * TPS + 2 * o] = x_ready[b][n * TPS + 2 * o + 1] = added

        row2_landed, w2_landed, wx_landed, moe_landed, sel_ready = [None], [None], [None], [None], [None]
        gw_landed = load("gw", gw[:, :, :], A["gate_w_t"].rearrange("(c p) e -> p c e", p=P))

        def drain(stage):
            for _ in stage:
                pass

        def chain(*stages):
            for stage in stages:
                yield from stage

        def advance(main, side, start=0, extra_every=0):
            for n, _ in enumerate(main):
                if n >= start:
                    next(side, None)
                if extra_every and n % extra_every == extra_every - 1:
                    next(side, None)

        def weave(main, side):
            advance(main, side)
            drain(side)

        w_out0 = w_attn0[:, :, 3 * D:4 * D]
        w_outx = w_x[:, :, 3 * D:4 * D]
        ox_e = [[hx[b][:, c, :] for c in range(DC)] for b in range(BATCH)]

        def probabilities_after_stacks():
            pt.hold_back(*lasts())
            yield

        weights_done = []

        def small_inputs():
            nonlocal mask_ready
            weights_done.append(ffn_weights())
            mask_ready = mask_weights()
            stacks.hold_back(masks_ready, mask_ready)
            pt.hold_back(mask_ready)

        other = linear_inputs(1)
        advance(linear_inputs(0), other, INPUTS_LEAD)
        advance(linear_heads(0), other)
        advance(chain(probabilities_after_stacks(), finish_attention(0, w_out0, w0_landed, ready[0][3]), feature_inputs(0),
                      context_attention(0, "b")), other)
        drain(other)
        stacks.idle.reverse()
        first_stack["a", 1] = load_stacks("a", 1, 0)
        for i, v in enumerate((A["L1_attn_b_attn"][2 * D:3 * D], A["L1_attn_b_proj"], A["L1_xattn_bv"])):
            row2_landed[0] = load("row2", bias_row[:, i, :], spread(v, D), *lasts())
        load("w2", w_qkv, A["L1_attn_w_attn"].rearrange("(c p) n -> p c n", p=P))
        w2_landed[0] = load("w2", w_proj, A["L1_attn_w_proj"].rearrange("(c p) n -> p c n", p=P))
        stacks.hold_back(pe.last())
        other = chain(finish_context(0, ox[0], w_fc, wa_landed, ready[0][4]), spline_ffn(0), attention_inputs(0))
        advance(chain(linear_heads(1), probabilities_after_stacks(), finish_attention(1, w_out0, w0_landed, ready[1][3]), feature_inputs(1),
                      context_attention(1, "b")), other, extra_every=EXTRA_EVERY)
        row3_landed = load("row3", bias_row[:, 3, :], spread(A["L1_xattn_bo"], D), *lasts())
        wx_landed[0] = load("wx", w_x, A["L1_xattn_w"].rearrange("(c p) n -> p c n", p=P))
        drain(other)
        stacks.hold_back(*lasts())
        stacks.add(stack_slots[2], *lasts())
        drain(softmax_attention(
            chain(finish_context(1, ox[1], w_fc, wa_landed, ready[1][4]), spline_ffn(1), attention_inputs(1)),
            lambda: chain(finish_attention(0, w_proj, w2_landed[0], inputs[0][2]), masked_inputs(0))))
        pt.hold_back(*lasts())
        moe_landed[0] = load_experts(lasts())
        sel_ready[0] = dve.do(lambda e: e.tensor_copy(sel[0:PARTS * EXPERTS], const("parts")[0:PARTS * EXPERTS, :].unsqueeze(2)
                                                      .to_broadcast([PARTS * EXPERTS, EXPERTS, P])), *lasts())
        weave(context_attention(0, "e"), chain(finish_attention(1, w_proj, w2_landed[0], inputs[1][2]), masked_inputs(1)))

        def split_first(waits):
            for x in range(SPLIT_EARLY):
                split_expert(x, waits)
                yield

        weave(context_attention(1, "e"), chain(finish_context(0, ox_e[0], w_outx, wx_landed[0], ready[0][4]), moe_inputs(0),
                                               split_first(lasts())))
        places_free = lasts()
        weave(moe(0), chain(finish_context(1, ox_e[1], w_outx, wx_landed[0], ready[1][4]), moe_inputs(1)))
        drain(moe(1))
        out_tiles = out.rearrange("b (t p) d -> p (b t) d", p=P)
        stored = landing("stored")
        for b in range(BATCH):
            for n in range(SPANS):
                t0 = b * TILES + n * TPS
                end = sp.dma(out_tiles[:, t0:t0 + TPS, :], X[:, t0:t0 + TPS, :], stored, *x_ready[b][n * TPS:(n + 1) * TPS])
        sp.wait(end, *lasts())
        for l in loads.values():
            sp.wait(l.last())


def lay_out(I):
    f = {k: np.ascontiguousarray(v) for k, v in I.items()}
    a = {"x": f["x"], "consts": constants()}
    a["ctx_t"] = np.ascontiguousarray(f["ctx_1024"].transpose(0, 2, 1))
    a["mask"] = f["mask_1x1xSxS2_ik0"].reshape(SEQ, CTX)
    a["L0_attn_w"] = np.concatenate([f[f"L0_attn_W{n}"].T for n in "qkvo"], axis=1)
    for n in ("L0_attn_bq", "L0_attn_bk", "L0_attn_bv", "L0_attn_bo", "L0_xattn_fc_b", "L0_ffn_knot_values", "L0_ffn_temperature",
              "L0_ffn_compress_w1", "L0_ffn_compress_b1", "L0_ffn_compress_b2", "L0_ffn_norm_gamma", "L0_ffn_norm_beta",
              "L0_ffn_output_scale", "L1_attn_w_attn", "L1_attn_b_attn", "L1_attn_w_proj", "L1_attn_b_proj", "L1_xattn_bq",
              "L1_xattn_bk", "L1_xattn_bv", "L1_xattn_bo", "L1_ffn_Wg", "L1_ffn_Wu", "L1_ffn_Wd", "L1_ffn_sg", "L1_ffn_su", "L1_ffn_sd"):
        a[n] = f[n]
    bd = np.zeros((2, P, P), np.float32)
    for v in range(2):
        for j in range(HPG):
            r = (v * HPG + j) * HD
            bd[v, r:r + HD, j * STRIP:j * STRIP + HD] = f["L0_xattn_fm_w"].T
            bd[v, r:r + HD, j * STRIP + HD:(j + 1) * STRIP] = f["L0_xattn_fm_w"].T
    a["fm_bd"] = bd
    cols = [f["L0_attn_bq"], f["L0_attn_bk"], np.tile(f["L0_xattn_fm_b"], P // HD), np.zeros(3 * P, np.float32),
            f["L1_xattn_bq"], f["L1_xattn_bk"], f["L1_attn_b_attn"][:2 * D]]
    a["bias_cols"] = np.ascontiguousarray(np.concatenate(cols).reshape(16, P).T)
    a["fm_b_row"] = np.tile(f["L0_xattn_fm_b"], P // HD).reshape(1, P)
    a["sign_row"] = np.where(np.arange(P) % STRIP < HD, 1.0, -1.0).astype(np.float32).reshape(1, P)
    a["fc_w_t"] = np.ascontiguousarray(f["L0_xattn_fc_w"].T)
    a["sig_t"] = np.ascontiguousarray(f["L0_ffn_signatures_raw"].T)
    a["spline_table"] = np.concatenate([f["L0_ffn_spline_w1"].reshape(TILES_FFN, 2 * GRID), f["L0_ffn_spline_b1"],
                                        f["L0_ffn_spline_w2"].reshape(TILES_FFN, GRID), f["L0_ffn_spline_b2"],
                                        f["L0_ffn_directions"]], axis=1)
    a["compress_w2_t"] = np.ascontiguousarray(f["L0_ffn_compress_w2"].T)
    a["L1_xattn_w"] = np.concatenate([f[f"L1_xattn_w{n}"].T for n in "qkvo"], axis=1)
    a["gate_w_t"] = np.ascontiguousarray(f["L1_ffn_gate_w"].T)
    return a


def kernel(**inputs):
    import concourse.bacc as bacc
    from concourse.bass_utils import run_bass_kernel_spmd

    arrays = lay_out({k: np.asarray(v) for k, v in inputs.items()})
    nc = bacc.Bacc("TRN2", target_bir_lowering=False, num_devices=1)
    args = {k: nc.dram_tensor(f"in_{k}", v.shape, mybir.dt.from_np(v.dtype), kind="ExternalInput").ap() for k, v in arrays.items()}
    out = nc.dram_tensor("out", (BATCH, SEQ, D), F32, kind="ExternalOutput").ap()
    build(nc, args, out)
    r = run_bass_kernel_spmd(nc, [{f"in_{k}": v for k, v in arrays.items()}], core_ids=[0])
    return r.results[0]["out"]
```
